# Optimizing a Trainium2 kernel written in Bass

```python
import numpy as np
import jax
import jax.numpy as jnp

def _softmax(x, axis=-1):
    return jax.nn.softmax(x, axis=axis)

def _gelu(x):
    return jax.nn.gelu(x, approximate=True)

def _silu(x):
    return jax.nn.silu(x)

def _sigmoid(x):
    return jax.nn.sigmoid(x)

def _layernorm(x, axis=-1, eps=1e-05):
    m = jnp.mean(x, axis=axis, keepdims=True)
    v = jnp.var(x, axis=axis, keepdims=True)
    return (x - m) / jnp.sqrt(v + eps)

def _scatter_add(tgt, idx, src, axis=0):
    return tgt.at[idx].add(src)

def _segment_sum(src, seg, n):
    return jax.ops.segment_sum(src, seg, n)
kernel_name = 'mk_xattn_ffn_d2_seqx_r4_53aaa3'

def setup_inputs(seed: int=0):
    np.random.seed(seed)
    _w = jnp.asarray

    def _rec_inputs():
        import jax
        import jax.numpy as jnp
        _rk = jax.random.key(seed)
        x = 7.22e-05 + 1 * jax.random.normal(jax.random.fold_in(_rk, 1), (4, 512, 256), jnp.float32)
        _lenS = 512 - jax.random.randint(jax.random.fold_in(_rk, 7), (4,), 0, max(1, 512 // 4) + 1, jnp.int32)
        _lenS2 = 64 - jax.random.randint(jax.random.fold_in(_rk, 8), (4,), 0, max(1, 64 // 4) + 1, jnp.int32)
        _ctx_1024P = jax.random.normal(jax.random.fold_in(_rk, 11), (4, 16, 256), jnp.float32)
        _ctx_1024c = jax.random.dirichlet(jax.random.fold_in(_rk, 511), 0.3 * jnp.ones((16,), jnp.float32), (4, 64))
        _ctx_1024t = jnp.einsum('bsk,bkd->bsd', _ctx_1024c, _ctx_1024P)
        _ctx_1024t = _ctx_1024t * jax.lax.rsqrt(jnp.mean(jnp.square(_ctx_1024t)) + 1e-12) * 0.953939
        ctx_1024 = -1.39393e-06 + 0.999914 * (_ctx_1024t + 0.3 * jax.random.normal(jax.random.fold_in(_rk, 611), (4, 64, 256), jnp.float32))
        _validS = jnp.arange(512)[None, :] < _lenS[:, None]
        _validS2 = jnp.arange(64)[None, :] < _lenS2[:, None]
        _causal = jnp.tril(jnp.ones((512, 512), dtype=bool))
        mask_1x1xSxS2_ik1 = jnp.where(jnp.broadcast_to(_validS2[0:1, None, None, :], (1, 1, 512, 64)), 1, 0).astype(jnp.int32)
        return (x, ctx_1024, mask_1x1xSxS2_ik1)
    x, ctx_1024, mask_1x1xSxS2_ik1 = _rec_inputs()

    def _L0_xattn_setup():
        import jax, jax.numpy as jnp
        import numpy as np
        EPS = 1e-05

        def layernorm(x, g, b):
            mu = jnp.mean(x, axis=-1, keepdims=True)
            var = jnp.var(x, axis=-1, keepdims=True)
            return (x - mu) * jax.lax.rsqrt(var + EPS) * g + b
        DIM = 256
        CTX = 256
        HEADS = 12
        DHEAD = 64
        INNER = HEADS * DHEAD
        B = 4
        F = 512
        J = 256
        key = jax.random.key(seed)
        ks = jax.random.split(key, 8)
        s = lambda d: 1.0 / np.sqrt(d)
        return {'x': jax.random.normal(ks[0], (B, F, DIM), jnp.float32), 'tab_x': jax.random.normal(ks[1], (B, J, CTX), jnp.float32), 'tab_g': jnp.ones((CTX,), jnp.float32), 'tab_b': jnp.zeros((CTX,), jnp.float32), 'vid_g': jnp.ones((DIM,), jnp.float32), 'vid_b': jnp.zeros((DIM,), jnp.float32), 'Wq': jax.random.normal(ks[2], (DIM, INNER), jnp.float32) * s(DIM), 'Wk': jax.random.normal(ks[3], (CTX, INNER), jnp.float32) * s(CTX), 'Wv': jax.random.normal(ks[4], (CTX, INNER), jnp.float32) * s(CTX), 'q_g': jnp.ones((INNER,), jnp.float32), 'q_b': jnp.zeros((INNER,), jnp.float32), 'k_g': jnp.ones((INNER,), jnp.float32), 'k_b': jnp.zeros((INNER,), jnp.float32), 'Wo': jax.random.normal(ks[5], (INNER, DIM), jnp.float32) * s(INNER), 'bo': jnp.zeros((DIM,), jnp.float32)}
    _L0_xattn_all = _L0_xattn_setup()
    _L0_xattn_in = {k: v for k, v in _L0_xattn_all.items() if k in ('tab_g', 'tab_b', 'vid_g', 'vid_b', 'Wq', 'Wk', 'Wv', 'q_g', 'q_b', 'k_g', 'k_b', 'Wo', 'bo')}
    del _L0_xattn_all

    def _L0_ffn_setup():
        import jax, jax.numpy as jnp
        import numpy as np
        D_IN, D_HID = (256, 1024)

        def _ternary(key, shape):
            return jax.random.randint(key, shape, -1, 2).astype(jnp.float32)

        def _tlin(x, w, s):
            return jnp.einsum('bsi,oi->bso', x, w) * s
        key = jax.random.key(seed)
        ks = jax.random.split(key, 12)
        inv = lambda fan: 1.0 / np.sqrt(fan).astype(np.float32)
        return {'x': jax.random.normal(ks[0], (4, 512, D_IN), dtype=jnp.float32), 'w1_w': _ternary(ks[1], (D_HID, D_IN)), 'w1_s': jax.random.uniform(ks[2], (D_HID,), dtype=jnp.float32) * inv(D_IN), 'w2_w': _ternary(ks[3], (D_HID, D_IN)), 'w2_s': jax.random.uniform(ks[4], (D_HID,), dtype=jnp.float32) * inv(D_IN), 'h1_w': _ternary(ks[5], (D_HID, D_HID)), 'h1_s': jax.random.uniform(ks[6], (D_HID,), dtype=jnp.float32) * inv(D_HID), 'h2_w': _ternary(ks[7], (D_HID, D_HID)), 'h2_s': jax.random.uniform(ks[8], (D_HID,), dtype=jnp.float32) * inv(D_HID), 'w3_w': _ternary(ks[9], (D_IN, D_HID)), 'w3_s': jax.random.uniform(ks[10], (D_IN,), dtype=jnp.float32) * inv(D_HID)}
    _L0_ffn_all = _L0_ffn_setup()
    _L0_ffn_in = {k: v for k, v in _L0_ffn_all.items() if k in ('w1_w', 'w1_s', 'w2_w', 'w2_s', 'h1_w', 'h1_s', 'h2_w', 'h2_s', 'w3_w', 'w3_s')}
    del _L0_ffn_all

    def _L1_xattn_setup():
        import jax, jax.numpy as jnp
        import numpy as np
        D_MODEL = 256
        NUM_HEADS = 16
        D_K = D_MODEL // NUM_HEADS
        B, S = (4, 512)
        key = jax.random.key(seed)
        ks = jax.random.split(key, 12)
        std = 1.0 / np.sqrt(D_MODEL)
        mk = lambda k: jax.random.normal(k, (D_MODEL, D_MODEL), jnp.float32) * std
        return {'q': jax.random.normal(ks[0], (B, S, D_MODEL), jnp.float32), 'k': jax.random.normal(ks[1], (B, S, D_MODEL), jnp.float32), 'v': jax.random.normal(ks[2], (B, S, D_MODEL), jnp.float32), 'mask': jax.random.randint(ks[3], (1, 1, S, S), 0, 2, jnp.int32), 'Wq': mk(ks[4]), 'bq': jnp.zeros((D_MODEL,), jnp.float32), 'Wk': mk(ks[5]), 'bk': jnp.zeros((D_MODEL,), jnp.float32), 'Wv': mk(ks[6]), 'bv': jnp.zeros((D_MODEL,), jnp.float32), 'Wo': mk(ks[7]), 'bo': jnp.zeros((D_MODEL,), jnp.float32)}
    _L1_xattn_all = _L1_xattn_setup()
    _L1_xattn_in = {k: v for k, v in _L1_xattn_all.items() if k in ('Wq', 'bq', 'Wk', 'bk', 'Wv', 'bv', 'Wo', 'bo')}
    del _L1_xattn_all

    def _L1_ffn_setup():
        import jax, jax.numpy as jnp
        import numpy as np
        D = 256
        N_EXP = 8
        TOP_K = 1
        key = jax.random.key(seed)
        ks = jax.random.split(key, 7)
        s = 0.02
        return {'x': jax.random.normal(ks[0], (4, 512, D), jnp.float32), 'gate_w': jax.random.normal(ks[1], (D, N_EXP), jnp.float32) * s, 'gate_b': jnp.zeros((N_EXP,), jnp.float32), 'w1': jax.random.normal(ks[2], (N_EXP, D, 4 * D), jnp.float32) * s, 'b1': jnp.zeros((N_EXP, 4 * D), jnp.float32), 'w2': jax.random.normal(ks[3], (N_EXP, 4 * D, D), jnp.float32) * s, 'b2': jnp.zeros((N_EXP, D), jnp.float32)}
    _L1_ffn_all = _L1_ffn_setup()
    _L1_ffn_in = {k: v for k, v in _L1_ffn_all.items() if k in ('gate_w', 'gate_b', 'w1', 'b1', 'w2', 'b2')}
    del _L1_ffn_all
    return {'x': x, 'ctx_1024': ctx_1024, 'mask_1x1xSxS2_ik1': mask_1x1xSxS2_ik1, 'L0_xattn_tab_g': _L0_xattn_in['tab_g'], 'L0_xattn_tab_b': _L0_xattn_in['tab_b'], 'L0_xattn_vid_g': _L0_xattn_in['vid_g'], 'L0_xattn_vid_b': _L0_xattn_in['vid_b'], 'L0_xattn_Wq': _L0_xattn_in['Wq'], 'L0_xattn_Wk': _L0_xattn_in['Wk'], 'L0_xattn_Wv': _L0_xattn_in['Wv'], 'L0_xattn_q_g': _L0_xattn_in['q_g'], 'L0_xattn_q_b': _L0_xattn_in['q_b'], 'L0_xattn_k_g': _L0_xattn_in['k_g'], 'L0_xattn_k_b': _L0_xattn_in['k_b'], 'L0_xattn_Wo': _L0_xattn_in['Wo'], 'L0_xattn_bo': _L0_xattn_in['bo'], 'L0_ffn_w1_w': _L0_ffn_in['w1_w'], 'L0_ffn_w1_s': _L0_ffn_in['w1_s'], 'L0_ffn_w2_w': _L0_ffn_in['w2_w'], 'L0_ffn_w2_s': _L0_ffn_in['w2_s'], 'L0_ffn_h1_w': _L0_ffn_in['h1_w'], 'L0_ffn_h1_s': _L0_ffn_in['h1_s'], 'L0_ffn_h2_w': _L0_ffn_in['h2_w'], 'L0_ffn_h2_s': _L0_ffn_in['h2_s'], 'L0_ffn_w3_w': _L0_ffn_in['w3_w'], 'L0_ffn_w3_s': _L0_ffn_in['w3_s'], 'L1_xattn_Wq': _L1_xattn_in['Wq'], 'L1_xattn_bq': _L1_xattn_in['bq'], 'L1_xattn_Wk': _L1_xattn_in['Wk'], 'L1_xattn_bk': _L1_xattn_in['bk'], 'L1_xattn_Wv': _L1_xattn_in['Wv'], 'L1_xattn_bv': _L1_xattn_in['bv'], 'L1_xattn_Wo': _L1_xattn_in['Wo'], 'L1_xattn_bo': _L1_xattn_in['bo'], 'L1_ffn_gate_w': _L1_ffn_in['gate_w'], 'L1_ffn_gate_b': _L1_ffn_in['gate_b'], 'L1_ffn_w1': _L1_ffn_in['w1'], 'L1_ffn_b1': _L1_ffn_in['b1'], 'L1_ffn_w2': _L1_ffn_in['w2'], 'L1_ffn_b2': _L1_ffn_in['b2']}

def reference(x, ctx_1024, mask_1x1xSxS2_ik1, L0_xattn_tab_g, L0_xattn_tab_b, L0_xattn_vid_g, L0_xattn_vid_b, L0_xattn_Wq, L0_xattn_Wk, L0_xattn_Wv, L0_xattn_q_g, L0_xattn_q_b, L0_xattn_k_g, L0_xattn_k_b, L0_xattn_Wo, L0_xattn_bo, L0_ffn_w1_w, L0_ffn_w1_s, L0_ffn_w2_w, L0_ffn_w2_s, L0_ffn_h1_w, L0_ffn_h1_s, L0_ffn_h2_w, L0_ffn_h2_s, L0_ffn_w3_w, L0_ffn_w3_s, L1_xattn_Wq, L1_xattn_bq, L1_xattn_Wk, L1_xattn_bk, L1_xattn_Wv, L1_xattn_bv, L1_xattn_Wo, L1_xattn_bo, L1_ffn_gate_w, L1_ffn_gate_b, L1_ffn_w1, L1_ffn_b1, L1_ffn_w2, L1_ffn_b2):
    import jax
    import jax.numpy as jnp

    def _L0_xattn_ref(x, tab_x, tab_g, tab_b, vid_g, vid_b, Wq, Wk, Wv, q_g, q_b, k_g, k_b, Wo, bo):
        import jax, jax.numpy as jnp
        import numpy as np
        EPS = 1e-05

        def layernorm(x, g, b):
            mu = jnp.mean(x, axis=-1, keepdims=True)
            var = jnp.var(x, axis=-1, keepdims=True)
            return (x - mu) * jax.lax.rsqrt(var + EPS) * g + b
        DIM = 256
        CTX = 256
        HEADS = 12
        DHEAD = 64
        INNER = HEADS * DHEAD
        B = 4
        F = 512
        J = 256
        scale = DHEAD ** (-0.5)
        kv_in = layernorm(tab_x, tab_g, tab_b)
        q = layernorm(layernorm(x, vid_g, vid_b) @ Wq, q_g, q_b)
        k = layernorm(kv_in @ Wk, k_g, k_b)
        v = kv_in @ Wv
        split = lambda t: t.reshape(t.shape[0], t.shape[1], HEADS, DHEAD).transpose(0, 2, 1, 3)
        q, k, v = (split(q) * scale, split(k), split(v))
        sim = jnp.einsum('bhid,bhjd->bhij', q, k)
        attn = jax.nn.softmax(sim, axis=-1)
        out = jnp.einsum('bhij,bhjd->bhid', attn, v)
        out = out.transpose(0, 2, 1, 3).reshape(x.shape[0], x.shape[1], INNER)
        return out @ Wo + bo

    def _L0_ffn_ref(x, w1_w, w1_s, w2_w, w2_s, h1_w, h1_s, h2_w, h2_s, w3_w, w3_s):
        import jax, jax.numpy as jnp
        import numpy as np
        D_IN, D_HID = (256, 1024)

        def _ternary(key, shape):
            return jax.random.randint(key, shape, -1, 2).astype(jnp.float32)

        def _tlin(x, w, s):
            return jnp.einsum('bsi,oi->bso', x, w) * s
        h = jax.nn.silu(_tlin(x, w1_w, w1_s)) * _tlin(x, w2_w, w2_s)
        h = jax.nn.gelu(_tlin(h, h1_w, h1_s), approximate=False)
        h = jax.nn.gelu(_tlin(h, h2_w, h2_s), approximate=False)
        return _tlin(h, w3_w, w3_s)

    def _L1_xattn_ref(q, k, v, mask, Wq, bq, Wk, bk, Wv, bv, Wo, bo):
        import jax, jax.numpy as jnp
        import numpy as np
        D_MODEL = 256
        NUM_HEADS = 16
        D_K = D_MODEL // NUM_HEADS
        B, S = (4, 512)
        N = q.shape[0]

        def proj(x, W, b):
            y = x @ W.T + b
            return y.reshape(N, -1, NUM_HEADS, D_K).transpose(0, 2, 1, 3)
        qh, kh, vh = (proj(q, Wq, bq), proj(k, Wk, bk), proj(v, Wv, bv))
        scores = jnp.einsum('bhqd,bhkd->bhqk', qh, kh) / jnp.sqrt(jnp.float32(D_K))
        scores = jnp.where(mask == 0, jnp.float32(-1000000000.0), scores)
        attn = jax.nn.softmax(scores, axis=-1)
        x = jnp.einsum('bhqk,bhkd->bhqd', attn, vh)
        x = x.transpose(0, 2, 1, 3).reshape(N, -1, NUM_HEADS * D_K)
        return x @ Wo.T + bo

    def _L1_ffn_ref(x, gate_w, gate_b, w1, b1, w2, b2):
        import jax, jax.numpy as jnp
        import numpy as np
        D = 256
        N_EXP = 8
        TOP_K = 1
        b, s, d = x.shape
        xf = x.reshape(-1, d)
        logits = xf @ gate_w + gate_b
        pb = jax.nn.softmax(logits, axis=-1)
        _, idx = jax.lax.top_k(pb, TOP_K)
        sel = jnp.any(idx[:, :, None] == jnp.arange(N_EXP)[None, None, :], axis=1)
        weights = pb * sel

        def expert_step(acc, params):
            w1e, b1e, w2e, b2e, wgt = params
            h = jax.nn.gelu(xf @ w1e + b1e, approximate=False)
            y = h @ w2e + b2e
            return (acc + wgt[:, None] * y, None)
        out0 = jnp.zeros_like(xf)
        out, _ = jax.lax.scan(expert_step, out0, (w1, b1, w2, b2, weights.T))
        return out.reshape(b, s, d)
    x = x + _L0_xattn_ref(_layernorm(x, axis=-1), ctx_1024, L0_xattn_tab_g, L0_xattn_tab_b, L0_xattn_vid_g, L0_xattn_vid_b, L0_xattn_Wq, L0_xattn_Wk, L0_xattn_Wv, L0_xattn_q_g, L0_xattn_q_b, L0_xattn_k_g, L0_xattn_k_b, L0_xattn_Wo, L0_xattn_bo)
    x = x + _L0_ffn_ref(_layernorm(x, axis=-1), L0_ffn_w1_w, L0_ffn_w1_s, L0_ffn_w2_w, L0_ffn_w2_s, L0_ffn_h1_w, L0_ffn_h1_s, L0_ffn_h2_w, L0_ffn_h2_s, L0_ffn_w3_w, L0_ffn_w3_s)
    x = x + _L1_xattn_ref(_layernorm(x, axis=-1), ctx_1024, ctx_1024, mask_1x1xSxS2_ik1, L1_xattn_Wq, L1_xattn_bq, L1_xattn_Wk, L1_xattn_bk, L1_xattn_Wv, L1_xattn_bv, L1_xattn_Wo, L1_xattn_bo)
    x = x + _L1_ffn_ref(_layernorm(x, axis=-1), L1_ffn_gate_w, L1_ffn_gate_b, L1_ffn_w1, L1_ffn_b1, L1_ffn_w2, L1_ffn_b2)
    return x

_drawn_inputs = setup_inputs


def setup_inputs(seed=0):
    import zlib

    import numpy as np

    out = dict(_drawn_inputs(seed))
    spreads = {'L0_xattn_tab_g': (1.0, 0.2),
     'L0_xattn_tab_b': (0.0, 0.1),
     'L0_xattn_vid_g': (1.0, 0.2),
     'L0_xattn_vid_b': (0.0, 0.1),
     'L0_xattn_q_g': (1.0, 0.2),
     'L0_xattn_q_b': (0.0, 0.1),
     'L0_xattn_k_g': (1.0, 0.2),
     'L0_xattn_k_b': (0.0, 0.1),
     'L0_xattn_bo': (0.0, 0.1),
     'L1_xattn_bq': (0.0, 0.1),
     'L1_xattn_bk': (0.0, 0.1),
     'L1_xattn_bv': (0.0, 0.1),
     'L1_xattn_bo': (0.0, 0.1),
     'L1_ffn_gate_b': (0.0, 0.1),
     'L1_ffn_b1': (0.0, 0.1),
     'L1_ffn_b2': (0.0, 0.1)}
    factors = {}
    for name, (base, spread) in spreads.items():
        noise = np.random.default_rng([zlib.crc32(name.encode()), seed]).standard_normal(out[name].shape)
        drawn = base * np.exp(spread * noise) if base else spread * noise
        out[name] = jnp.asarray(drawn.astype(out[name].dtype))
    for name, factor in factors.items():
        out[name] = (out[name] * factor).astype(out[name].dtype)
    return out
```

```python
from contextlib import ExitStack

import numpy as np

import concourse.bass as bass
from concourse import mybir

F32 = mybir.dt.float32
I32 = mybir.dt.int32
U32 = mybir.dt.uint32
ALU = mybir.AluOpType
ACT = mybir.ActivationFunctionType
AX = mybir.AxisListType

P = 128
B, S, D = 4, 512, 256
KEYS = 64
ROWS = B * KEYS
TT = S // P
NT = B * TT
KD = D // P
H0, DH0 = 12, 64
INNER = H0 * DH0
PAIRS = H0 // 2
HALF = INNER // 2
HP = H0 // 2
H1, DH1 = 16, 16
G1 = P // DH1
NG1 = H1 // G1
PAIRS1 = H1 // 2
HID = 1024
KH = HID // P
E = 8
MT = NT + E
UE = 4
EPS = 1e-5

COLS, NCOLS = {}, 0
for _name, _n in (("vid_g", KD), ("vid_b", KD), ("tab_g", KD), ("tab_b", KD), ("q_g", PAIRS), ("q_b", PAIRS),
                  ("k_g", PAIRS), ("k_b", PAIRS), ("bq", KD), ("bk", KD), ("w1_s", KH), ("w2_s", KH),
                  ("h1_s", KH), ("h2_s", KH)):
    COLS[_name] = NCOLS
    NCOLS += _n
ROW_AT, NROWS = {}, 0
for _name, _n in (("bo0", D), ("s3", D), ("bv", D), ("bo1", D), ("gate_b", E)):
    ROW_AT[_name] = NROWS
    NROWS += _n
CONST_AT, NCONST = {}, 0
for _name, _n in (("ident", P), ("before", P), ("ones", P), ("kmask", G1), ("vmask", TT * P), ("down", E),
                  ("full", NT), ("tile_no", MT), ("minus_half", NT)):
    CONST_AT[_name] = NCONST
    NCONST += _n

A_TP = KD + 2 * PAIRS
A_MM = 2 * TT
C_TP = KD + PAIRS1
F_ACT = 3 * KH
F_DVE = KH + TT
RING = 6


def after(eng, sem, turn, per_turn, n):
    eng.wait_ge(sem, turn * per_turn + (n + 1))


class Order:

    def __init__(self, eng, sem, turn=None, per_turn=0):
        self.eng, self.sem, self.turn, self.per_turn, self.n = eng, sem, turn, per_turn, 0

    def mark(self, ins):
        ins.then_inc(self.sem, 1)
        self.n += 1

    def join(self):
        if self.turn is None:
            self.eng.wait_ge(self.sem, self.n)
        else:
            after(self.eng, self.sem, self.turn, self.per_turn, self.n)

    def step(self, ins):
        self.mark(ins)
        self.join()

    def end(self):
        assert self.n == self.per_turn, (self.n, self.per_turn)


def build(nc, x, ctxt, mask, cols_d, rows_d, const_d, wk0_d, wv0_d, wq0_d, wo0_d, wk1_d, wv1_d, wq1_d, wo1_d,
          fw1_d, fw2_d, fh1_d, fh2_d, fw3_d, gate_w_d, ew1_d, eb1_d, ew2_d, eb2_d, sorted_x, sorted_y, out):
    top = ExitStack()
    with top:
        base = -(-nc.sbuf_base // 128) * 128

        def at(name, shape, kb, dt=F32):
            return nc.alloc_sbuf_tensor_at(name, shape, dt, offset=base + int(kb * 1024))

        def sem(name):
            return top.enter_context(nc.semaphore(name))

        x_res = at("x_res", [P, NT, D], 0)
        xn = at("xn", [P, NT, D], 16)
        const = at("const", [P, NCONST], 32)
        cols = at("cols", [P, NCOLS], 36)
        stats = at("stats", [P, NT, 12], 36.5)
        mean_var = at("mean_var", [P, NT, 2], 37.25)
        var_eps = at("var_eps", [P, NT], 37.375)
        rstd = at("rstd", [P, NT], 37.4375)
        head_max = at("head_max", [P, TT, H1], 205.25)
        head_sum = at("head_sum", [P, TT, H1], 205.5)
        scaled = at("scaled", [P, 2 * PAIRS + KD], 37.75)
        rows = at("rows", [P, NROWS], 38)
        k1T = at("k1T", [P, NG1, ROWS], 42.5)
        v1 = at("v1", [P, B, D], 44.5)
        keep = at("keep", [P, TT, KEYS], 48.5)
        fill = at("fill", [P, TT, KEYS], 49.5)
        wq1 = at("wq1", [P, KD, D], 50.5)
        wo1 = at("wo1", [P, KD, D], 52.5)
        gate_w = at("gate_w", [P, KD, E], 54.5)
        k1_blocks = at("k1_blocks", [P, NG1, G1, KEYS], 55)
        v1_blocks = at("v1_blocks", [P, PAIRS1, P], 59)
        fw1 = at("fw1", [P, KD, HID], 63)
        fw2 = at("fw2", [P, KD, HID], 71)
        fh1 = at("fh1", [P, KH, HID], 79)
        fw3 = at("fw3", [P, KH, D], 111)
        v0 = at("v0", [P, B, INNER], 119)
        k0T = at("k0T", [P, PAIRS, ROWS], 131)
        wq0 = at("wq0", [P, KD, INNER], 137)
        wo0 = at("wo0", [P, PAIRS, D], 143)
        k0_blocks = at("k0_blocks", [P, PAIRS, P], 149)
        v0_blocks = at("v0_blocks", [P, PAIRS, P], 152)
        fh2 = at("fh2", [P, KH, HID], 119)
        wk0 = at("wk0", [P, KD, INNER], 155)
        wv0 = at("wv0", [P, KD, INNER], 161)
        wk1 = at("wk1", [P, KD, D], 167)
        wv1 = at("wv1", [P, KD, D], 169)
        c_raw = at("c_raw", [P, 2, D], 171)
        c_norm = at("c_norm", [P, 2, D], 173)
        kvT = at("kvT", [P, KD, ROWS], 175)
        kvT2 = at("kvT2", [P, KD, B, 2, KEYS], 177)
        cT = at("cT", [P, KD, ROWS], 181)
        cT2 = at("cT2", [P, KD, B, 2, KEYS], 183)
        k_norm = at("k_norm", [P, 2, INNER], 187)
        mask_i = at("mask_i", [P, TT, KEYS], 193, I32)
        zeros = at("zeros", [P, D], 194)
        a_tok = at("a_tok", [P, TT, INNER], 155)
        a_feat = at("a_feat", [P, PAIRS, S], 167)
        a_pT = at("a_pT", [P, PAIRS, S], 179)
        a_xT = at("a_xT", [P, KD, S], 191)
        a_tmp = at("a_tmp", [P, 2, D], 195)
        f_xT = at("f_xT", [P, KD, S], 155)
        f_silu = at("f_silu", [P, 2, S], 159)
        f_ha = at("f_ha", [P, KH, S], 163)
        f_hb = at("f_hb", [P, KH, S], 179)
        f_tmp = at("f_tmp", [P, 2, D], 195)
        c_xT = at("c_xT", [P, KD, S], 155)
        c_qT = at("c_qT", [P, NG1, S], 159)
        c_tok = at("c_tok", [P, TT, H1, KEYS], 163)
        c_pT = at("c_pT", [P, PAIRS1, S], 179)
        c_oT = at("c_oT", [P, NG1, S], 195)
        c_tmp = at("c_tmp", [P, 2, D], 199)
        ew1 = at("ew1", [P, UE, KD, HID], 63)
        ew2 = at("ew2", [P, UE, KH, D], 95)
        eb1 = at("eb1", [P, UE, KH], 127)
        eb2 = at("eb2", [P, UE, D], 128)
        y_back = at("y_back", [P, NT, D], 132)
        xs = at("xs", [P, UE, D], 148)
        xsT = at("xsT", [P, UE, KD, P], 180)
        hT = at("hT", [P, 2, KH, P], 184)
        ys = at("ys", [P, UE, D], 192)
        g_xT = at("g_xT", [P, B, KD, S], 155)
        g_e = at("g_e", [P, NT, E], 171)
        g_max = at("g_max", [P, NT], 171.5)
        g_sum = at("g_sum", [P, NT], 171.75)
        g_inv = at("g_inv", [P, NT], 172)
        g_eq = at("g_eq", [P, NT, E], 172.5)
        g_top = at("g_top", [P, NT], 173)
        g_hot = at("g_hot", [P, NT, E], 173.5)
        weight = at("weight", [P, NT], 174)
        g_pre = at("g_pre", [P, NT + 1, E], 174.5)
        g_tot = at("g_tot", [P, NT, E], 175.5)
        g_cmp = at("g_cmp", [P, E, NT], 176)
        g_tiles = at("g_tiles", [P, E], 176.5)
        g_start = at("g_start", [P, E + 1], 176.75)
        g_slot = at("g_slot", [P, NT, E], 177)
        g_slotf = at("g_slotf", [P, NT], 177.5)
        slot = at("slot", [P, NT], 177.75, U32)
        g_cmp2 = at("g_cmp2", [P, MT, E], 178)
        g_eid = at("g_eid", [P, MT], 179)
        g_base = at("g_base", [P, E], 179.25)
        expert = at("expert", [P, MT], 179.5, I32)

        x_in = at("x_in", [P, TT, D], 201)
        a_new = at("a_new", [P, TT, D], 197)
        c_new = at("c_new", [P, TT, D], 67)

        ps = top.enter_context(nc.psum_tensor("ps", [P, 8, 512], F32))

        def con(name, n):
            return const[:, CONST_AT[name]:CONST_AT[name] + n]

        def col(name, i=0):
            return cols[:, COLS[name] + i:COLS[name] + i + 1]

        def row(name, n=D):
            return rows[:, ROW_AT[name]:ROW_AT[name] + n]

        ident = con("ident", P)
        x_tiles = x.rearrange("b (j p) d -> p (b j) d", p=P)
        out_tiles = out.rearrange("b (j p) d -> p (b j) d", p=P)

        ld_small, ld_kv, ld_x, ld_attn, ld_ffn, ld_h2 = (sem(n) for n in (
            "ld_small", "ld_kv", "ld_x", "ld_attn", "ld_ffn", "ld_h2"))
        zero_filled = sem("zero_filled")

        loop_sems = []

        def loop_sem(name):
            loop_sems.append(sem(name))
            return loop_sems[-1]

        a_tp_full, a_tp_out, a_mm_full, a_mm_taken, a_pv_full, a_pv_out, a_wo_full, a_wo_taken, a_exp, a_prob, \
            a_blocks, a_var, a_rstd, a_xn, a_dve = (loop_sem("a_" + n) for n in (
                "tp_full", "tp_out", "mm_full", "mm_taken", "pv_full", "pv_out", "wo_full", "wo_taken", "exp",
                "prob", "blocks", "var", "rstd", "xn", "dve"))
        a_in, f_in, c_in, a_kept, f_kept, c_kept = (loop_sem(n + m) for m in ("_in", "_kept") for n in "afc")
        f_tp_full, f_tp_out, f_mm_full, f_act_out, f_dve_out, f_var, f_rstd, f_xn, f_dve = (
            loop_sem("f_" + n) for n in ("tp_full", "tp_out", "mm_full", "act_out", "dve_out", "var", "rstd",
                                         "xn", "dve"))
        c_tp_full, c_tp_out, c_q_full, c_q_out, c_s_full, c_s_taken, c_pv_full, c_pv_out, c_wo_full, c_wo_taken, \
            c_sub, c_exp, c_prob, c_blocks, c_var, c_rstd, c_xn, c_dve = (loop_sem("c_" + n) for n in (
                "tp_full", "tp_out", "q_full", "q_out", "s_full", "s_taken", "pv_full", "pv_out", "wo_full",
                "wo_taken", "sub", "exp", "prob", "blocks", "var", "rstd", "xn", "dve"))
        e_tp_full, e_tp_out, e_up_full, e_h_out, e_y_out, e_y_free = (
            loop_sem("e_" + n) for n in ("tp_full", "tp_out", "up_full", "h_out", "y_out", "y_free"))
        e_stored = sem("e_stored")
        e_loaded = [sem(f"e_loaded{u}") for u in range(UE)]
        e_down_full = sem("e_down_full")

        def moments(order, i, chunks):
            nc.vector.nop(nofuse=True)
            for c, chunk in enumerate(chunks):
                order.mark(nc.vector.bn_stats(stats[:, i, 6 * c:6 * c + 6], chunk))
            order.join()
            nc.vector.nop(nofuse=True)
            order.step(nc.vector.bn_aggr(mean_var[:, i, :], stats[:, i, 0:6 * len(chunks)]))

        def add_eps(i, n=1):
            return nc.vector.tensor_scalar_add(var_eps[:, i:i + n], mean_var[:, i:i + n, 1], EPS)

        def rstd_pow(i, n=1):
            return nc.gpsimd.tensor_tensor(rstd[:, i:i + n], var_eps[:, i:i + n], con("minus_half", n), ALU.pow)

        def center_scale(dst, src, i):
            return nc.vector.tensor_scalar(dst, src, mean_var[:, i, 0:1], rstd[:, i:i + 1], ALU.subtract, ALU.mult)

        p_var, p_rstd, p_cnorm, p_knorm, p_pe, p_act, p_v1, p_dve, p_zero = (sem("p_" + n) for n in (
            "var", "rstd", "cnorm", "knorm", "pe", "act", "v1", "dve", "zero"))
        with nc.Block() as block:

            @block.sync
            def _(sp):
                sp.dma_start(c_raw[:], ctxt.rearrange("(r b) k d -> (b k) r d", r=2)).then_inc(ld_small, 16)
                sp.dma_start(const[:], const_d).then_inc(ld_small, 16)
                sp.dma_start(cols[:], cols_d).then_inc(ld_small, 16)
                sp.dma_start(rows[:], rows_d.partition_broadcast(P)).then_inc(ld_small, 16)
                for dst, src in ((wv0, wv0_d), (wk0, wk0_d), (wk1, wk1_d), (wv1, wv1_d)):
                    sp.dma_start(dst[:], src).then_inc(ld_kv, 16)
                sp.dma_start(mask_i[:], mask.rearrange("a b (j p) k -> p (a b j) k", p=P)).then_inc(ld_kv, 16)
                sp.dma_start(x_res[:], x_tiles).then_inc(ld_x, 16)
                for dst, src in ((wq0, wq0_d), (wo0, wo0_d), (wq1, wq1_d), (wo1, wo1_d), (gate_w, gate_w_d)):
                    sp.dma_start(dst[:], src).then_inc(ld_attn, 16)
                for dst, src in ((fw1, fw1_d), (fw2, fw2_d), (fh1, fh1_d), (fw3, fw3_d)):
                    sp.dma_start(dst[:], src).then_inc(ld_ffn, 16)
                sp.wait_ge(p_zero, 3)
                sp.dma_start(sorted_x.rearrange("(t p) d -> p t d", p=P),
                             zeros[:].unsqueeze(1).broadcast_to([P, MT, D])).then_inc(zero_filled, 16)
                sp.wait_ge(zero_filled, 16)

            @block.gpsimd
            def _(pool):
                for s in loop_sems:
                    pool.sem_inc(s, 1)
                pool.sem_inc(e_down_full, UE)
                pool.memset(zeros[:], 0.0).then_inc(p_zero, 1)
                pool.memset(k0_blocks[:], 0.0).then_inc(p_zero, 1)
                pool.memset(v0_blocks[:], 0.0).then_inc(p_zero, 1)
                pool.wait_ge(ld_small, 64)
                for n, (i, m) in enumerate(((0, 2), (2, 1), (3, 1), (0, NT), (0, NT))):
                    pool.wait_ge(p_var, n + 1)
                    rstd_pow(i, m).then_inc(p_rstd, 1)

            @block.vector
            def _(dve):
                order = Order(dve, p_dve)
                dve.wait_ge(ld_small, 64)
                for i in range(2):
                    moments(order, i, [c_raw[:, i, :]])
                add_eps(0, 2).then_inc(p_var, 1)
                nc.vector.tensor_scalar_mul(scaled[:, 0:2 * PAIRS], cols[:, COLS["q_g"]:COLS["q_g"] + 2 * PAIRS],
                                            DH0 ** -0.5)
                nc.vector.tensor_scalar_mul(scaled[:, 2 * PAIRS:], cols[:, COLS["bq"]:COLS["bq"] + KD], DH1 ** -0.5)
                dve.wait_ge(p_rstd, 1)
                for i in range(2):
                    center_scale(c_norm[:, i, :], c_raw[:, i, :], i).then_inc(p_cnorm, 1)
                dve.wait_ge(ld_kv, 80)
                order.step(nc.vector.tensor_copy(keep[:], mask_i[:]))
                order.step(nc.vector.tensor_scalar(keep[:], keep[:], 0.0, None, ALU.not_equal))
                order.step(nc.vector.tensor_scalar(fill[:], keep[:], -1.0, 1e9, ALU.add, ALU.mult))
                for r in range(2):
                    dve.wait_ge(p_pe, 9 + r)
                    banks = [ps[:, 2 * r + h, 0:HALF] for h in range(2)]
                    moments(order, 2 + r, banks)
                    add_eps(2 + r).then_inc(p_var, 1)
                    dve.wait_ge(p_rstd, 2 + r)
                    center_scale(k_norm[:, r, :].rearrange("p (h n) -> p h n", h=2),
                                 ps[:, 2 * r:2 * r + 2, 0:HALF], 2 + r).then_inc(p_knorm, 1)
                for b in range(B):
                    dve.wait_ge(p_pe, 13 + b)
                    nc.vector.tensor_tensor(v1[:, b, :], ps[:, 5 + 2 * (b % 2), 0:D], row("bv"), ALU.add)\
                        .then_inc(p_v1, 1)
                dve.wait_ge(ld_x, 16)
                for n, src in ((0, x_res), (1, xn)):
                    for t in range(NT):
                        order.mark(nc.vector.bn_stats(stats[:, t, 0:6], src[:, t, :]))
                    order.join()
                    for t in range(NT):
                        order.mark(nc.vector.bn_aggr(mean_var[:, t, :], stats[:, t, 0:6]))
                    order.join()
                    add_eps(0, NT).then_inc(p_var, 1)
                    dve.wait_ge(p_rstd, 4 + n)
                    for t in range(NT):
                        order.mark(center_scale(xn[:, t, :], src[:, t, :], t))
                    order.join()

            @block.tensor
            def _(pe):
                pe.wait_ge(ld_small, 64)
                pe.wait_ge(p_cnorm, 2)
                for bank, src in ((0, c_norm), (2, c_raw)):
                    for k in range(KD):
                        for r in range(2):
                            ins = nc.tensor.transpose(ps[:, bank + k, r * P:(r + 1) * P],
                                                      src[:, r, k * P:(k + 1) * P], ident)
                        ins.then_inc(p_pe, 1)
                pe.wait_ge(ld_kv, 80)
                for b in range(B):
                    pe.wait_ge(p_act, 4 if b < 2 else 7 + b)
                    for h in range(2):
                        for k in range(KD):
                            ins = nc.tensor.matmul(ps[:, 4 + 2 * (b % 2) + h, 0:HALF],
                                                   kvT2[:, k, b].rearrange("p a s -> p (a s)"),
                                                   wv0[:, k, h * HALF:(h + 1) * HALF],
                                                   start=(k == 0), stop=(k == KD - 1))
                    ins.then_inc(p_pe, 1)
                pe.wait_ge(p_act, 8)
                for r in range(2):
                    for h in range(2):
                        for k in range(KD):
                            ins = nc.tensor.matmul(ps[:, 2 * r + h, 0:HALF], kvT[:, k, r * P:(r + 1) * P],
                                                   wk0[:, k, h * HALF:(h + 1) * HALF],
                                                   start=(k == 0), stop=(k == KD - 1))
                    ins.then_inc(p_pe, 1)
                for o in range(NG1):
                    pe.wait_ge(p_act, 11 + o)
                    for k in range(KD):
                        ins = nc.tensor.matmul(ps[:, 4 + 2 * o, 0:ROWS], wk1[:, k, o * P:(o + 1) * P], cT[:, k, :],
                                               start=(k == 0), stop=(k == KD - 1))
                    ins.then_inc(p_pe, 1)
                for b in range(B):
                    if b >= 2:
                        pe.wait_ge(p_v1, b - 1)
                    for k in range(KD):
                        ins = nc.tensor.matmul(ps[:, 5 + 2 * (b % 2), 0:D],
                                               cT2[:, k, b].rearrange("p a s -> p (a s)"), wv1[:, k, :],
                                               start=(k == 0), stop=(k == KD - 1))
                    ins.then_inc(p_pe, 1)
                pe.wait_ge(p_knorm, 2)
                for g in range(PAIRS):
                    pe.wait_ge(p_act, 13 + g)
                    for r in range(2):
                        ins = nc.tensor.transpose(ps[:, 4 + 2 * (g % 2), r * P:(r + 1) * P],
                                                  k_norm[:, r, g * P:(g + 1) * P], ident)
                    ins.then_inc(p_pe, 1)

            @block.scalar
            def _(act):
                for n, (bank, one, two) in enumerate(((0, kvT, kvT2), (2, cT, cT2))):
                    for k in range(KD):
                        act.wait_ge(p_pe, 2 * n + k + 1)
                        src = ps[:, bank + k, 0:ROWS]
                        how = dict(scale=col("tab_g", k), bias=col("tab_b", k)) if n == 0 else {}
                        nc.scalar.activation(one[:, k, :], src, ACT.Identity, **how).then_inc(p_act, 1)
                        twice = src.rearrange("p (b s) -> p b s", b=B)
                        for half in range(2):
                            ins = nc.scalar.activation(two[:, k, :, half, :], twice, ACT.Identity, **how)
                        ins.then_inc(p_act, 1)
                for b in range(B):
                    act.wait_ge(p_pe, 5 + b)
                    nc.scalar.activation(v0[:, b, :].rearrange("p (h n) -> p h n", h=2),
                                         ps[:, 4 + 2 * (b % 2):6 + 2 * (b % 2), 0:HALF], ACT.Identity)\
                        .then_inc(p_act, 1)
                for o in range(NG1):
                    act.wait_ge(p_pe, 11 + o)
                    nc.scalar.activation(k1T[:, o, :], ps[:, 4 + 2 * o, 0:ROWS], ACT.Identity, bias=col("bk", o))\
                        .then_inc(p_act, 1)
                for g in range(PAIRS):
                    act.wait_ge(p_pe, 17 + g)
                    nc.scalar.activation(k0T[:, g, :], ps[:, 4 + 2 * (g % 2), 0:ROWS], ACT.Identity,
                                         scale=col("k_g", g), bias=col("k_b", g)).then_inc(p_act, 1)

        def residual_and_norm(dve, order, turn, full, taken, var, rstd_done, norm_done, banks, tmp, new, scale=None,
                              bias=None):
            def signal(which, j):
                s, per_turn, first = which
                after(dve, s, turn, per_turn, first + j + 1)

            def tile(buf, j):
                return buf[:, bass.ts(turn * TT + j, 1), :].rearrange("p a d -> p (a d)")

            def add(j):
                signal(full, j)
                by, op = (bias, ALU.add) if scale is None else (scale, ALU.mult)
                nc.vector.tensor_tensor(tmp[:, j % 2, :], ps[:, banks[j], 0:D], by, op).then_inc(taken[0], 1)
                signal(taken, j)
                order.step(nc.vector.tensor_tensor(new[:, j, :], tile(x_res, j), tmp[:, j % 2, :], ALU.add))
                moments(order, j, [new[:, j, :]])
                add_eps(j).then_inc(var[0], 1)

            def finish(j):
                signal(rstd_done, j)
                center_scale(tile(xn, j), new[:, j, :], j).then_inc(norm_done, 1)

            for j in range(TT):
                add(j)
                if j:
                    finish(j - 1)
            finish(TT - 1)

        A_DVE = TT * 3 + TT * 4 + TT * 3
        with nc.Block() as block:

            @block.gpsimd
            def _(pool):
                with pool.Fori(0, B) as i:
                    after(pool, a_tp_full, i, A_TP, 0)
                    pool.tensor_copy(x_in[:], xn[:, bass.ts(i, TT), :]).then_inc(a_in, 1)
                    after(pool, a_pv_full, i, PAIRS, 0)
                    after(pool, a_in, i, 1, 1)
                    for h in range(2):
                        half = slice(h * DH0, (h + 1) * DH0)
                        if h:
                            after(pool, a_blocks, i, 4, 2)
                        pool.tensor_copy(k0_blocks[half, :, half], k0T[half, :, bass.ts(i, KEYS)])\
                            .then_inc(a_blocks, 1)
                        after(pool, a_blocks, i, 4, 2 * h + 1)
                        pool.tensor_copy(v0_blocks[half, :, half],
                                         v0[half, bass.ts(i, 1), :].rearrange("p a (g c) -> p (a g) c", g=PAIRS)[
                                             :, :, half]).then_inc(a_blocks, 1)
                    after(pool, a_blocks, i, 4, 4)
                    for j in range(TT):
                        after(pool, a_var, i, 2 * TT, j + 1)
                        rstd_pow(TT + j).then_inc(a_rstd, 1)
                    for j in range(TT):
                        after(pool, a_var, i, 2 * TT, TT + j + 1)
                        rstd_pow(j).then_inc(a_rstd, 1)
                        pool.tensor_copy(x_res[:, bass.ts(i * TT + j, 1), :], a_new[:, j:j + 1, :]).then_inc(a_kept, 1)

            @block.tensor
            def _(pe):
                pe.wait_ge(ld_attn, 80)
                with pe.Fori(0, B) as i:
                    after(pe, a_in, i, 1, 1)
                    after(pe, a_tp_out, i, A_TP, 0)
                    for k in range(KD):
                        for j in range(TT):
                            ins = nc.tensor.transpose(ps[:, k, j * P:(j + 1) * P], x_in[:, j, k * P:(k + 1) * P],
                                                      ident)
                        ins.then_inc(a_tp_full, 1)
                    after(pe, a_tp_out, i, A_TP, KD)
                    after(pe, a_mm_taken, i, A_MM, 0)
                    for j in range(TT):
                        if j >= 2:
                            after(pe, a_mm_taken, i, A_MM, j - 1)
                        for h in range(2):
                            for k in range(KD):
                                ins = nc.tensor.matmul(ps[:, 2 + 2 * (j % 2) + h, 0:HALF],
                                                       a_xT[:, k, j * P:(j + 1) * P],
                                                       wq0[:, k, h * HALF:(h + 1) * HALF],
                                                       start=(k == 0), stop=(k == KD - 1))
                        ins.then_inc(a_mm_full, 1)
                    after(pe, a_mm_taken, i, A_MM, TT)
                    for g in range(PAIRS):
                        after(pe, a_tp_out, i, A_TP, KD + g - 1)
                        for j in range(TT):
                            ins = nc.tensor.transpose(ps[:, g % 2, j * P:(j + 1) * P],
                                                      a_tok[:, j, g * P:(g + 1) * P], ident)
                        ins.then_inc(a_tp_full, 1)
                    after(pe, a_tp_out, i, A_TP, KD + PAIRS)
                    after(pe, a_blocks, i, 4, 4)
                    for j in range(TT):
                        after(pe, a_mm_taken, i, A_MM, TT + j - 1)
                        for g in range(PAIRS):
                            ins = nc.tensor.matmul(
                                ps[:, 2 + 2 * (j % 2) + g // 3, (g % 3) * P:(g % 3 + 1) * P],
                                a_feat[:, g, j * P:(j + 1) * P], k0_blocks[:, g, :], start=True, stop=True)
                        ins.then_inc(a_mm_full, 1)
                    after(pe, a_prob, i, TT, TT)
                    for g in range(PAIRS):
                        after(pe, a_tp_out, i, A_TP, KD + PAIRS + g - 1)
                        for j in range(TT):
                            ins = nc.tensor.transpose(ps[:, g % 2, j * P:(j + 1) * P],
                                                      a_tok[:, j, g * P:(g + 1) * P], ident)
                        ins.then_inc(a_tp_full, 1)
                    after(pe, a_wo_taken, i, TT, 0)
                    for g in range(PAIRS):
                        after(pe, a_tp_out, i, A_TP, KD + PAIRS + g + 1)
                        after(pe, a_pv_out, i, PAIRS, max(g - 1, 0))
                        nc.tensor.matmul(ps[:, 6 + g % 2, :], v0_blocks[:, g, :], a_pT[:, g, :],
                                         start=True, stop=True).then_inc(a_pv_full, 1)
                    after(pe, a_pv_out, i, PAIRS, PAIRS)
                    for j in range(TT):
                        after(pe, a_wo_taken, i, TT, max(j - 1, 0))
                        for g in range(PAIRS):
                            ins = nc.tensor.matmul(ps[:, 7 - j % 2, 0:D], a_feat[:, g, j * P:(j + 1) * P],
                                                   wo0[:, g, :], start=(g == 0), stop=(g == PAIRS - 1))
                        ins.then_inc(a_wo_full, 1)

            @block.scalar
            def _(act):
                with act.Fori(0, B) as i:
                    for k in range(KD):
                        after(act, a_tp_full, i, A_TP, k + 1)
                        nc.scalar.activation(a_xT[:, k, :], ps[:, k, :], ACT.Identity, scale=col("vid_g", k),
                                             bias=col("vid_b", k)).then_inc(a_tp_out, 1)
                    for g in range(PAIRS):
                        after(act, a_tp_full, i, A_TP, KD + g + 1)
                        nc.scalar.activation(a_feat[:, g, :], ps[:, g % 2, :], ACT.Identity,
                                             scale=scaled[:, g:g + 1], bias=scaled[:, PAIRS + g:PAIRS + g + 1])\
                            .then_inc(a_tp_out, 1)
                    for j in range(TT):
                        after(act, a_mm_taken, i, A_MM, TT + j + 1)
                        nc.scalar.activation(a_tok[:, j, :], a_tok[:, j, :], ACT.Exp).then_inc(a_exp, 1)
                    for g in range(PAIRS):
                        after(act, a_tp_full, i, A_TP, KD + PAIRS + g + 1)
                        nc.scalar.activation(a_pT[:, g, :], ps[:, g % 2, :], ACT.Identity).then_inc(a_tp_out, 1)
                    for g in range(PAIRS):
                        after(act, a_pv_full, i, PAIRS, g + 1)
                        nc.scalar.activation(a_feat[:, g, :], ps[:, 6 + g % 2, :], ACT.Identity)\
                            .then_inc(a_pv_out, 1)

            @block.vector
            def _(dve):
                with dve.Fori(0, B) as i:
                    order = Order(dve, a_dve, i, A_DVE)

                    def q_moments(j):
                        after(dve, a_mm_full, i, A_MM, j + 1)
                        moments(order, TT + j, [ps[:, 2 + 2 * (j % 2) + h, 0:HALF] for h in range(2)])
                        add_eps(TT + j).then_inc(a_var, 1)

                    def q_norm(j):
                        after(dve, a_rstd, i, 2 * TT, j + 1)
                        center_scale(a_tok[:, j, :].rearrange("p (h n) -> p h n", h=2),
                                     ps[:, 2 + 2 * (j % 2):4 + 2 * (j % 2), 0:HALF], TT + j)\
                            .then_inc(a_mm_taken, 1)

                    q_moments(0)
                    for j in range(TT):
                        if j + 1 < TT:
                            q_moments(j + 1)
                        q_norm(j)

                    def subtract_max(j):
                        after(dve, a_mm_full, i, A_MM, TT + j + 1)
                        top_ = head_max[:, j, 0:H0]
                        banks = ps[:, 2 + 2 * (j % 2):4 + 2 * (j % 2), 0:HALF].rearrange(
                            "p h (n k) -> p h n k", k=KEYS)
                        order.step(nc.vector.tensor_reduce(top_.rearrange("p (h n) -> p h n", h=2), banks, AX.X,
                                                           ALU.max))
                        for h in range(2):
                            ins = nc.vector.tensor_tensor(
                                a_tok[:, j, h * HALF:(h + 1) * HALF].rearrange("p (n k) -> p n k", k=KEYS),
                                banks[:, h], top_[:, h * HP:(h + 1) * HP].unsqueeze(2).broadcast_to([P, HP, KEYS]),
                                ALU.subtract)
                            if h == 0:
                                order.mark(ins)
                        ins.then_inc(a_mm_taken, 1)

                    def divide(j):
                        after(dve, a_exp, i, TT, j + 1)
                        sums = head_sum[:, j, 0:H0]
                        heads = a_tok[:, j, :].rearrange("p (n k) -> p n k", k=KEYS)
                        order.step(nc.vector.tensor_reduce(sums, heads, AX.X, ALU.add))
                        order.step(nc.vector.reciprocal(sums, sums))
                        nc.vector.tensor_tensor(heads, heads, sums.unsqueeze(2).broadcast_to([P, H0, KEYS]), ALU.mult)\
                            .then_inc(a_prob, 1)

                    subtract_max(0)
                    for j in range(TT):
                        if j + 1 < TT:
                            subtract_max(j + 1)
                        divide(j)
                    residual_and_norm(dve, order, i, (a_wo_full, TT, 0), (a_wo_taken, TT, 0), (a_var, 2 * TT, TT),
                                      (a_rstd, 2 * TT, TT), a_xn, [7, 6, 7, 6], a_tmp, a_new, bias=row("bo0"))
                    order.end()

        def ring_bank(n):
            return 2 + n % RING

        def ring_free(pe, turn, n):
            n -= RING
            if n < 0:
                after(pe, f_act_out, turn, F_ACT, 0)
                after(pe, f_dve_out, turn, F_DVE, 0)
            elif n < 2 * KH:
                after(pe, *((f_dve_out, turn, F_DVE) if n % 2 else (f_act_out, turn, F_ACT)), n // 2 + 1)
            elif n < 4 * KH:
                after(pe, f_act_out, turn, F_ACT, KH + n - 2 * KH + 1)
            else:
                after(pe, f_dve_out, turn, F_DVE, KH + n - 4 * KH + 1)

        F_MM = 4 * KH + TT
        assert F_MM % RING == 0
        with nc.Block() as block:

            @block.sync
            def _(sp):
                sp.dma_start(fh2[:], fh2_d).then_inc(ld_h2, 16)

            @block.gpsimd
            def _(pool):
                with pool.Fori(0, B) as i:
                    after(pool, f_tp_full, i, KD, 0)
                    pool.tensor_copy(x_in[:], xn[:, bass.ts(i, TT), :]).then_inc(f_in, 1)
                    for j in range(TT):
                        after(pool, f_var, i, TT, j + 1)
                        rstd_pow(j).then_inc(f_rstd, 1)
                        pool.tensor_copy(x_res[:, bass.ts(i * TT + j, 1), :], a_new[:, j:j + 1, :]).then_inc(f_kept, 1)

            @block.tensor
            def _(pe):
                pe.wait_ge(ld_ffn, 64)
                pe.wait_ge(ld_h2, 16)
                with pe.Fori(0, B) as i:
                    after(pe, f_in, i, 1, 1)
                    after(pe, f_tp_out, i, KD, 0)
                    for k in range(KD):
                        for j in range(TT):
                            ins = nc.tensor.transpose(ps[:, k, j * P:(j + 1) * P], x_in[:, j, k * P:(k + 1) * P],
                                                      ident)
                        ins.then_inc(f_tp_full, 1)
                    after(pe, f_tp_out, i, KD, KD)
                    for o in range(KH):
                        for n, w in ((2 * o, fw1), (2 * o + 1, fw2)):
                            ring_free(pe, i, n)
                            for k in range(KD):
                                ins = nc.tensor.matmul(ps[:, ring_bank(n), :], w[:, k, o * P:(o + 1) * P],
                                                       f_xT[:, k, :], start=(k == 0), stop=(k == KD - 1))
                            ins.then_inc(f_mm_full, 1)
                    for first, w, src, ready in ((2 * KH, fh1, f_ha, (f_dve_out, F_DVE, 0)),
                                                 (3 * KH, fh2, f_hb, (f_act_out, F_ACT, KH))):
                        for o in range(KH):
                            ring_free(pe, i, first + o)
                            for k in range(KH):
                                if o == 0:
                                    after(pe, ready[0], i, ready[1], ready[2] + k + 1)
                                ins = nc.tensor.matmul(ps[:, ring_bank(first + o), :], w[:, k, o * P:(o + 1) * P],
                                                       src[:, k, :], start=(k == 0), stop=(k == KH - 1))
                            ins.then_inc(f_mm_full, 1)
                    for j in range(TT):
                        n = 4 * KH + j
                        ring_free(pe, i, n)
                        for k in range(KH):
                            if j == 0:
                                after(pe, f_act_out, i, F_ACT, 2 * KH + k + 1)
                            ins = nc.tensor.matmul(ps[:, ring_bank(n), 0:D], f_ha[:, k, j * P:(j + 1) * P],
                                                   fw3[:, k, :], start=(k == 0), stop=(k == KH - 1))
                        ins.then_inc(f_mm_full, 1)

            @block.scalar
            def _(act):
                with act.Fori(0, B) as i:
                    for k in range(KD):
                        after(act, f_tp_full, i, KD, k + 1)
                        nc.scalar.activation(f_xT[:, k, :], ps[:, k, :], ACT.Identity).then_inc(f_tp_out, 1)
                    for o in range(KH):
                        after(act, f_mm_full, i, F_MM, 2 * o + 1)
                        if o >= 2:
                            after(act, f_dve_out, i, F_DVE, o - 1)
                        nc.scalar.activation(f_silu[:, o % 2, :], ps[:, ring_bank(2 * o), :], ACT.Silu,
                                             scale=col("w1_s", o)).then_inc(f_act_out, 1)
                    for first, dst, scale in ((2 * KH, f_hb, "h1_s"), (3 * KH, f_ha, "h2_s")):
                        for o in range(KH):
                            after(act, f_mm_full, i, F_MM, first + o + 1)
                            nc.scalar.activation(dst[:, o, :], ps[:, ring_bank(first + o), :], ACT.Gelu,
                                                 scale=col(scale, o)).then_inc(f_act_out, 1)

            @block.vector
            def _(dve):
                with dve.Fori(0, B) as i:
                    order = Order(dve, f_dve, i, 3 * TT)
                    for o in range(KH):
                        after(dve, f_mm_full, i, F_MM, 2 * o + 2)
                        after(dve, f_act_out, i, F_ACT, o + 1)
                        nc.vector.scalar_tensor_tensor(f_ha[:, o, :], ps[:, ring_bank(2 * o + 1), :],
                                                       col("w2_s", o), f_silu[:, o % 2, :], ALU.mult, ALU.mult)\
                            .then_inc(f_dve_out, 1)
                    residual_and_norm(dve, order, i, (f_mm_full, F_MM, 4 * KH), (f_dve_out, F_DVE, KH),
                                      (f_var, TT, 0), (f_rstd, TT, 0), f_xn,
                                      [ring_bank(4 * KH + j) for j in range(TT)], f_tmp, a_new, scale=row("s3"))
                    order.end()

        with nc.Block() as block:

            @block.gpsimd
            def _(pool):
                with pool.Fori(0, B) as i:
                    after(pool, c_tp_full, i, C_TP, 0)
                    pool.tensor_copy(x_in[:], xn[:, bass.ts(i, TT), :]).then_inc(c_in, 1)
                    after(pool, c_pv_full, i, NG1, 0)
                    for o in range(NG1):
                        pool.tensor_tensor(k1_blocks[:, o],
                                           k1T[:, o, bass.ts(i, KEYS)].unsqueeze(1).broadcast_to([P, G1, KEYS]),
                                           con("kmask", G1).unsqueeze(2).broadcast_to([P, G1, KEYS]), ALU.mult)\
                            .then_inc(c_blocks, 1)
                        pool.tensor_tensor(v1_blocks[:, o * TT:(o + 1) * TT, :],
                                           v1[:, bass.ts(i, 1), o * P:(o + 1) * P].broadcast_to([P, TT, P]),
                                           con("vmask", TT * P).rearrange("p (a c) -> p a c", c=P), ALU.mult)\
                            .then_inc(c_blocks, 1)
                    for j in range(TT):
                        after(pool, c_var, i, TT, j + 1)
                        rstd_pow(j).then_inc(c_rstd, 1)
                        pool.tensor_copy(x_res[:, bass.ts(i * TT + j, 1), :], c_new[:, j:j + 1, :]).then_inc(c_kept, 1)

            @block.tensor
            def _(pe):
                with pe.Fori(0, B) as i:
                    after(pe, c_in, i, 1, 1)
                    after(pe, c_tp_out, i, C_TP, 0)
                    for k in range(KD):
                        for j in range(TT):
                            ins = nc.tensor.transpose(ps[:, k, j * P:(j + 1) * P], x_in[:, j, k * P:(k + 1) * P],
                                                      ident)
                        ins.then_inc(c_tp_full, 1)
                    after(pe, c_tp_out, i, C_TP, KD)
                    after(pe, c_wo_taken, i, TT, 0)
                    for o in range(NG1):
                        for k in range(KD):
                            ins = nc.tensor.matmul(ps[:, 6 + o, :], wq1[:, k, o * P:(o + 1) * P], c_xT[:, k, :],
                                                   start=(k == 0), stop=(k == KD - 1))
                        ins.then_inc(c_q_full, 1)
                    after(pe, c_q_out, i, NG1, NG1)
                    after(pe, c_blocks, i, 2 * NG1, 2 * NG1)
                    for j in range(TT):
                        after(pe, c_s_taken, i, TT, max(j - 1, 0))
                        for o in range(NG1):
                            ins = nc.tensor.matmul(ps[:, 2 + 2 * (j % 2) + o, :], c_qT[:, o, j * P:(j + 1) * P],
                                                   k1_blocks[:, o].rearrange("p g k -> p (g k)"),
                                                   start=True, stop=True)
                        ins.then_inc(c_s_full, 1)
                    after(pe, c_prob, i, TT, TT)
                    for g in range(PAIRS1):
                        after(pe, c_tp_out, i, C_TP, KD + g - 1)
                        for j in range(TT):
                            ins = nc.tensor.transpose(ps[:, g % 2, j * P:(j + 1) * P],
                                                      c_tok[:, j, 2 * g:2 * g + 2, :].rearrange("p a k -> p (a k)"),
                                                      ident)
                        ins.then_inc(c_tp_full, 1)
                    for o in range(NG1):
                        for q in range(TT):
                            g = o * TT + q
                            after(pe, c_tp_out, i, C_TP, KD + g + 1)
                            ins = nc.tensor.matmul(ps[:, 6 + o, :], v1_blocks[:, g, :], c_pT[:, g, :],
                                                   start=(q == 0), stop=(q == TT - 1))
                        ins.then_inc(c_pv_full, 1)
                    after(pe, c_pv_out, i, NG1, NG1)
                    for j in range(TT):
                        after(pe, c_wo_taken, i, TT, max(j - 1, 0))
                        for o in range(NG1):
                            ins = nc.tensor.matmul(ps[:, 7 - j % 2, 0:D], c_oT[:, o, j * P:(j + 1) * P],
                                                   wo1[:, o, :], start=(o == 0), stop=(o == NG1 - 1))
                        ins.then_inc(c_wo_full, 1)

            @block.scalar
            def _(act):
                with act.Fori(0, B) as i:
                    for k in range(KD):
                        after(act, c_tp_full, i, C_TP, k + 1)
                        nc.scalar.activation(c_xT[:, k, :], ps[:, k, :], ACT.Identity).then_inc(c_tp_out, 1)
                    for o in range(NG1):
                        after(act, c_q_full, i, NG1, o + 1)
                        nc.scalar.activation(c_qT[:, o, :], ps[:, 6 + o, :], ACT.Identity, scale=DH1 ** -0.5,
                                             bias=scaled[:, 2 * PAIRS + o:2 * PAIRS + o + 1]).then_inc(c_q_out, 1)
                    for j in range(TT):
                        after(act, c_sub, i, TT, j + 1)
                        nc.scalar.activation(c_tok[:, j], c_tok[:, j], ACT.Exp).then_inc(c_exp, 1)
                    for g in range(PAIRS1):
                        after(act, c_tp_full, i, C_TP, KD + g + 1)
                        nc.scalar.activation(c_pT[:, g, :], ps[:, g % 2, :], ACT.Identity).then_inc(c_tp_out, 1)
                    for o in range(NG1):
                        after(act, c_pv_full, i, NG1, o + 1)
                        nc.scalar.activation(c_oT[:, o, :], ps[:, 6 + o, :], ACT.Identity).then_inc(c_pv_out, 1)

            @block.vector
            def _(dve):
                with dve.Fori(0, B) as i:
                    order = Order(dve, c_dve, i, 8 * TT)

                    def subtract_max(j):
                        after(dve, c_s_full, i, TT, j + 1)
                        mask_row = keep[:, j:j + 1, :].broadcast_to([P, G1, KEYS])
                        for o in range(NG1):
                            ins = nc.vector.tensor_tensor(
                                c_tok[:, j, o * G1:(o + 1) * G1, :],
                                ps[:, 2 + 2 * (j % 2) + o, :].rearrange("p (g k) -> p g k", k=KEYS), mask_row,
                                ALU.mult)
                            if o == 0:
                                order.mark(ins)
                        ins.then_inc(c_s_taken, 1)
                        order.join()
                        after(dve, c_s_taken, i, TT, j + 1)
                        order.step(nc.vector.tensor_tensor(c_tok[:, j], c_tok[:, j],
                                                           fill[:, j:j + 1, :].broadcast_to([P, H1, KEYS]), ALU.add))
                        top_ = head_max[:, j, :]
                        order.step(nc.vector.tensor_reduce(top_, c_tok[:, j], AX.X, ALU.max))
                        nc.vector.tensor_tensor(c_tok[:, j], c_tok[:, j],
                                                top_.unsqueeze(2).broadcast_to([P, H1, KEYS]), ALU.subtract)\
                            .then_inc(c_sub, 1)

                    def divide(j):
                        after(dve, c_exp, i, TT, j + 1)
                        sums = head_sum[:, j, :]
                        order.step(nc.vector.tensor_reduce(sums, c_tok[:, j], AX.X, ALU.add))
                        order.step(nc.vector.reciprocal(sums, sums))
                        nc.vector.tensor_tensor(c_tok[:, j], c_tok[:, j],
                                                sums.unsqueeze(2).broadcast_to([P, H1, KEYS]), ALU.mult)\
                            .then_inc(c_prob, 1)

                    subtract_max(0)
                    for j in range(TT):
                        if j + 1 < TT:
                            subtract_max(j + 1)
                        divide(j)
                    residual_and_norm(dve, order, i, (c_wo_full, TT, 0), (c_wo_taken, TT, 0), (c_var, TT, 0),
                                      (c_rstd, TT, 0), c_xn, [7, 6, 7, 6], c_tmp, c_new, bias=row("bo1"))
                    order.end()

        g_tp, g_out, g_mm, g_v, g_act, g_dve, g_dve_own, slots_ready, expert_ready, scattered, gathered, combined, stored = (
            sem(n) for n in ("g_tp", "g_out", "g_mm", "g_v", "g_act", "g_dve", "g_dve_own", "slots_ready", "expert_ready",
                             "scattered", "gathered", "combined", "stored"))
        w1_rows = ew1_d.rearrange("e p k n -> (e p) k n")
        w2_rows = ew2_d.rearrange("e p k n -> (e p) k n")
        b1_rows = eb1_d.rearrange("e p k -> (e p) k")
        with nc.Block() as block:

            @block.sync
            def _(sp):
                sp.wait_ge(scattered, 16 * NT)
                sp.wait_ge(expert_ready, 1)
                with sp.Fori(0, MT // UE) as i:
                    for u in range(UE):
                        e = sp.value_load(expert[0:1, bass.ts(i * UE + u, 1)], min_val=0, max_val=E - 1)
                        sp.wait_ge(e_down_full, i * UE + (u + 1))
                        after(sp, e_y_out, i, UE, 0)
                        for dst, src in ((xs[:, u, :], sorted_x[bass.ts(i * UE + u, P), :]),
                                         (ew1[:, u], w1_rows[bass.ts(e, P)]),
                                         (eb1[:, u, :], b1_rows[bass.ts(e, P), :]),
                                         (ew2[:, u], w2_rows[bass.ts(e, P)]),
                                         (eb2[:, u, :], eb2_d[bass.ts(e, 1), :].broadcast_to([P, D]))):
                            sp.dma_start(dst, src).then_inc(e_loaded[u], 16)
                for b in range(B):
                    sp.wait_ge(combined, TT * (b + 1))
                    sp.dma_start(out_tiles[:, b * TT:(b + 1) * TT, :], x_res[:, b * TT:(b + 1) * TT, :])\
                        .then_inc(stored, 16)
                sp.wait_ge(stored, 16 * B)

            @block.gpsimd
            def _(pool):
                pool.wait_ge(slots_ready, 1)
                for t in range(NT):
                    pool.indirect_dma_start(sorted_x, bass.IndirectOffsetOnAxis(ap=slot[:, t:t + 1], axis=0),
                                            xn[:, t, :], None).then_inc(scattered, 16)
                with pool.Fori(0, MT // UE) as i:
                    for u in range(UE):
                        after(pool, e_y_out, i, UE, u + 1)
                        pool.dma_start(sorted_y[bass.ts(i * UE + u, P), :], ys[:, u, :]).then_inc(e_stored, 16)
                    pool.wait_ge(e_stored, i * (16 * UE) + 16 * UE)
                    pool.sem_inc(e_y_free, 1)
                for t in range(NT):
                    pool.indirect_dma_start(y_back[:, t, :], None, sorted_y,
                                            bass.IndirectOffsetOnAxis(ap=slot[:, t:t + 1], axis=0))\
                        .then_inc(gathered, 16)
                pool.wait_ge(gathered, 16 * NT)

            @block.tensor
            def _(pe):
                for b in range(B):
                    for k in range(KD):
                        if b:
                            pe.wait_ge(g_out, KD * (b - 1) + k + 1)
                        for j in range(TT):
                            ins = nc.tensor.transpose(ps[:, k, j * P:(j + 1) * P],
                                                      xn[:, b * TT + j, k * P:(k + 1) * P], ident)
                        ins.then_inc(g_tp, 1)
                for b in range(B):
                    pe.wait_ge(g_out, KD * (b + 1))
                    for j in range(TT):
                        for k in range(KD):
                            t = b * TT + j
                            ins = nc.tensor.matmul(ps[:, 2, t * E:(t + 1) * E], g_xT[:, b, k, j * P:(j + 1) * P],
                                                   gate_w[:, k, :], start=(k == 0), stop=(k == KD - 1))
                ins.then_inc(g_mm, 1)
                pe.wait_ge(g_v, 2)
                hot = g_hot[:].rearrange("p t e -> p (t e)")
                nc.tensor.matmul(ps[:, 3, 0:P], con("before", P), hot, start=True, stop=True).then_inc(g_mm, 1)
                nc.tensor.matmul(ps[:, 4, 0:P], con("ones", P), hot, start=True, stop=True).then_inc(g_mm, 1)
                pe.wait_ge(g_dve, 1)

                with pe.Fori(0, MT // UE) as i:
                    def up(u):
                        pe.wait_ge(e_loaded[u], i * 80 + 80)
                        after(pe, e_tp_out, i, UE, u)
                        for k in range(KD):
                            ins = nc.tensor.transpose(ps[:, 0, k * P:(k + 1) * P], xs[:, u, k * P:(k + 1) * P],
                                                      ident)
                        ins.then_inc(e_tp_full, 1)
                        after(pe, e_tp_out, i, UE, u + 1)
                        after(pe, e_h_out, i, UE, max(u - 1, 0))
                        for o in range(KH):
                            for k in range(KD):
                                ins = nc.tensor.matmul(
                                    ps[:, 2 + 2 * (u % 2) + o // 4, (o % 4) * P:(o % 4 + 1) * P],
                                    ew1[:, u, k, o * P:(o + 1) * P], xsT[:, u, k, :],
                                    start=(k == 0), stop=(k == KD - 1))
                        ins.then_inc(e_up_full, 1)

                    def down(u):
                        after(pe, e_h_out, i, UE, u + 1)
                        after(pe, e_y_out, i, UE, max(u - 1, 0))
                        for k in range(KH):
                            ins = nc.tensor.matmul(ps[:, 6 + u % 2, 0:D], hT[:, u % 2, k, :], ew2[:, u, k, :],
                                                   start=(k == 0), stop=(k == KH - 1))
                        ins.then_inc(e_down_full, 1)

                    up(0)
                    for u in range(1, UE):
                        up(u)
                        down(u - 1)
                    down(UE - 1)

            @block.scalar
            def _(act):
                for b in range(B):
                    for k in range(KD):
                        act.wait_ge(g_tp, KD * b + k + 1)
                        nc.scalar.activation(g_xT[:, b, k, :], ps[:, k, :], ACT.Identity).then_inc(g_out, 1)
                act.wait_ge(g_v, 1)
                nc.scalar.activation(g_e[:], g_e[:], ACT.Exp).then_inc(g_act, 1)
                with act.Fori(0, MT // UE) as i:
                    for u in range(UE):
                        after(act, e_tp_full, i, UE, u + 1)
                        nc.scalar.activation(xsT[:, u].rearrange("p k n -> p (k n)"), ps[:, 0, 0:D], ACT.Identity)\
                            .then_inc(e_tp_out, 1)
                        after(act, e_up_full, i, UE, u + 1)
                        act.wait_ge(e_down_full, i * UE + (u - 1 + UE))
                        for o in range(KH):
                            ins = nc.scalar.activation(hT[:, u % 2, o, :],
                                                       ps[:, 2 + 2 * (u % 2) + o // 4, (o % 4) * P:(o % 4 + 1) * P],
                                                       ACT.Gelu, bias=eb1[:, u, o:o + 1])
                        ins.then_inc(e_h_out, 1)

            @block.vector
            def _(dve):
                order = Order(dve, g_dve_own)

                def spread(ap, n=E):
                    return ap.unsqueeze(2).broadcast_to([P, NT, n])

                dve.wait_ge(g_mm, 1)
                order.step(nc.vector.tensor_tensor(
                    g_e[:], ps[:, 2, 0:NT * E].rearrange("p (t e) -> p t e", e=E),
                    row("gate_b", E).unsqueeze(1).broadcast_to([P, NT, E]), ALU.add))
                order.step(nc.vector.tensor_reduce(g_max[:], g_e[:], AX.X, ALU.max))
                nc.vector.tensor_tensor(g_e[:], g_e[:], spread(g_max[:]), ALU.subtract).then_inc(g_v, 1)
                dve.wait_ge(g_act, 1)
                order.step(nc.vector.tensor_reduce(g_sum[:], g_e[:], AX.X, ALU.add))
                order.step(nc.vector.reciprocal(g_inv[:], g_sum[:]))
                order.step(nc.vector.tensor_tensor(g_e[:], g_e[:], spread(g_inv[:]), ALU.mult))
                order.step(nc.vector.tensor_reduce(weight[:], g_e[:], AX.X, ALU.max))
                order.step(nc.vector.tensor_tensor(g_eq[:], g_e[:], spread(weight[:]), ALU.is_equal))
                order.step(nc.vector.tensor_tensor(
                    g_eq[:], g_eq[:], con("down", E).unsqueeze(1).broadcast_to([P, NT, E]), ALU.mult))
                order.step(nc.vector.tensor_reduce(g_top[:], g_eq[:], AX.X, ALU.max))
                nc.vector.tensor_tensor(g_hot[:], g_eq[:], spread(g_top[:]), ALU.is_equal).then_inc(g_v, 1)
                dve.wait_ge(g_mm, 3)
                order.mark(nc.vector.memset(g_pre[:, 0, :], 0.0))
                order.mark(nc.vector.memset(g_start[:, 0:1], 0.0))
                order.step(nc.vector.tensor_copy(g_tot[:].rearrange("p t e -> p (t e)"), ps[:, 4, 0:P]))
                for t in range(NT):
                    order.step(nc.vector.tensor_tensor(g_pre[:, t + 1, :], g_pre[:, t, :], g_tot[:, t, :], ALU.add))
                order.step(nc.vector.tensor_tensor(g_cmp[:], g_pre[:, NT, :].unsqueeze(2).broadcast_to([P, E, NT]),
                                                   con("full", NT).unsqueeze(1).broadcast_to([P, E, NT]),
                                                   ALU.is_gt))
                order.step(nc.vector.tensor_reduce(g_tiles[:], g_cmp[:], AX.X, ALU.add))
                for e in range(E):
                    order.step(nc.vector.tensor_tensor(g_start[:, e + 1:e + 2], g_start[:, e:e + 1],
                                                       g_tiles[:, e:e + 1], ALU.add))
                order.step(nc.vector.tensor_tensor(g_cmp2[:], con("tile_no", MT).unsqueeze(2).broadcast_to([P, MT, E]),
                                                   g_start[:, 1:E + 1].unsqueeze(1).broadcast_to([P, MT, E]),
                                                   ALU.is_ge))
                order.step(nc.vector.tensor_reduce(g_eid[:], g_cmp2[:], AX.X, ALU.add))
                order.step(nc.vector.tensor_scalar(g_eid[:], g_eid[:], float(E - 1), None, ALU.min))
                nc.vector.tensor_copy(expert[:], g_eid[:]).then_inc(expert_ready, 1)
                order.step(nc.vector.tensor_scalar(g_base[:], g_start[:, 0:E], float(P), None, ALU.mult))
                order.step(nc.vector.tensor_tensor(g_slot[:], g_pre[:, 0:NT, :],
                                                   g_base[:].unsqueeze(1).broadcast_to([P, NT, E]), ALU.add))
                ins = nc.vector.tensor_tensor(g_slot[:].rearrange("p t e -> p (t e)"), ps[:, 3, 0:P],
                                              g_slot[:].rearrange("p t e -> p (t e)"), ALU.add)
                ins.then_inc(g_dve, 1)
                dve.wait_ge(g_dve, 1)
                order.step(nc.vector.tensor_tensor(g_slot[:], g_slot[:], g_hot[:], ALU.mult))
                order.step(nc.vector.tensor_reduce(g_slotf[:], g_slot[:], AX.X, ALU.add))
                nc.vector.tensor_copy(slot[:], g_slotf[:]).then_inc(slots_ready, 1)
                with dve.Fori(0, MT // UE) as i:
                    for u in range(UE):
                        dve.wait_ge(e_down_full, i * UE + (u + 1 + UE))
                        if u == 0:
                            after(dve, e_y_free, i, 1, 0)
                        nc.vector.tensor_tensor(ys[:, u, :], ps[:, 6 + u % 2, 0:D], eb2[:, u, :], ALU.add)\
                            .then_inc(e_y_out, 1)
                dve.wait_ge(gathered, 16 * NT)
                for t in range(NT):
                    nc.vector.scalar_tensor_tensor(x_res[:, t, :], y_back[:, t, :], weight[:, t:t + 1], x_res[:, t, :],
                                                   ALU.mult, ALU.add).then_inc(combined, 1)


def chunks(w):
    k, n = w.shape
    return np.ascontiguousarray(w.reshape(k // P, P, n).transpose(1, 0, 2))


def shape_constants():
    p = np.arange(P)
    c = np.zeros((P, NCONST), np.float32)

    def put(name, a):
        a = np.asarray(a, np.float32).reshape(a.shape[0], -1)
        c[:, CONST_AT[name]:CONST_AT[name] + a.shape[1]] = a

    put("ident", np.eye(P))
    put("before", p[:, None] < p[None, :])
    put("ones", np.ones((P, P)))
    put("kmask", p[:, None] // DH1 == np.arange(G1)[None, :])
    put("vmask", (p // DH1)[None, None, :] == 2 * np.arange(TT)[None, :, None] + (p // KEYS)[:, None, None])
    put("down", np.broadcast_to(E - np.arange(E), (P, E)))
    put("full", np.broadcast_to(P * np.arange(NT), (P, NT)))
    put("tile_no", np.broadcast_to(np.arange(MT), (P, MT)))
    put("minus_half", np.full((P, NT), -0.5))
    return c


def kernel(**inputs):
    import concourse.bacc as bacc
    from concourse.bass_utils import run_bass_kernel_spmd

    a = {k: np.asarray(v) for k, v in inputs.items()}
    f0, f1 = "L0_xattn_", "L1_xattn_"
    cols = [a[f0 + n] for n in ("vid_g", "vid_b", "tab_g", "tab_b", "q_g", "q_b", "k_g", "k_b")]
    cols += [a[f1 + n] for n in ("bq", "bk")] + [a["L0_ffn_" + n] for n in ("w1_s", "w2_s", "h1_s", "h2_s")]
    rows = [a[f0 + "bo"], a["L0_ffn_w3_s"], a[f1 + "bv"], a[f1 + "bo"], a["L1_ffn_gate_b"]]
    arrays = {
        "in_x": a["x"], "in_ctx": a["ctx_1024"], "in_mask": a["mask_1x1xSxS2_ik1"],
        "in_cols": np.concatenate([v.reshape(-1, P).T for v in cols], axis=1),
        "in_rows": np.concatenate(rows), "in_const": shape_constants(),
        "in_wk0": chunks(a[f0 + "Wk"]), "in_wv0": chunks(a[f0 + "Wv"]), "in_wq0": chunks(a[f0 + "Wq"]),
        "in_wo0": chunks(a[f0 + "Wo"]),
        "in_wk1": chunks(a[f1 + "Wk"].T), "in_wv1": chunks(a[f1 + "Wv"].T), "in_wq1": chunks(a[f1 + "Wq"].T),
        "in_wo1": chunks(a[f1 + "Wo"].T),
        "in_fw1": chunks(a["L0_ffn_w1_w"].T), "in_fw2": chunks(a["L0_ffn_w2_w"].T),
        "in_fh1": chunks(a["L0_ffn_h1_w"].T), "in_fh2": chunks(a["L0_ffn_h2_w"].T),
        "in_fw3": chunks(a["L0_ffn_w3_w"].T), "in_gate_w": chunks(a["L1_ffn_gate_w"]),
        "in_ew1": a["L1_ffn_w1"].reshape(E, KD, P, HID).transpose(0, 2, 1, 3),
        "in_eb1": a["L1_ffn_b1"].reshape(E, KH, P).transpose(0, 2, 1),
        "in_ew2": a["L1_ffn_w2"].reshape(E, KH, P, D).transpose(0, 2, 1, 3),
        "in_eb2": a["L1_ffn_b2"],
    }
    arrays = {k: np.ascontiguousarray(v) for k, v in arrays.items()}
    nc = bacc.Bacc("TRN2", target_bir_lowering=False, num_devices=1)
    args = [nc.dram_tensor(k, v.shape, mybir.dt.from_np(v.dtype), kind="ExternalInput").ap()
            for k, v in arrays.items()]
    scratch = [nc.dram_tensor(k, (MT * P, D), F32, kind="Internal").ap() for k in ("sorted_x", "sorted_y")]
    out = nc.dram_tensor("out_0", (B, S, D), F32, kind="ExternalOutput").ap()
    build(nc, *args, *scratch, out)
    return run_bass_kernel_spmd(nc, [arrays], core_ids=[0]).results[0]["out_0"]
```

```python
from contextlib import ExitStack

import numpy as np

import concourse.bass as bass
from concourse import mybir

F32 = mybir.dt.float32
F32R = mybir.dt.float32r
I32 = mybir.dt.int32
U32 = mybir.dt.uint32
ALU = mybir.AluOpType
ACT = mybir.ActivationFunctionType
AX = mybir.AxisListType

P = 128
B, S, D = 4, 512, 256
KEYS = 64
ROWS = B * KEYS
TT = S // P
NT = B * TT
KD = D // P
H0, DH0 = 12, 64
INNER = H0 * DH0
PAIRS = H0 // 2
HALF = INNER // 2
HP = H0 // 2
H1, DH1 = 16, 16
G1 = P // DH1
NG1 = H1 // G1
PAIRS1 = H1 // 2
HID = 1024
KH = HID // P
E = 8
TURN = 4
MT = NT + E
EPS = 1e-5

COLS, NCOLS = {}, 0
for _name, _n in (("vid_g", KD), ("vid_b", KD), ("tab_g", KD), ("tab_b", KD), ("q_g", PAIRS), ("q_b", PAIRS),
                  ("k_g", PAIRS), ("k_b", PAIRS), ("bq", KD), ("bk", KD), ("w1_s", KH), ("w2_s", KH),
                  ("h1_s", KH), ("h2_s", KH)):
    COLS[_name] = NCOLS
    NCOLS += _n
ROW_AT, NROWS = {}, 0
for _name, _n in (("bo0", D), ("s3", D), ("bv", D), ("bo1", D), ("gate_b", E)):
    ROW_AT[_name] = NROWS
    NROWS += _n
CONST_AT, NCONST = {}, 0
for _name, _n in (("ident", P), ("before", P), ("ones", P), ("kmask", G1), ("vmask", TT * P), ("down", E),
                  ("full", NT), ("tile_no", MT), ("minus_half", NT)):
    CONST_AT[_name] = NCONST
    NCONST += _n

A_TP = KD + 2 * PAIRS
A_MM = 2 * TT
C_TP = KD + PAIRS1
F_HID = 3 * KH
RING = 6


def after(eng, sem, turn, per_turn, n):
    eng.wait_ge(sem, turn * per_turn + (n + 1))


class Order:

    def __init__(self, eng, sem, turn=None, per_turn=0):
        self.eng, self.sem, self.turn, self.per_turn, self.n = eng, sem, turn, per_turn, 0

    def mark(self, ins):
        ins.then_inc(self.sem, 1)
        self.n += 1

    def join(self):
        if self.turn is None:
            self.eng.wait_ge(self.sem, self.n)
        else:
            after(self.eng, self.sem, self.turn, self.per_turn, self.n)

    def step(self, ins):
        self.mark(ins)
        self.join()

    def end(self):
        assert self.n == self.per_turn, (self.n, self.per_turn)


def build(nc, x, ctxt, mask, cols_d, rows_d, const_d, wk0_d, wv0_d, wq0_d, wo0_d, wk1_d, wv1_d, wq1_d, wo1_d,
          fw1_d, fw2_d, fh1_d, fh2_d, fw3_d, gate_w_d, ew1_d, eb1_d, ew2_d, eb2_d, sorted_x, sorted_y, ffn_copy, out):
    top = ExitStack()
    with top:
        base = -(-nc.sbuf_base // 128) * 128

        def at(name, shape, kb, dt=F32):
            return nc.alloc_sbuf_tensor_at(name, shape, dt, offset=base + int(kb * 1024))

        def sem(name):
            return top.enter_context(nc.semaphore(name))

        x_res = at("x_res", [P, NT, D], 0)
        const = at("const", [P, NCONST], 16)
        cols = at("cols", [P, NCOLS], 20)
        stats = at("stats", [P, NT, 12], 20.5)
        mean_var = at("mean_var", [P, NT, 2], 21.25)
        var_eps = at("var_eps", [P, NT], 21.375)
        rstd = at("rstd", [P, NT], 21.4375)
        scaled = at("scaled", [P, 2 * PAIRS + KD], 21.5)
        mean_all = at("mean_all", [P, NT], 21.625)
        rstd_all = at("rstd_all", [P, NT], 21.6875)
        weight_bits_f = at("weight_bits_f", [P, 2], 21.78125)
        inexact = at("inexact", [P, 2], 21.8125, I32)
        rows = at("rows", [P, NROWS], 22)
        head_max = at("head_max", [P, TT, H1], 26.25)
        head_sum = at("head_sum", [P, TT, H1], 26.5)
        k1T = at("k1T", [P, NG1, ROWS], 27)
        v1 = at("v1", [P, B, D], 29)
        wq1 = at("wq1", [P, KD, D], 33)
        wo1 = at("wo1", [P, KD, D], 35)
        gate_w = at("gate_w", [P, KD, E], 37)
        keep = at("keep", [P, TT, KEYS], 205.5)
        fill = at("fill", [P, TT, KEYS], 206.5)
        x_in = at("x_in", [P, TT, D], 199.5)
        fw1 = at("fw1", [P, KD, HID], 37.5)
        fw2 = at("fw2", [P, KD, HID], 45.5)
        fh1 = at("fh1", [P, KH, HID], 53.5)
        fw3 = at("fw3", [P, KH, D], 85.5)
        fh2 = at("fh2", [P, KH, HID], 93.5)
        v0 = at("v0", [P, B, INNER], 93.5)
        k0T = at("k0T", [P, PAIRS, ROWS], 105.5)
        wq0 = at("wq0", [P, KD, INNER], 111.5)
        wo0 = at("wo0", [P, PAIRS, D], 117.5)
        k0_blocks = at("k0_blocks", [P, PAIRS, P], 123.5)
        v0_blocks = at("v0_blocks", [P, PAIRS, P], 126.5)
        a_tok = at("a_tok", [P, TT, INNER], 129.5)
        a_feat = at("a_feat", [P, PAIRS, S], 153.5)
        a_pT = at("a_pT", [P, PAIRS, S], 165.5)
        a_xT = at("a_xT", [P, KD, S], 177.5)
        a_tmp = at("a_tmp", [P, 2, D], 181.5)
        xn = at("xn", [P, NT, D], 183.5)
        a_new = at("a_new", [P, 2, D], 149.5)
        wk0 = at("wk0", [P, KD, INNER], 129.5)
        wv0 = at("wv0", [P, KD, INNER], 135.5)
        wk1 = at("wk1", [P, KD, D], 141.5)
        wv1 = at("wv1", [P, KD, D], 143.5)
        c_raw = at("c_raw", [P, 2, D], 145.5)
        ctx_norm = at("ctx_norm", [P, 2, D], 147.5)
        kvT = at("kvT", [P, KD, ROWS], 149.5)
        kvT2 = at("kvT2", [P, KD, B, 2, KEYS], 151.5)
        cT = at("cT", [P, KD, ROWS], 155.5)
        cT2 = at("cT2", [P, KD, B, 2, KEYS], 157.5)
        k_norm = at("k_norm", [P, 2, INNER], 161.5)
        mask_i = at("mask_i", [P, TT, KEYS], 167.5, I32)
        zeros = at("zeros", [P, D], 168.5)
        f_ha = [at("f_ha_" + n, [P, KH, S], kb, F32R) for n, kb in (("hi", 125.5), ("lo", 141.5))]
        f_hb = [at("f_hb_" + n, [P, KH, S], kb, F32R) for n, kb in (("hi", 157.5), ("lo", 173.5))]
        f_xT = [at("f_xT_" + n, [P, KD, S], kb, F32R) for n, kb in (("hi", 157.5), ("lo", 161.5))]
        f_raw = at("f_raw", [P, 3, S], 189.5)
        any_bits = at("any_bits", [P, KD * HID + KH * HID // 2 + KH * D // 2], 125.5, I32)
        f_tmp = at("f_tmp", [P, 2, D], 195.5)
        f_new = at("f_new", [P, 2, D], 197.5)
        c_tok = at("c_tok", [P, TT, H1, KEYS], 127.5)
        c_pT = at("c_pT", [P, PAIRS1, S], 143.5)
        c_xT = at("c_xT", [P, KD, S], 159.5)
        c_tmp = at("c_tmp", [P, 2, D], 163.5)
        k1_blocks = at("k1_blocks", [P, NG1, G1, KEYS], 181.5)
        v1_blocks = at("v1_blocks", [P, PAIRS1, P], 185.5)
        c_qT = at("c_qT", [P, NG1, S], 189.5)
        c_oT = at("c_oT", [P, NG1, S], 193.5)
        c_new = at("c_new", [P, 2, D], 197.5)
        ew1 = at("ew1", [P, E, KD, HID], 37.5)
        ew2 = at("ew2", [P, E, KH, D], 101.5)
        xn_e = at("xn_e", [P, NT, D], 165.5)
        h_tok = at("h_tok", [P, 2, HID], 165.5)
        hT = at("hT", [P, 2, KH, P], 173.5)
        g_xT = at("g_xT", [P, 2, KD, S], 181.5)
        eb1 = at("eb1", [P, TURN, HID], 181.5)
        eb2 = at("eb2", [P, TURN, D], 27)
        xs = at("xs", [P, TURN, D], 31)
        xsT = at("xsT", [P, 2, KD, P], 35)
        ys = at("ys", [P, TURN, D], 22)
        y_back = at("y_back", [P, NT, D], 37.5)
        g_e = at("g_e", [P, NT, E], 197.5)
        g_max = at("g_max", [P, NT], 198)
        g_sum = at("g_sum", [P, NT], 198.25)
        g_inv = at("g_inv", [P, NT], 198.5)
        g_eq = at("g_eq", [P, NT, E], 199)
        g_top = at("g_top", [P, NT], 199.5)
        g_hot = at("g_hot", [P, NT, E], 200)
        weight = at("weight", [P, NT], 200.5)
        g_pre = at("g_pre", [P, NT + 1, E], 201)
        g_tot = at("g_tot", [P, NT, E], 202)
        g_cmp = at("g_cmp", [P, E, NT], 202.5)
        g_tiles = at("g_tiles", [P, E], 203)
        g_start = at("g_start", [P, E + 1], 203.25)
        g_slot = at("g_slot", [P, NT, E], 203.5)
        g_slotf = at("g_slotf", [P, NT], 204)
        slot = at("slot", [P, NT], 204.25, U32)
        g_cmp2 = at("g_cmp2", [P, MT, E], 204.5)
        g_eid = at("g_eid", [P, MT], 205.5)
        g_base = at("g_base", [P, E], 205.75)
        expert = at("expert", [P, MT], 206, I32)

        ps = top.enter_context(nc.psum_tensor("ps", [P, 8, 512], F32))

        def con(name, n):
            return const[:, CONST_AT[name]:CONST_AT[name] + n]

        def col(name, i=0):
            return cols[:, COLS[name] + i:COLS[name] + i + 1]

        def row(name, n=D):
            return rows[:, ROW_AT[name]:ROW_AT[name] + n]

        ident = con("ident", P)
        x_tiles = x.rearrange("b (j p) d -> p (b j) d", p=P)
        out_tiles = out.rearrange("b (j p) d -> p (b j) d", p=P)

        ld_small, ld_kv, ld_x, ld_attn, ld_ffn, ld_h2 = (sem(n) for n in (
            "ld_small", "ld_kv", "ld_x", "ld_attn", "ld_ffn", "ld_h2"))
        zero_filled, ffn_copied = sem("zero_filled"), sem("ffn_copied")

        loop_sems = []

        def loop_sem(name):
            loop_sems.append(sem(name))
            return loop_sems[-1]

        a_tp_full, a_tp_out, a_mm_full, a_mm_taken, a_pv_full, a_pv_out, a_wo_full, a_wo_taken, a_exp, a_prob, \
            a_blocks, a_var, a_rstd, a_norm, a_dve = (loop_sem("a_" + n) for n in (
                "tp_full", "tp_out", "mm_full", "mm_taken", "pv_full", "pv_out", "wo_full", "wo_taken", "exp",
                "prob", "blocks", "var", "rstd", "norm", "dve"))
        a_in, f_in, c_in, a_kept, f_kept, c_kept = (loop_sem(n + m) for m in ("_in", "_kept") for n in "afc")
        f_tp_full, f_x_hi, f_x_lo, f_mm_full, f_act_out, f_up_taken, f_split, f_y_taken, f_var, f_norm, f_dve = (
            loop_sem("f_" + n) for n in ("tp_full", "x_hi", "x_lo", "mm_full", "act_out", "up_taken", "split",
                                         "y_taken", "var", "norm", "dve"))
        f_bits_sum, f_bits_or, f_checked, f_check_own = (sem("f_" + n) for n in ("bits_sum", "bits_or", "checked",
                                                                                 "check_own"))
        c_tp_full, c_tp_out, c_q_full, c_q_out, c_s_full, c_s_taken, c_pv_full, c_pv_out, c_wo_full, c_wo_taken, \
            c_sub, c_exp, c_prob, c_blocks, c_var, c_norm, c_rows, c_dve = (loop_sem("c_" + n) for n in (
                "tp_full", "tp_out", "q_full", "q_out", "s_full", "s_taken", "pv_full", "pv_out", "wo_full",
                "wo_taken", "sub", "exp", "prob", "blocks", "var", "norm", "rows", "dve"))
        e_tp_full, e_xT, e_up_full, e_pre, e_h, e_ht_full, e_hT, e_down_full, e_y_out, e_y_free = (
            loop_sem("e_" + n) for n in ("tp_full", "xT", "up_full", "pre", "h", "ht_full", "hT", "down_full",
                                         "y_out", "y_free"))
        e_stored, ld_ew = sem("e_stored"), sem("ld_ew")
        e_loaded = [sem(f"e_loaded{u}") for u in range(TURN)]

        def moments(order, i, chunks):
            nc.vector.nop(nofuse=True)
            for c, chunk in enumerate(chunks):
                order.mark(nc.vector.bn_stats(stats[:, i, 6 * c:6 * c + 6], chunk))
            order.join()
            nc.vector.nop(nofuse=True)
            order.step(nc.vector.bn_aggr(mean_var[:, i, :], stats[:, i, 0:6 * len(chunks)]))

        def add_eps(i, n=1):
            return nc.vector.tensor_scalar_add(var_eps[:, i:i + n], mean_var[:, i:i + n, 1], EPS)

        def rstd_pow(i, n=1):
            return nc.gpsimd.tensor_tensor(rstd[:, i:i + n], var_eps[:, i:i + n], con("minus_half", n), ALU.pow)

        def center_scale(dst, src, i):
            return nc.vector.tensor_scalar(dst, src, mean_var[:, i, 0:1], rstd[:, i:i + 1], ALU.subtract, ALU.mult)

        p_var, p_rstd, p_cnorm, p_knorm, p_pe, p_act, p_v1, p_dve, p_zero = (sem("p_" + n) for n in (
            "var", "rstd", "cnorm", "knorm", "pe", "act", "v1", "dve", "zero"))
        with nc.Block() as block:

            @block.sync
            def _(sp):
                sp.dma_start(c_raw[:], ctxt.rearrange("(r b) k d -> (b k) r d", r=2)).then_inc(ld_small, 16)
                sp.dma_start(const[:], const_d).then_inc(ld_small, 16)
                sp.dma_start(cols[:], cols_d).then_inc(ld_small, 16)
                sp.dma_start(rows[:], rows_d.partition_broadcast(P)).then_inc(ld_small, 16)
                for dst, src in ((wv0, wv0_d), (wk0, wk0_d), (wk1, wk1_d), (wv1, wv1_d)):
                    sp.dma_start(dst[:], src).then_inc(ld_kv, 16)
                sp.dma_start(mask_i[:], mask.rearrange("a b (j p) k -> p (a b j) k", p=P)).then_inc(ld_kv, 16)
                sp.dma_start(x_res[:], x_tiles).then_inc(ld_x, 16)
                for dst, src in ((wq0, wq0_d), (wo0, wo0_d), (wq1, wq1_d), (wo1, wo1_d), (gate_w, gate_w_d)):
                    sp.dma_start(dst[:], src).then_inc(ld_attn, 16)
                for dst, src in zip(ffn_copy, (fw1_d, fw2_d, fh1_d, fw3_d, fh2_d)):
                    sp.dma_start(dst, src).then_inc(ffn_copied, 16)
                sp.wait_ge(ffn_copied, 16 * 5)
                for dst, src in zip((fw1, fw2, fh1, fw3), ffn_copy):
                    sp.dma_start(dst[:], src).then_inc(ld_ffn, 16)
                sp.wait_ge(p_zero, 3)
                sp.dma_start(sorted_x.rearrange("(t p) d -> p t d", p=P),
                             zeros[:].unsqueeze(1).broadcast_to([P, MT, D])).then_inc(zero_filled, 16)
                sp.wait_ge(zero_filled, 16)

            @block.gpsimd
            def _(pool):
                for s in loop_sems:
                    pool.sem_inc(s, 1)
                for s in (e_y_out, e_y_free):
                    pool.sem_inc(s, TURN - 1)
                pool.memset(zeros[:], 0.0).then_inc(p_zero, 1)
                pool.memset(k0_blocks[:], 0.0).then_inc(p_zero, 1)
                pool.memset(v0_blocks[:], 0.0).then_inc(p_zero, 1)
                pool.wait_ge(ld_small, 64)
                for n, (i, m) in enumerate(((0, 2), (2, 1), (3, 1), (0, NT), (0, NT))):
                    pool.wait_ge(p_var, n + 1)
                    rstd_pow(i, m).then_inc(p_rstd, 1)

            @block.vector
            def _(dve):
                order = Order(dve, p_dve)
                dve.wait_ge(ld_small, 64)
                for i in range(2):
                    moments(order, i, [c_raw[:, i, :]])
                add_eps(0, 2).then_inc(p_var, 1)
                nc.vector.tensor_scalar_mul(scaled[:, 0:2 * PAIRS], cols[:, COLS["q_g"]:COLS["q_g"] + 2 * PAIRS],
                                            DH0 ** -0.5)
                nc.vector.tensor_scalar_mul(scaled[:, 2 * PAIRS:], cols[:, COLS["bq"]:COLS["bq"] + KD], DH1 ** -0.5)
                dve.wait_ge(p_rstd, 1)
                for i in range(2):
                    center_scale(ctx_norm[:, i, :], c_raw[:, i, :], i).then_inc(p_cnorm, 1)
                dve.wait_ge(ld_kv, 80)
                order.step(nc.vector.tensor_copy(keep[:], mask_i[:]))
                order.step(nc.vector.tensor_scalar(keep[:], keep[:], 0.0, None, ALU.not_equal))
                order.step(nc.vector.tensor_scalar(fill[:], keep[:], -1.0, 1e9, ALU.add, ALU.mult))
                for r in range(2):
                    dve.wait_ge(p_pe, 9 + r)
                    banks = [ps[:, 2 * r + h, 0:HALF] for h in range(2)]
                    moments(order, 2 + r, banks)
                    add_eps(2 + r).then_inc(p_var, 1)
                    dve.wait_ge(p_rstd, 2 + r)
                    center_scale(k_norm[:, r, :].rearrange("p (h n) -> p h n", h=2),
                                 ps[:, 2 * r:2 * r + 2, 0:HALF], 2 + r).then_inc(p_knorm, 1)
                for b in range(B):
                    dve.wait_ge(p_pe, 13 + b)
                    nc.vector.tensor_tensor(v1[:, b, :], ps[:, 5 + 2 * (b % 2), 0:D], row("bv"), ALU.add)\
                        .then_inc(p_v1, 1)
                dve.wait_ge(ld_x, 16)
                for n, src in ((0, x_res), (1, xn)):
                    for t in range(NT):
                        order.mark(nc.vector.bn_stats(stats[:, t, 0:6], src[:, t, :]))
                    order.join()
                    for t in range(NT):
                        order.mark(nc.vector.bn_aggr(mean_var[:, t, :], stats[:, t, 0:6]))
                    order.join()
                    add_eps(0, NT).then_inc(p_var, 1)
                    dve.wait_ge(p_rstd, 4 + n)
                    for t in range(NT):
                        order.mark(center_scale(xn[:, t, :], src[:, t, :], t))
                    order.join()

            @block.tensor
            def _(pe):
                pe.wait_ge(ld_small, 64)
                pe.wait_ge(p_cnorm, 2)
                for bank, src in ((0, ctx_norm), (2, c_raw)):
                    for k in range(KD):
                        for r in range(2):
                            ins = nc.tensor.transpose(ps[:, bank + k, r * P:(r + 1) * P],
                                                      src[:, r, k * P:(k + 1) * P], ident)
                        ins.then_inc(p_pe, 1)
                pe.wait_ge(ld_kv, 80)
                for b in range(B):
                    pe.wait_ge(p_act, 4 if b < 2 else 7 + b)
                    for h in range(2):
                        for k in range(KD):
                            ins = nc.tensor.matmul(ps[:, 4 + 2 * (b % 2) + h, 0:HALF],
                                                   kvT2[:, k, b].rearrange("p a s -> p (a s)"),
                                                   wv0[:, k, h * HALF:(h + 1) * HALF],
                                                   start=(k == 0), stop=(k == KD - 1))
                    ins.then_inc(p_pe, 1)
                pe.wait_ge(p_act, 8)
                for r in range(2):
                    for h in range(2):
                        for k in range(KD):
                            ins = nc.tensor.matmul(ps[:, 2 * r + h, 0:HALF], kvT[:, k, r * P:(r + 1) * P],
                                                   wk0[:, k, h * HALF:(h + 1) * HALF],
                                                   start=(k == 0), stop=(k == KD - 1))
                    ins.then_inc(p_pe, 1)
                for o in range(NG1):
                    pe.wait_ge(p_act, 11 + o)
                    for k in range(KD):
                        ins = nc.tensor.matmul(ps[:, 4 + 2 * o, 0:ROWS], wk1[:, k, o * P:(o + 1) * P], cT[:, k, :],
                                               start=(k == 0), stop=(k == KD - 1))
                    ins.then_inc(p_pe, 1)
                for b in range(B):
                    if b >= 2:
                        pe.wait_ge(p_v1, b - 1)
                    for k in range(KD):
                        ins = nc.tensor.matmul(ps[:, 5 + 2 * (b % 2), 0:D],
                                               cT2[:, k, b].rearrange("p a s -> p (a s)"), wv1[:, k, :],
                                               start=(k == 0), stop=(k == KD - 1))
                    ins.then_inc(p_pe, 1)
                pe.wait_ge(p_knorm, 2)
                for g in range(PAIRS):
                    pe.wait_ge(p_act, 13 + g)
                    for r in range(2):
                        ins = nc.tensor.transpose(ps[:, 4 + 2 * (g % 2), r * P:(r + 1) * P],
                                                  k_norm[:, r, g * P:(g + 1) * P], ident)
                    ins.then_inc(p_pe, 1)

            @block.scalar
            def _(act):
                for n, (bank, one, two) in enumerate(((0, kvT, kvT2), (2, cT, cT2))):
                    for k in range(KD):
                        act.wait_ge(p_pe, 2 * n + k + 1)
                        src = ps[:, bank + k, 0:ROWS]
                        how = dict(scale=col("tab_g", k), bias=col("tab_b", k)) if n == 0 else {}
                        nc.scalar.activation(one[:, k, :], src, ACT.Identity, **how).then_inc(p_act, 1)
                        twice = src.rearrange("p (b s) -> p b s", b=B)
                        for half in range(2):
                            ins = nc.scalar.activation(two[:, k, :, half, :], twice, ACT.Identity, **how)
                        ins.then_inc(p_act, 1)
                for b in range(B):
                    act.wait_ge(p_pe, 5 + b)
                    nc.scalar.activation(v0[:, b, :].rearrange("p (h n) -> p h n", h=2),
                                         ps[:, 4 + 2 * (b % 2):6 + 2 * (b % 2), 0:HALF], ACT.Identity)\
                        .then_inc(p_act, 1)
                for o in range(NG1):
                    act.wait_ge(p_pe, 11 + o)
                    nc.scalar.activation(k1T[:, o, :], ps[:, 4 + 2 * o, 0:ROWS], ACT.Identity, bias=col("bk", o))\
                        .then_inc(p_act, 1)
                for g in range(PAIRS):
                    act.wait_ge(p_pe, 17 + g)
                    nc.scalar.activation(k0T[:, g, :], ps[:, 4 + 2 * (g % 2), 0:ROWS], ACT.Identity,
                                         scale=col("k_g", g), bias=col("k_b", g)).then_inc(p_act, 1)

        def add_residual(dve, order, turn, full, taken, var, kept, banks, tmp, new, scale=None, bias=None):
            for j in range(TT):
                after(dve, full[0], turn, full[1], full[2] + j + 1)
                by, op = (bias, ALU.add) if scale is None else (scale, ALU.mult)
                nc.vector.tensor_tensor(tmp[:, j % 2, :], ps[:, banks[j], 0:D], by, op).then_inc(taken[0], 1)
                after(dve, taken[0], turn, taken[1], taken[2] + j + 1)
                after(dve, kept, turn, TT, max(j - 1, 0))
                order.step(nc.vector.tensor_tensor(
                    new[:, j % 2, :], x_res[:, bass.ts(turn * TT + j, 1), :].rearrange("p a d -> p (a d)"),
                    tmp[:, j % 2, :], ALU.add))
                moments(order, j, [new[:, j % 2, :]])
                add_eps(j).then_inc(var, 1)

        def keep_rows(pool, turn, var, per_turn, first, kept, new, norm):
            for j in range(TT):
                after(pool, var, turn, per_turn, first + j + 1)
                pool.tensor_copy(x_res[:, bass.ts(turn * TT + j, 1), :], new[:, j % 2:j % 2 + 1, :])\
                    .then_inc(kept, 1)
            pool.nop(nofuse=True)
            nc.gpsimd.tensor_tensor(rstd_all[:, bass.ts(turn, TT)], var_eps[:, 0:TT], con("minus_half", TT),
                                    ALU.pow).then_inc(norm, 1)
            pool.tensor_copy(mean_all[:, bass.ts(turn, TT)], mean_var[:, 0:TT, 0]).then_inc(norm, 1)

        def normalise(pool, dst, batch, done, done_turn, per_turn, first):
            def wide(ap):
                return ap.unsqueeze(2).broadcast_to([P, TT, D])

            pool.nop(nofuse=True)
            pool.tensor_tensor(dst, x_res[:, bass.ts(batch, TT), :], wide(mean_all[:, bass.ts(batch, TT)]),
                               ALU.subtract).then_inc(done, 1)
            after(pool, done, done_turn, per_turn, first + 1)
            pool.nop(nofuse=True)
            pool.tensor_tensor(dst, dst, wide(rstd_all[:, bass.ts(batch, TT)]), ALU.mult).then_inc(done, 1)

        A_DVE = TT * 3 + TT * 4 + TT * 3
        with nc.Block() as block:

            @block.gpsimd
            def _(pool):
                with pool.Fori(0, B) as i:
                    after(pool, a_tp_full, i, A_TP, 0)
                    pool.tensor_copy(x_in[:], xn[:, bass.ts(i, TT), :]).then_inc(a_in, 1)
                    after(pool, a_pv_full, i, PAIRS, 0)
                    after(pool, a_in, i, 1, 1)
                    for h in range(2):
                        half = slice(h * DH0, (h + 1) * DH0)
                        if h:
                            after(pool, a_blocks, i, 4, 2)
                        pool.tensor_copy(k0_blocks[half, :, half], k0T[half, :, bass.ts(i, KEYS)])\
                            .then_inc(a_blocks, 1)
                        after(pool, a_blocks, i, 4, 2 * h + 1)
                        pool.tensor_copy(v0_blocks[half, :, half],
                                         v0[half, bass.ts(i, 1), :].rearrange("p a (g c) -> p (a g) c", g=PAIRS)[
                                             :, :, half]).then_inc(a_blocks, 1)
                    after(pool, a_blocks, i, 4, 4)
                    for j in range(TT):
                        after(pool, a_var, i, 2 * TT, j + 1)
                        rstd_pow(TT + j).then_inc(a_rstd, 1)
                    keep_rows(pool, i, a_var, 2 * TT, TT, a_kept, a_new, a_norm)
                pool.wait_ge(a_norm, 2 * B + 1)
                normalise(pool, x_in[:], 0, f_in, 0, 2, 0)

            @block.tensor
            def _(pe):
                pe.wait_ge(ld_attn, 80)
                with pe.Fori(0, B) as i:
                    after(pe, a_in, i, 1, 1)
                    after(pe, a_tp_out, i, A_TP, 0)
                    for k in range(KD):
                        for j in range(TT):
                            ins = nc.tensor.transpose(ps[:, k, j * P:(j + 1) * P], x_in[:, j, k * P:(k + 1) * P],
                                                      ident)
                        ins.then_inc(a_tp_full, 1)
                    after(pe, a_tp_out, i, A_TP, KD)
                    after(pe, a_mm_taken, i, A_MM, 0)
                    for j in range(TT):
                        if j >= 2:
                            after(pe, a_mm_taken, i, A_MM, j - 1)
                        for h in range(2):
                            for k in range(KD):
                                ins = nc.tensor.matmul(ps[:, 2 + 2 * (j % 2) + h, 0:HALF],
                                                       a_xT[:, k, j * P:(j + 1) * P],
                                                       wq0[:, k, h * HALF:(h + 1) * HALF],
                                                       start=(k == 0), stop=(k == KD - 1))
                        ins.then_inc(a_mm_full, 1)
                    after(pe, a_mm_taken, i, A_MM, TT)
                    for g in range(PAIRS):
                        after(pe, a_tp_out, i, A_TP, KD + g - 1)
                        for j in range(TT):
                            ins = nc.tensor.transpose(ps[:, g % 2, j * P:(j + 1) * P],
                                                      a_tok[:, j, g * P:(g + 1) * P], ident)
                        ins.then_inc(a_tp_full, 1)
                    after(pe, a_tp_out, i, A_TP, KD + PAIRS)
                    after(pe, a_blocks, i, 4, 4)
                    for j in range(TT):
                        after(pe, a_mm_taken, i, A_MM, TT + j - 1)
                        for g in range(PAIRS):
                            ins = nc.tensor.matmul(
                                ps[:, 2 + 2 * (j % 2) + g // 3, (g % 3) * P:(g % 3 + 1) * P],
                                a_feat[:, g, j * P:(j + 1) * P], k0_blocks[:, g, :], start=True, stop=True)
                        ins.then_inc(a_mm_full, 1)
                    after(pe, a_prob, i, TT, TT)
                    for g in range(PAIRS):
                        after(pe, a_tp_out, i, A_TP, KD + PAIRS + g - 1)
                        for j in range(TT):
                            ins = nc.tensor.transpose(ps[:, g % 2, j * P:(j + 1) * P],
                                                      a_tok[:, j, g * P:(g + 1) * P], ident)
                        ins.then_inc(a_tp_full, 1)
                    after(pe, a_wo_taken, i, TT, 0)
                    for g in range(PAIRS):
                        after(pe, a_tp_out, i, A_TP, KD + PAIRS + g + 1)
                        after(pe, a_pv_out, i, PAIRS, max(g - 1, 0))
                        nc.tensor.matmul(ps[:, 6 + g % 2, :], v0_blocks[:, g, :], a_pT[:, g, :],
                                         start=True, stop=True).then_inc(a_pv_full, 1)
                    after(pe, a_pv_out, i, PAIRS, PAIRS)
                    for j in range(TT):
                        after(pe, a_wo_taken, i, TT, max(j - 1, 0))
                        for g in range(PAIRS):
                            ins = nc.tensor.matmul(ps[:, 7 - j % 2, 0:D], a_feat[:, g, j * P:(j + 1) * P],
                                                   wo0[:, g, :], start=(g == 0), stop=(g == PAIRS - 1))
                        ins.then_inc(a_wo_full, 1)

            @block.scalar
            def _(act):
                with act.Fori(0, B) as i:
                    for k in range(KD):
                        after(act, a_tp_full, i, A_TP, k + 1)
                        nc.scalar.activation(a_xT[:, k, :], ps[:, k, :], ACT.Identity, scale=col("vid_g", k),
                                             bias=col("vid_b", k)).then_inc(a_tp_out, 1)
                    for g in range(PAIRS):
                        after(act, a_tp_full, i, A_TP, KD + g + 1)
                        nc.scalar.activation(a_feat[:, g, :], ps[:, g % 2, :], ACT.Identity,
                                             scale=scaled[:, g:g + 1], bias=scaled[:, PAIRS + g:PAIRS + g + 1])\
                            .then_inc(a_tp_out, 1)
                    for j in range(TT):
                        after(act, a_mm_taken, i, A_MM, TT + j + 1)
                        nc.scalar.activation(a_tok[:, j, :], a_tok[:, j, :], ACT.Exp).then_inc(a_exp, 1)
                    for g in range(PAIRS):
                        after(act, a_tp_full, i, A_TP, KD + PAIRS + g + 1)
                        nc.scalar.activation(a_pT[:, g, :], ps[:, g % 2, :], ACT.Identity).then_inc(a_tp_out, 1)
                    for g in range(PAIRS):
                        after(act, a_pv_full, i, PAIRS, g + 1)
                        nc.scalar.activation(a_feat[:, g, :], ps[:, 6 + g % 2, :], ACT.Identity)\
                            .then_inc(a_pv_out, 1)

            @block.vector
            def _(dve):
                with dve.Fori(0, B) as i:
                    order = Order(dve, a_dve, i, A_DVE)

                    def q_moments(j):
                        after(dve, a_mm_full, i, A_MM, j + 1)
                        moments(order, TT + j, [ps[:, 2 + 2 * (j % 2) + h, 0:HALF] for h in range(2)])
                        add_eps(TT + j).then_inc(a_var, 1)

                    def q_norm(j):
                        after(dve, a_rstd, i, TT, j + 1)
                        center_scale(a_tok[:, j, :].rearrange("p (h n) -> p h n", h=2),
                                     ps[:, 2 + 2 * (j % 2):4 + 2 * (j % 2), 0:HALF], TT + j)\
                            .then_inc(a_mm_taken, 1)

                    q_moments(0)
                    for j in range(TT):
                        if j + 1 < TT:
                            q_moments(j + 1)
                        q_norm(j)

                    def subtract_max(j):
                        after(dve, a_mm_full, i, A_MM, TT + j + 1)
                        top_ = head_max[:, j, 0:H0]
                        banks = ps[:, 2 + 2 * (j % 2):4 + 2 * (j % 2), 0:HALF].rearrange(
                            "p h (n k) -> p h n k", k=KEYS)
                        order.step(nc.vector.tensor_reduce(top_.rearrange("p (h n) -> p h n", h=2), banks, AX.X,
                                                           ALU.max))
                        for h in range(2):
                            ins = nc.vector.tensor_tensor(
                                a_tok[:, j, h * HALF:(h + 1) * HALF].rearrange("p (n k) -> p n k", k=KEYS),
                                banks[:, h], top_[:, h * HP:(h + 1) * HP].unsqueeze(2).broadcast_to([P, HP, KEYS]),
                                ALU.subtract)
                            if h == 0:
                                order.mark(ins)
                        ins.then_inc(a_mm_taken, 1)

                    def divide(j):
                        after(dve, a_exp, i, TT, j + 1)
                        sums = head_sum[:, j, 0:H0]
                        heads = a_tok[:, j, :].rearrange("p (n k) -> p n k", k=KEYS)
                        order.step(nc.vector.tensor_reduce(sums, heads, AX.X, ALU.add))
                        order.step(nc.vector.reciprocal(sums, sums))
                        nc.vector.tensor_tensor(heads, heads, sums.unsqueeze(2).broadcast_to([P, H0, KEYS]), ALU.mult)\
                            .then_inc(a_prob, 1)

                    subtract_max(0)
                    for j in range(TT):
                        if j + 1 < TT:
                            subtract_max(j + 1)
                        divide(j)
                    add_residual(dve, order, i, (a_wo_full, TT, 0), (a_wo_taken, TT, 0), a_var, a_kept,
                                 [7, 6, 7, 6], a_tmp, a_new, bias=row("bo0"))
                    order.end()

        def ring_bank(n):
            return 2 + n % RING

        def ring_free(pe, turn, n):
            n -= RING
            if n < 0:
                after(pe, f_y_taken, turn, TT, 0)
            elif n < 2 * KH:
                after(pe, *((f_up_taken, turn, KH) if n % 2 else (f_act_out, turn, F_HID)), n // 2 + 1)
            elif n < 4 * KH:
                after(pe, f_act_out, turn, F_HID, KH + n - 2 * KH + 1)
            else:
                after(pe, f_y_taken, turn, TT, n - 4 * KH + 1)

        F_MM = 4 * KH + TT
        with nc.Block() as block:

            @block.sync
            def _(sp):
                sp.dma_start(fh2[:], ffn_copy[4]).then_inc(ld_h2, 16)

            @block.gpsimd
            def _(pool):
                with pool.Fori(0, B) as i:
                    keep_rows(pool, i, f_var, TT, 0, f_kept, f_new, f_norm)
                    after(pool, f_norm, i, 2, 2)
                    normalise(pool, x_in[:], (i + 1) % B, f_in, i + 1, 2, 0)

            @block.tensor
            def _(pe):
                def product(exact, out, w, x, w_at, x_at, signal, swap=False, ready=None):
                    n = w.shape[1]

                    def passes(one_pass):
                        for k in range(n):
                            if ready is not None:
                                ready(k)
                            for part in range(2):
                                wk = w[:, k, w_at].bitcast(F32R) if one_pass else w[:, k, w_at]
                                xk = x[part][:, k, x_at]
                                xk = xk if one_pass else xk.bitcast(F32)
                                ins = nc.tensor.matmul(out, *((xk, wk) if swap else (wk, xk)),
                                                       start=(k == 0 and part == 0),
                                                       stop=(k == n - 1 and part == 1))
                        ins.then_inc(signal, 1)

                    with pe.If(exact == 0):
                        passes(True)
                    with pe.Else():
                        passes(False)

                pe.wait_ge(f_bits_or, 1)
                nc.tensor.matmul(ps[:, 2, 0:1], con("ones", P), weight_bits_f[:, 0:1], start=True, stop=True)\
                    .then_inc(f_bits_sum, 1)
                pe.wait_ge(f_bits_or, 2)
                nc.tensor.matmul(ps[:, 3, 0:1], con("ones", P), weight_bits_f[:, 1:2], start=True, stop=True)\
                    .then_inc(f_bits_sum, 1)
                pe.wait_ge(f_checked, 2)
                with pe.Fori(0, B) as i:
                    first = pe.value_load(inexact[0:1, 0:1])
                    second = pe.value_load(inexact[0:1, 1:2])
                    after(pe, f_in, i, 2, 2)
                    after(pe, f_x_lo, i, KD, 0)
                    for k in range(KD):
                        for j in range(TT):
                            ins = nc.tensor.transpose(ps[:, k, j * P:(j + 1) * P], x_in[:, j, k * P:(k + 1) * P],
                                                      ident)
                        ins.then_inc(f_tp_full, 1)
                    after(pe, f_x_lo, i, KD, KD)
                    for o in range(KH):
                        for n, w in ((2 * o, fw1), (2 * o + 1, fw2)):
                            ring_free(pe, i, n)
                            product(first, ps[:, ring_bank(n), :], w, f_xT, slice(o * P, (o + 1) * P),
                                    slice(0, S), f_mm_full)
                    for at_, flag, w, src in ((2 * KH, first, fh1, f_ha), (3 * KH, second, fh2, f_hb)):
                        for o in range(KH):
                            ring_free(pe, i, at_ + o)
                            ready = (lambda k: after(pe, f_split, i, F_HID, at_ - 2 * KH + k + 1)) if o == 0 else None
                            product(flag, ps[:, ring_bank(at_ + o), :], w, src, slice(o * P, (o + 1) * P),
                                    slice(0, S), f_mm_full, ready=ready)
                    for j in range(TT):
                        ring_free(pe, i, 4 * KH + j)
                        ready = (lambda k: after(pe, f_split, i, F_HID, 2 * KH + k + 1)) if j == 0 else None
                        product(first, ps[:, ring_bank(4 * KH + j), 0:D], fw3, f_ha, slice(0, D),
                                slice(j * P, (j + 1) * P), f_mm_full, swap=True, ready=ready)

            @block.scalar
            def _(act):
                with act.Fori(0, B) as i:
                    for k in range(KD):
                        after(act, f_tp_full, i, KD, k + 1)
                        nc.scalar.activation(f_xT[0][:, k, :], ps[:, k, :], ACT.Identity).then_inc(f_x_hi, 1)
                    for m in range(F_HID):
                        o = m % KH
                        n = 2 * o if m < KH else m + KH
                        after(act, f_mm_full, i, F_MM, n + 1)
                        after(act, f_split, i, F_HID, max(m - 2, 0))
                        nc.scalar.activation(f_raw[:, m % 3, :], ps[:, ring_bank(n), :],
                                             ACT.Silu if m < KH else ACT.Gelu,
                                             scale=col(("w1_s", "h1_s", "h2_s")[m // KH], o)).then_inc(f_act_out, 1)

            @block.vector
            def _(dve):
                order = Order(dve, f_check_own)
                for c, weights in enumerate(((fw1, fw2, fh1, fw3), (fh2,))):
                    dve.wait_ge(ld_h2 if c else ld_ffn, 16 if c else 64)
                    used = 0
                    for w in weights:
                        bits = w[:].bitcast(I32).rearrange("p k n -> p (k n)")
                        n = bits.shape[1] // 2
                        order.mark(nc.vector.tensor_tensor(any_bits[:, used:used + n], bits[:, 0:n], bits[:, n:2 * n],
                                                           ALU.bitwise_or))
                        used += n
                    order.join()
                    while used > S:
                        n = used // 2
                        order.step(nc.vector.tensor_tensor(any_bits[:, 0:n], any_bits[:, 0:n], any_bits[:, n:2 * n],
                                                           ALU.bitwise_or))
                        used = n
                    order.step(nc.vector.tensor_scalar(any_bits[:, 0:used], any_bits[:, 0:used], 0xFFF, None,
                                                       ALU.bitwise_and))
                    nc.vector.tensor_reduce(weight_bits_f[:, c:c + 1], any_bits[:, 0:used], AX.X, ALU.max)\
                        .then_inc(f_bits_or, 1)
                    dve.wait_ge(f_bits_sum, c + 1)
                    nc.vector.tensor_copy(inexact[:, c:c + 1], ps[:, 2 + c, 0:1]).then_inc(f_checked, 1)
                with dve.Fori(0, B) as i:
                    order = Order(dve, f_dve, i, F_HID + 3 * TT)
                    for k in range(KD):
                        after(dve, f_x_hi, i, KD, k + 1)
                        nc.vector.tensor_tensor(f_xT[1][:, k, :], ps[:, k, :], f_xT[0][:, k, :].bitcast(F32),
                                                ALU.subtract).then_inc(f_x_lo, 1)
                    for m in range(F_HID):
                        o = m % KH
                        raw = f_raw[:, m % 3, :]
                        if m < KH:
                            after(dve, f_mm_full, i, F_MM, 2 * o + 2)
                            after(dve, f_act_out, i, F_HID, m + 1)
                            nc.vector.scalar_tensor_tensor(raw, ps[:, ring_bank(2 * o + 1), :], col("w2_s", o), raw,
                                                           ALU.mult, ALU.mult).then_inc(f_up_taken, 1)
                            after(dve, f_up_taken, i, KH, o + 1)
                        else:
                            after(dve, f_act_out, i, F_HID, m + 1)
                        hi, lo = (part[:, o, :] for part in (f_hb if m // KH == 1 else f_ha))
                        order.step(nc.vector.tensor_copy(hi, raw))
                        nc.vector.tensor_tensor(lo, raw, hi.bitcast(F32), ALU.subtract).then_inc(f_split, 1)
                    add_residual(dve, order, i, (f_mm_full, F_MM, 4 * KH), (f_y_taken, TT, 0), f_var, f_kept,
                                 [ring_bank(4 * KH + j) for j in range(TT)], f_tmp, f_new, scale=row("s3"))
                    order.end()

        EARLY = 3
        with nc.Block() as block:

            @block.sync
            def _(sp):
                sp.dma_start(ew1[:], ew1_d.rearrange("e p k n -> p e k n")).then_inc(ld_ew, 16)
                sp.dma_start(ew2[:, 0:EARLY], ew2_d[0:EARLY].rearrange("e p k n -> p e k n")).then_inc(ld_ew, 16)

            @block.gpsimd
            def _(pool):
                pool.sem_inc(c_in, 2)
                with pool.Fori(0, B) as i:
                    after(pool, c_pv_full, i, NG1, 0)
                    pool.nop(nofuse=True)
                    for o in range(NG1):
                        pool.tensor_tensor(k1_blocks[:, o],
                                           k1T[:, o, bass.ts(i, KEYS)].unsqueeze(1).broadcast_to([P, G1, KEYS]),
                                           con("kmask", G1).unsqueeze(2).broadcast_to([P, G1, KEYS]), ALU.mult)\
                            .then_inc(c_blocks, 1)
                        pool.tensor_tensor(v1_blocks[:, o * TT:(o + 1) * TT, :],
                                           v1[:, bass.ts(i, 1), o * P:(o + 1) * P].broadcast_to([P, TT, P]),
                                           con("vmask", TT * P).rearrange("p (a c) -> p a c", c=P), ALU.mult)\
                            .then_inc(c_blocks, 1)
                    keep_rows(pool, i, c_var, TT, 0, c_kept, c_new, c_norm)
                    after(pool, c_norm, i, 2, 2)
                    normalise(pool, x_in[:], (i + 1) % B, c_in, i + 1, 2, 0)
                    normalise(pool, xn_e[:, bass.ts(i, TT), :], i, c_rows, i, 2, 0)

            @block.tensor
            def _(pe):
                with pe.Fori(0, B) as i:
                    after(pe, c_in, i, 2, 2)
                    after(pe, c_tp_out, i, C_TP, 0)
                    for k in range(KD):
                        for j in range(TT):
                            ins = nc.tensor.transpose(ps[:, k, j * P:(j + 1) * P], x_in[:, j, k * P:(k + 1) * P],
                                                      ident)
                        ins.then_inc(c_tp_full, 1)
                    after(pe, c_tp_out, i, C_TP, KD)
                    after(pe, c_wo_taken, i, TT, 0)
                    for o in range(NG1):
                        for k in range(KD):
                            ins = nc.tensor.matmul(ps[:, 6 + o, :], wq1[:, k, o * P:(o + 1) * P], c_xT[:, k, :],
                                                   start=(k == 0), stop=(k == KD - 1))
                        ins.then_inc(c_q_full, 1)
                    after(pe, c_q_out, i, NG1, NG1)
                    after(pe, c_blocks, i, 2 * NG1, 2 * NG1)
                    for j in range(TT):
                        after(pe, c_s_taken, i, TT, max(j - 1, 0))
                        for o in range(NG1):
                            ins = nc.tensor.matmul(ps[:, 2 + 2 * (j % 2) + o, :], c_qT[:, o, j * P:(j + 1) * P],
                                                   k1_blocks[:, o].rearrange("p g k -> p (g k)"),
                                                   start=True, stop=True)
                        ins.then_inc(c_s_full, 1)
                    after(pe, c_prob, i, TT, TT)
                    for g in range(PAIRS1):
                        after(pe, c_tp_out, i, C_TP, KD + g - 1)
                        for j in range(TT):
                            ins = nc.tensor.transpose(ps[:, g % 2, j * P:(j + 1) * P],
                                                      c_tok[:, j, 2 * g:2 * g + 2, :].rearrange("p a k -> p (a k)"),
                                                      ident)
                        ins.then_inc(c_tp_full, 1)
                    for o in range(NG1):
                        for q in range(TT):
                            g = o * TT + q
                            after(pe, c_tp_out, i, C_TP, KD + g + 1)
                            ins = nc.tensor.matmul(ps[:, 6 + o, :], v1_blocks[:, g, :], c_pT[:, g, :],
                                                   start=(q == 0), stop=(q == TT - 1))
                        ins.then_inc(c_pv_full, 1)
                    after(pe, c_pv_out, i, NG1, NG1)
                    for j in range(TT):
                        after(pe, c_wo_taken, i, TT, max(j - 1, 0))
                        for o in range(NG1):
                            ins = nc.tensor.matmul(ps[:, 7 - j % 2, 0:D], c_oT[:, o, j * P:(j + 1) * P],
                                                   wo1[:, o, :], start=(o == 0), stop=(o == NG1 - 1))
                        ins.then_inc(c_wo_full, 1)

            @block.scalar
            def _(act):
                with act.Fori(0, B) as i:
                    for k in range(KD):
                        after(act, c_tp_full, i, C_TP, k + 1)
                        nc.scalar.activation(c_xT[:, k, :], ps[:, k, :], ACT.Identity).then_inc(c_tp_out, 1)
                    for o in range(NG1):
                        after(act, c_q_full, i, NG1, o + 1)
                        nc.scalar.activation(c_qT[:, o, :], ps[:, 6 + o, :], ACT.Identity, scale=DH1 ** -0.5,
                                             bias=scaled[:, 2 * PAIRS + o:2 * PAIRS + o + 1]).then_inc(c_q_out, 1)
                    for j in range(TT):
                        after(act, c_sub, i, TT, j + 1)
                        nc.scalar.activation(c_tok[:, j], c_tok[:, j], ACT.Exp).then_inc(c_exp, 1)
                    for g in range(PAIRS1):
                        after(act, c_tp_full, i, C_TP, KD + g + 1)
                        nc.scalar.activation(c_pT[:, g, :], ps[:, g % 2, :], ACT.Identity).then_inc(c_tp_out, 1)
                    for o in range(NG1):
                        after(act, c_pv_full, i, NG1, o + 1)
                        nc.scalar.activation(c_oT[:, o, :], ps[:, 6 + o, :], ACT.Identity).then_inc(c_pv_out, 1)

            @block.vector
            def _(dve):
                with dve.Fori(0, B) as i:
                    order = Order(dve, c_dve, i, 8 * TT)

                    def subtract_max(j):
                        after(dve, c_s_full, i, TT, j + 1)
                        mask_row = keep[:, j:j + 1, :].broadcast_to([P, G1, KEYS])
                        for o in range(NG1):
                            ins = nc.vector.tensor_tensor(
                                c_tok[:, j, o * G1:(o + 1) * G1, :],
                                ps[:, 2 + 2 * (j % 2) + o, :].rearrange("p (g k) -> p g k", k=KEYS), mask_row,
                                ALU.mult)
                            if o == 0:
                                order.mark(ins)
                        ins.then_inc(c_s_taken, 1)
                        order.join()
                        after(dve, c_s_taken, i, TT, j + 1)
                        order.step(nc.vector.tensor_tensor(c_tok[:, j], c_tok[:, j],
                                                           fill[:, j:j + 1, :].broadcast_to([P, H1, KEYS]), ALU.add))
                        top_ = head_max[:, j, :]
                        order.step(nc.vector.tensor_reduce(top_, c_tok[:, j], AX.X, ALU.max))
                        nc.vector.tensor_tensor(c_tok[:, j], c_tok[:, j],
                                                top_.unsqueeze(2).broadcast_to([P, H1, KEYS]), ALU.subtract)\
                            .then_inc(c_sub, 1)

                    def divide(j):
                        after(dve, c_exp, i, TT, j + 1)
                        sums = head_sum[:, j, :]
                        order.step(nc.vector.tensor_reduce(sums, c_tok[:, j], AX.X, ALU.add))
                        order.step(nc.vector.reciprocal(sums, sums))
                        nc.vector.tensor_tensor(c_tok[:, j], c_tok[:, j],
                                                sums.unsqueeze(2).broadcast_to([P, H1, KEYS]), ALU.mult)\
                            .then_inc(c_prob, 1)

                    subtract_max(0)
                    for j in range(TT):
                        if j + 1 < TT:
                            subtract_max(j + 1)
                        divide(j)
                    add_residual(dve, order, i, (c_wo_full, TT, 0), (c_wo_taken, TT, 0), c_var, c_kept,
                                 [7, 6, 7, 6], c_tmp, c_new, bias=row("bo1"))
                    order.end()

        g_tp, g_out, g_mm, g_v, g_act, g_dve, g_dve_own, slots_ready, expert_ready, scattered, gathered, combined, stored = (
            sem(n) for n in ("g_tp", "g_out", "g_mm", "g_v", "g_act", "g_dve", "g_dve_own", "slots_ready", "expert_ready",
                             "scattered", "gathered", "combined", "stored"))
        with nc.Block() as block:

            @block.sync
            def _(sp):
                sp.dma_start(ew2[:, EARLY:E], ew2_d[EARLY:E].rearrange("e p k n -> p e k n")).then_inc(ld_ew, 16)
                sp.wait_ge(scattered, 16 * NT)
                sp.wait_ge(expert_ready, 1)
                with sp.Fori(0, MT // TURN) as i:
                    for u in range(TURN):
                        t = i * TURN + u
                        e = sp.value_load(expert[0:1, bass.ts(t, 1)], min_val=0, max_val=E - 1)
                        after(sp, e_y_out, i, TURN, u)
                        for dst, src in ((xs[:, u, :], sorted_x[bass.ts(t, P), :]),
                                         (eb1[:, u, :], eb1_d[bass.ts(e, 1), :].broadcast_to([P, HID])),
                                         (eb2[:, u, :], eb2_d[bass.ts(e, 1), :].broadcast_to([P, D]))):
                            sp.dma_start(dst, src).then_inc(e_loaded[u], 16)
                for b in range(B):
                    sp.wait_ge(combined, TT * (b + 1))
                    sp.dma_start(out_tiles[:, b * TT:(b + 1) * TT, :], x_res[:, b * TT:(b + 1) * TT, :])\
                        .then_inc(stored, 16)
                sp.wait_ge(stored, 16 * B)

            @block.gpsimd
            def _(pool):
                pool.wait_ge(slots_ready, 1)
                for t in range(NT):
                    pool.indirect_dma_start(sorted_x, bass.IndirectOffsetOnAxis(ap=slot[:, t:t + 1], axis=0),
                                            xn_e[:, t, :], None).then_inc(scattered, 16)
                with pool.Fori(0, MT // TURN) as i:
                    for u in range(TURN):
                        after(pool, e_y_out, i, TURN, TURN + u)
                        pool.dma_start(sorted_y[bass.ts(i * TURN + u, P), :], ys[:, u, :]).then_inc(e_stored, 16)
                        pool.wait_ge(e_stored, i * (16 * TURN) + (16 * u + 16))
                        pool.sem_inc(e_y_free, 1)
                for t in range(NT):
                    pool.indirect_dma_start(y_back[:, t, :], None, sorted_y,
                                            bass.IndirectOffsetOnAxis(ap=slot[:, t:t + 1], axis=0))\
                        .then_inc(gathered, 16)
                pool.wait_ge(gathered, 16 * NT)

            @block.tensor
            def _(pe):
                for b in range(B):
                    for k in range(KD):
                        if b:
                            pe.wait_ge(g_out, KD * (b - 1) + k + 1)
                        for j in range(TT):
                            ins = nc.tensor.transpose(ps[:, k, j * P:(j + 1) * P],
                                                      xn_e[:, b * TT + j, k * P:(k + 1) * P], ident)
                        ins.then_inc(g_tp, 1)
                    pe.wait_ge(g_out, KD * (b + 1))
                    for j in range(TT):
                        for k in range(KD):
                            t = b * TT + j
                            ins = nc.tensor.matmul(ps[:, 2, t * E:(t + 1) * E], g_xT[:, b % 2, k, j * P:(j + 1) * P],
                                                   gate_w[:, k, :], start=(k == 0), stop=(k == KD - 1))
                    ins.then_inc(g_mm, 1)
                pe.wait_ge(g_v, 2)
                hot = g_hot[:].rearrange("p t e -> p (t e)")
                nc.tensor.matmul(ps[:, 3, 0:P], con("before", P), hot, start=True, stop=True).then_inc(g_mm, 1)
                nc.tensor.matmul(ps[:, 4, 0:P], con("ones", P), hot, start=True, stop=True).then_inc(g_mm, 1)
                pe.wait_ge(expert_ready, 1)
                pe.wait_ge(g_dve, 1)
                pe.wait_ge(ld_ew, 48)

                def columns(i, v):
                    u = v % TURN
                    pe.wait_ge(e_loaded[u], i * 48 + 48 * (v // TURN + 1))
                    after(pe, e_xT, i, TURN, v)
                    for k in range(KD):
                        ins = nc.tensor.transpose(ps[:, 0, k * P:(k + 1) * P], xs[:, u, k * P:(k + 1) * P], ident)
                    ins.then_inc(e_tp_full, 1)

                def up(i, v):
                    e = pe.value_load(expert[0:1, bass.ts(i * TURN + v, 1)], min_val=0, max_val=E - 1)
                    after(pe, e_xT, i, TURN, v + 1)
                    for h in range(2):
                        for k in range(KD):
                            ins = nc.tensor.matmul(
                                ps[:, 2 + 2 * (v % 2) + h, :], xsT[:, v % 2, k, :],
                                ew1[:, bass.ts(e, 1), k, h * S:(h + 1) * S].rearrange("p a n -> p (a n)"),
                                start=(k == 0), stop=(k == KD - 1))
                        ins.then_inc(e_up_full, 1)

                def hidden(i, u):
                    after(pe, e_hT, i, 2 * TURN, 2 * u)
                    for k in range(KH):
                        if k % 4 == 0:
                            after(pe, e_h, i, 2 * TURN, 2 * u + 1 + k // 4)
                        ins = nc.tensor.transpose(ps[:, 6 + k // 4, (k % 4) * P:(k % 4 + 1) * P],
                                                  h_tok[:, u % 2, k * P:(k + 1) * P], ident)
                        if k % 4 == 3:
                            ins.then_inc(e_ht_full, 1)

                def down(i, u):
                    e = pe.value_load(expert[0:1, bass.ts(i * TURN + u, 1)], min_val=0, max_val=E - 1)
                    after(pe, e_y_out, i, TURN, TURN + u - 1)
                    for k in range(KH):
                        if k % 4 == 0:
                            after(pe, e_hT, i, 2 * TURN, 2 * u + 1 + k // 4)
                        ins = nc.tensor.matmul(ps[:, 1, 0:D], hT[:, u % 2, k, :],
                                               ew2[:, bass.ts(e, 1), k, :].rearrange("p a n -> p (a n)"),
                                               start=(k == 0), stop=(k == KH - 1))
                    ins.then_inc(e_down_full, 1)

                def tile(i, u, more=True):
                    if more:
                        columns(i, u + 1)
                    hidden(i, u)
                    if more:
                        up(i, u + 1)
                    down(i, u)

                columns(0, 0)
                up(0, 0)
                with pe.Fori(0, MT // TURN - 1) as i:
                    for u in range(TURN):
                        tile(i, u)
                for u in range(TURN):
                    tile(MT // TURN - 1, u, more=u + 1 < TURN)

            @block.scalar
            def _(act):
                for b in range(B):
                    for k in range(KD):
                        act.wait_ge(g_tp, KD * b + k + 1)
                        if b >= 2:
                            act.wait_ge(g_mm, b - 1)
                        nc.scalar.activation(g_xT[:, b % 2, k, :], ps[:, k, :], ACT.Identity).then_inc(g_out, 1)
                act.wait_ge(g_v, 1)
                nc.scalar.activation(g_e[:], g_e[:], ACT.Exp).then_inc(g_act, 1)
                with act.Fori(0, MT // TURN) as i:
                    for u in range(TURN):
                        for h in range(2):
                            after(act, e_pre, i, 2 * TURN, 2 * u + h + 1)
                            half = h_tok[:, u % 2, h * S:(h + 1) * S]
                            nc.scalar.activation(half, half, ACT.Gelu).then_inc(e_h, 1)

            @block.vector
            def _(dve):
                order = Order(dve, g_dve_own)

                def spread(ap, n=E):
                    return ap.unsqueeze(2).broadcast_to([P, NT, n])

                dve.wait_ge(g_mm, B)
                order.step(nc.vector.tensor_tensor(
                    g_e[:], ps[:, 2, 0:NT * E].rearrange("p (t e) -> p t e", e=E),
                    row("gate_b", E).unsqueeze(1).broadcast_to([P, NT, E]), ALU.add))
                order.step(nc.vector.tensor_reduce(g_max[:], g_e[:], AX.X, ALU.max))
                nc.vector.tensor_tensor(g_e[:], g_e[:], spread(g_max[:]), ALU.subtract).then_inc(g_v, 1)
                dve.wait_ge(g_act, 1)
                order.step(nc.vector.tensor_reduce(g_sum[:], g_e[:], AX.X, ALU.add))
                order.step(nc.vector.reciprocal(g_inv[:], g_sum[:]))
                order.step(nc.vector.tensor_tensor(g_e[:], g_e[:], spread(g_inv[:]), ALU.mult))
                order.step(nc.vector.tensor_reduce(weight[:], g_e[:], AX.X, ALU.max))
                order.step(nc.vector.tensor_tensor(g_eq[:], g_e[:], spread(weight[:]), ALU.is_equal))
                order.step(nc.vector.tensor_tensor(
                    g_eq[:], g_eq[:], con("down", E).unsqueeze(1).broadcast_to([P, NT, E]), ALU.mult))
                order.step(nc.vector.tensor_reduce(g_top[:], g_eq[:], AX.X, ALU.max))
                nc.vector.tensor_tensor(g_hot[:], g_eq[:], spread(g_top[:]), ALU.is_equal).then_inc(g_v, 1)
                dve.wait_ge(g_mm, B + 2)
                order.mark(nc.vector.memset(g_pre[:, 0, :], 0.0))
                order.mark(nc.vector.memset(g_start[:, 0:1], 0.0))
                order.step(nc.vector.tensor_copy(g_tot[:].rearrange("p t e -> p (t e)"), ps[:, 4, 0:P]))
                for t in range(NT):
                    order.step(nc.vector.tensor_tensor(g_pre[:, t + 1, :], g_pre[:, t, :], g_tot[:, t, :], ALU.add))
                order.step(nc.vector.tensor_tensor(g_cmp[:], g_pre[:, NT, :].unsqueeze(2).broadcast_to([P, E, NT]),
                                                   con("full", NT).unsqueeze(1).broadcast_to([P, E, NT]),
                                                   ALU.is_gt))
                order.step(nc.vector.tensor_reduce(g_tiles[:], g_cmp[:], AX.X, ALU.add))
                for e in range(E):
                    order.step(nc.vector.tensor_tensor(g_start[:, e + 1:e + 2], g_start[:, e:e + 1],
                                                       g_tiles[:, e:e + 1], ALU.add))
                order.step(nc.vector.tensor_tensor(g_cmp2[:], con("tile_no", MT).unsqueeze(2).broadcast_to([P, MT, E]),
                                                   g_start[:, 1:E + 1].unsqueeze(1).broadcast_to([P, MT, E]),
                                                   ALU.is_ge))
                order.step(nc.vector.tensor_reduce(g_eid[:], g_cmp2[:], AX.X, ALU.add))
                order.step(nc.vector.tensor_scalar(g_eid[:], g_eid[:], float(E - 1), None, ALU.min))
                nc.vector.tensor_copy(expert[:], g_eid[:]).then_inc(expert_ready, 1)
                order.step(nc.vector.tensor_scalar(g_base[:], g_start[:, 0:E], float(P), None, ALU.mult))
                order.step(nc.vector.tensor_tensor(g_slot[:], g_pre[:, 0:NT, :],
                                                   g_base[:].unsqueeze(1).broadcast_to([P, NT, E]), ALU.add))
                ins = nc.vector.tensor_tensor(g_slot[:].rearrange("p t e -> p (t e)"), ps[:, 3, 0:P],
                                              g_slot[:].rearrange("p t e -> p (t e)"), ALU.add)
                ins.then_inc(g_dve, 1)
                dve.wait_ge(g_dve, 1)
                order.step(nc.vector.tensor_tensor(g_slot[:], g_slot[:], g_hot[:], ALU.mult))
                order.step(nc.vector.tensor_reduce(g_slotf[:], g_slot[:], AX.X, ALU.add))
                nc.vector.tensor_copy(slot[:], g_slotf[:]).then_inc(slots_ready, 1)

                def columns(i, v):
                    after(dve, e_tp_full, i, TURN, v + 1)
                    nc.vector.tensor_copy(xsT[:, v % 2].rearrange("p k n -> p (k n)"), ps[:, 0, 0:D])\
                        .then_inc(e_xT, 1)

                def biased(i, v):
                    for h in range(2):
                        after(dve, e_up_full, i, 2 * TURN, 2 * v + h + 1)
                        nc.vector.tensor_tensor(h_tok[:, v % 2, h * S:(h + 1) * S], ps[:, 2 + 2 * (v % 2) + h, :],
                                                eb1[:, v % TURN, h * S:(h + 1) * S], ALU.add).then_inc(e_pre, 1)

                def tile(i, u, more=True):
                    if more:
                        columns(i, u + 1)
                    for h in range(2):
                        after(dve, e_ht_full, i, 2 * TURN, 2 * u + h + 1)
                        nc.vector.tensor_copy(hT[:, u % 2, h * 4:(h + 1) * 4].rearrange("p k n -> p (k n)"),
                                              ps[:, 6 + h, :]).then_inc(e_hT, 1)
                    if more:
                        biased(i, u + 1)
                    after(dve, e_down_full, i, TURN, u + 1)
                    after(dve, e_y_free, i, TURN, u)
                    nc.vector.tensor_tensor(ys[:, u, :], ps[:, 1, 0:D], eb2[:, u, :], ALU.add).then_inc(e_y_out, 1)

                columns(0, 0)
                biased(0, 0)
                with dve.Fori(0, MT // TURN - 1) as i:
                    for u in range(TURN):
                        tile(i, u)
                for u in range(TURN):
                    tile(MT // TURN - 1, u, more=u + 1 < TURN)
                dve.wait_ge(gathered, 16 * NT)
                for t in range(NT):
                    nc.vector.scalar_tensor_tensor(x_res[:, t, :], y_back[:, t, :], weight[:, t:t + 1], x_res[:, t, :],
                                                   ALU.mult, ALU.add).then_inc(combined, 1)


def chunks(w):
    k, n = w.shape
    return np.ascontiguousarray(w.reshape(k // P, P, n).transpose(1, 0, 2))


def shape_constants():
    p = np.arange(P)
    c = np.zeros((P, NCONST), np.float32)

    def put(name, a):
        a = np.asarray(a, np.float32).reshape(a.shape[0], -1)
        c[:, CONST_AT[name]:CONST_AT[name] + a.shape[1]] = a

    put("ident", np.eye(P))
    put("before", p[:, None] < p[None, :])
    put("ones", np.ones((P, P)))
    put("kmask", p[:, None] // DH1 == np.arange(G1)[None, :])
    put("vmask", (p // DH1)[None, None, :] == 2 * np.arange(TT)[None, :, None] + (p // KEYS)[:, None, None])
    put("down", np.broadcast_to(E - np.arange(E), (P, E)))
    put("full", np.broadcast_to(P * np.arange(NT), (P, NT)))
    put("tile_no", np.broadcast_to(np.arange(MT), (P, MT)))
    put("minus_half", np.full((P, NT), -0.5))
    return c


def kernel(**inputs):
    import concourse.bacc as bacc
    from concourse.bass_utils import run_bass_kernel_spmd

    a = {k: np.asarray(v) for k, v in inputs.items()}
    f0, f1 = "L0_xattn_", "L1_xattn_"
    cols = [a[f0 + n] for n in ("vid_g", "vid_b", "tab_g", "tab_b", "q_g", "q_b", "k_g", "k_b")]
    cols += [a[f1 + n] for n in ("bq", "bk")] + [a["L0_ffn_" + n] for n in ("w1_s", "w2_s", "h1_s", "h2_s")]
    rows = [a[f0 + "bo"], a["L0_ffn_w3_s"], a[f1 + "bv"], a[f1 + "bo"], a["L1_ffn_gate_b"]]
    arrays = {
        "in_x": a["x"], "in_ctx": a["ctx_1024"], "in_mask": a["mask_1x1xSxS2_ik1"],
        "in_cols": np.concatenate([v.reshape(-1, P).T for v in cols], axis=1),
        "in_rows": np.concatenate(rows), "in_const": shape_constants(),
        "in_wk0": chunks(a[f0 + "Wk"]), "in_wv0": chunks(a[f0 + "Wv"]), "in_wq0": chunks(a[f0 + "Wq"]),
        "in_wo0": chunks(a[f0 + "Wo"]),
        "in_wk1": chunks(a[f1 + "Wk"].T), "in_wv1": chunks(a[f1 + "Wv"].T), "in_wq1": chunks(a[f1 + "Wq"].T),
        "in_wo1": chunks(a[f1 + "Wo"].T),
        "in_fw1": chunks(a["L0_ffn_w1_w"].T), "in_fw2": chunks(a["L0_ffn_w2_w"].T),
        "in_fh1": chunks(a["L0_ffn_h1_w"].T), "in_fh2": chunks(a["L0_ffn_h2_w"].T),
        "in_fw3": chunks(a["L0_ffn_w3_w"].T), "in_gate_w": chunks(a["L1_ffn_gate_w"]),
        "in_ew1": a["L1_ffn_w1"].reshape(E, KD, P, HID).transpose(0, 2, 1, 3),
        "in_eb1": a["L1_ffn_b1"],
        "in_ew2": a["L1_ffn_w2"].reshape(E, KH, P, D).transpose(0, 2, 1, 3),
        "in_eb2": a["L1_ffn_b2"],
    }
    arrays = {k: np.ascontiguousarray(v) for k, v in arrays.items()}
    nc = bacc.Bacc("TRN2", target_bir_lowering=False, num_devices=1)
    args = [nc.dram_tensor(k, v.shape, mybir.dt.from_np(v.dtype), kind="ExternalInput").ap()
            for k, v in arrays.items()]
    scratch = [nc.dram_tensor(k, (MT * P, D), F32, kind="Internal").ap() for k in ("sorted_x", "sorted_y")]
    out = nc.dram_tensor("out_0", (B, S, D), F32, kind="ExternalOutput").ap()
    ffn_copy = [nc.dram_tensor(k + "_copy", arrays["in_" + k].shape, F32, kind="Internal").ap()
                for k in ("fw1", "fw2", "fh1", "fw3", "fh2")]
    build(nc, *args, *scratch, ffn_copy, out)
    return run_bass_kernel_spmd(nc, [arrays], core_ids=[0]).results[0]["out_0"]
```

```python
from contextlib import ExitStack

import numpy as np

import concourse.bass as bass
from concourse import mybir

F32 = mybir.dt.float32
F32R = mybir.dt.float32r
I32 = mybir.dt.int32
U32 = mybir.dt.uint32
ALU = mybir.AluOpType
ACT = mybir.ActivationFunctionType
AX = mybir.AxisListType

P = 128
B, S, D = 4, 512, 256
KEYS = 64
ROWS = B * KEYS
TT = S // P
NT = B * TT
KD = D // P
H0, DH0 = 12, 64
INNER = H0 * DH0
PAIRS = H0 // 2
HALF = INNER // 2
HP = H0 // 2
H1, DH1 = 16, 16
G1 = P // DH1
NG1 = H1 // G1
PAIRS1 = H1 // 2
HID = 1024
KH = HID // P
E = 8
TURN = 4
MT = NT + E - 1
TURNS, TAIL = divmod(MT, TURN)
assert TAIL >= 2, "the turns reach two tiles ahead"
EPS = 1e-5

COLS, NCOLS = {}, 0
for _name, _n in (("vid_g", KD), ("vid_b", KD), ("tab_g", KD), ("tab_b", KD), ("q_g", PAIRS), ("q_b", PAIRS),
                  ("k_g", PAIRS), ("k_b", PAIRS), ("bq", KD), ("bk", KD), ("w1_s", KH), ("w2_s", KH),
                  ("h1_s", KH), ("h2_s", KH)):
    COLS[_name] = NCOLS
    NCOLS += _n
ROW_AT, NROWS = {}, 0
for _name, _n in (("bo0", D), ("s3", D), ("bv", D), ("bo1", D), ("gate_b", E)):
    ROW_AT[_name] = NROWS
    NROWS += _n
CONST_AT, NCONST = {}, 0
for _name, _n in (("ident", P), ("before", P), ("ones", P), ("kmask", G1), ("vmask", TT * P), ("down", E),
                  ("full", NT), ("tile_no", MT), ("minus_half", NT), ("token", NT)):
    CONST_AT[_name] = NCONST
    NCONST += _n

F_HID = 3 * KH
RING = 6
RD = D + 2
NOBODY = 2.0 * NT * P
BITS = 2 * HID


def after(eng, sem, turn, per_turn, n):
    eng.wait_ge(sem, turn * per_turn + (n + 1))


class Order:

    def __init__(self, eng, sem, turn=None, per_turn=0):
        self.eng, self.sem, self.turn, self.per_turn, self.n = eng, sem, turn, per_turn, 0

    def mark(self, ins):
        ins.then_inc(self.sem, 1)
        self.n += 1

    def join(self):
        if self.turn is None:
            self.eng.wait_ge(self.sem, self.n)
        else:
            after(self.eng, self.sem, self.turn, self.per_turn, self.n)

    def step(self, ins):
        self.mark(ins)
        self.join()

    def end(self):
        assert self.n == self.per_turn, (self.n, self.per_turn)


def build(nc, x, ctxt, mask, cols_d, rows_d, const_d, wk0_d, wv0_d, wq0_d, wo0_d, wk1_d, wv1_d, wq1_d, wo1_d,
          fw1_d, fw2_d, fh1_d, fh2_d, fw3_d, gate_w_d, ew1_d, eb1_d, ew2_d, eb2_d, sorted_x, x_rows, ffn_copy, out):
    top = ExitStack()
    with top:
        base = -(-nc.sbuf_base // 128) * 128

        def at(name, shape, kb, dt=F32):
            return nc.alloc_sbuf_tensor_at(name, shape, dt, offset=base + int(kb * 1024))

        def sem(name):
            return top.enter_context(nc.semaphore(name))

        x_res = at("x_res", [P, NT, D], 0)
        const = at("const", [P, NCONST], 16)
        cols = at("cols", [P, NCOLS], 20)
        stats = at("stats", [P, NT + 4, 12], 20.3125)
        mean_var = at("mean_var", [P, NT + 4, 2], 21.25)
        var_eps = at("var_eps", [P, NT + 4], 21.40625)
        rstd = at("rstd", [P, NT + 4], 26.75)
        scaled = at("scaled", [P, 2 * PAIRS + KD], 21.5)
        mean_all = at("mean_all", [P, NT], 21.625)
        rstd_all = at("rstd_all", [P, NT], 21.6875)
        weight_bits_f = at("weight_bits_f", [P, 2], 21.78125)
        inexact = at("inexact", [P, 2], 21.8125, I32)
        rows = at("rows", [P, NROWS], 22)
        head_max = at("head_max", [P, TT, H1], 26.25)
        head_sum = at("head_sum", [P, TT, H1], 26.5)
        k1T = at("k1T", [P, NG1, ROWS], 27)
        v1 = at("v1", [P, B, D], 29)
        wq1 = at("wq1", [P, KD, D], 33)
        wo1 = at("wo1", [P, KD, D], 35)
        gate_w = at("gate_w", [P, KD, E], 37.0625)
        keep = at("keep", [P, TT, KEYS], 205.625)
        fill = at("fill", [P, TT, KEYS], 206.625)
        x_in = at("x_in", [P, TT, D], 199.625)
        fw1 = at("fw1", [P, KD, HID], 37.5)
        fw2 = at("fw2", [P, KD, HID], 45.5)
        fh1 = at("fh1", [P, KH, HID], 53.5)
        fw3 = at("fw3", [P, KH, D], 85.5)
        fh2 = at("fh2", [P, KH, HID], 93.5)
        v0 = at("v0", [P, B, INNER], 93.5)
        k0T = at("k0T", [P, PAIRS, ROWS], 105.5)
        wq0 = at("wq0", [P, KD, INNER], 111.5)
        wo0 = at("wo0", [P, PAIRS, D], 117.5)
        k0_blocks = at("k0_blocks", [P, PAIRS, P], 123.5)
        v0_blocks = at("v0_blocks", [P, PAIRS, P], 126.5)
        a_q = at("a_q", [P, TT, INNER], 129.5)
        a_tok = at("a_tok", [P, TT, INNER], 141.5)
        a_feat = at("a_feat", [P, PAIRS, S], 153.5)
        a_pT = at("a_pT", [P, PAIRS, S], 165.5)
        a_xT = at("a_xT", [P, KD, S], 177.5)
        a_tmp = at("a_tmp", [P, 2, D], 181.5)
        xn = at("xn", [P, NT, D], 183.5)
        a_new = at("a_new", [P, 2, D], 203.625)
        wk0 = at("wk0", [P, KD, INNER], 129.5)
        wv0 = at("wv0", [P, KD, INNER], 135.5)
        wk1 = at("wk1", [P, KD, D], 141.5)
        wv1 = at("wv1", [P, KD, D], 143.5)
        c_raw = at("c_raw", [P, 2, D], 145.5)
        ctx_norm = at("ctx_norm", [P, 2, D], 147.5)
        kvT = at("kvT", [P, KD, ROWS], 149.5)
        kvT2 = at("kvT2", [P, KD, B, 2, KEYS], 151.5)
        cT = at("cT", [P, KD, ROWS], 155.5)
        cT2 = at("cT2", [P, KD, B, 2, KEYS], 157.5)
        k_norm = at("k_norm", [P, 2, INNER], 161.5)
        mask_i = at("mask_i", [P, TT, KEYS], 167.5, I32)
        f_ha = [at("f_ha_" + n, [P, KH, S], kb, F32R) for n, kb in (("hi", 125.5), ("lo", 141.5))]
        f_hb = [at("f_hb_" + n, [P, KH, S], kb, F32R) for n, kb in (("hi", 157.5), ("lo", 173.5))]
        f_xT = [at("f_xT_" + n, [P, KD, S], kb, F32R) for n, kb in (("hi", 157.5), ("lo", 161.5))]
        f_raw = at("f_raw", [P, 3, S], 189.5)
        any_bits = [at(f"any_bits{c}", [P, BITS], kb, I32) for c, kb in ((0, 129.5), (1, 173.5))]
        no_row = at("no_row", [P, RD], 203.75)
        f_tmp = at("f_tmp", [P, 2, D], 195.5)
        f_new = at("f_new", [P, 2, D], 197.5)
        c_tok = at("c_tok", [P, TT, H1, KEYS], 127.5)
        c_p = at("c_p", [P, TT, H1, KEYS], 109.5)
        c_pT = at("c_pT", [P, PAIRS1, S], 143.5)
        c_xT = at("c_xT", [P, KD, S], 159.5)
        k1_blocks = at("k1_blocks", [P, NG1, G1, KEYS], 181.625)
        v1_blocks = at("v1_blocks", [P, PAIRS1, P], 185.625)
        c_qT = at("c_qT", [P, NG1, S], 189.625)
        c_oT = at("c_oT", [P, NG1, S], 193.625)
        c_new = at("c_new", [P, 2, D], 197.625)
        ew1 = at("ew1", [P, E, KD, HID], 37.5)
        ew2 = at("ew2", [P, E, KH, D], 101.5)
        xn_e = at("xn_e", [P, NT, RD], 165.5)
        h_tok = at("h_tok", [P, 2, HID], 165.5)
        hT = at("hT", [P, 2, KH, P], 173.5)
        g_xT = at("g_xT", [P, 2, KD, S], 181.625)
        eb1 = at("eb1", [P, TURN, HID], 181.625)
        eb2 = at("eb2", [P, TURN, D], 27)
        xs = at("xs", [P, TURN, RD], 31)
        xsT = at("xsT", [P, 2, KD, P], 35.0625)
        ys = at("ys", [P, TURN, D], 22)
        res = at("res", [P, TURN, D], 197.625)
        token = at("token", [P, TURN], 206.25, U32)
        token_in = at("token_in", [P, TURN], 206.375, U32)
        g_e = at("g_e", [P, NT, E], 197.625)
        g_max = at("g_max", [P, NT], 198.125)
        g_sum = at("g_sum", [P, NT], 198.25)
        g_inv = at("g_inv", [P, NT], 198.5)
        g_eq = at("g_eq", [P, NT, E], 199)
        g_top = at("g_top", [P, NT], 199.5)
        g_hot = at("g_hot", [P, NT, E], 200)
        weight = at("weight", [P, NT], 200.5)
        g_pre = at("g_pre", [P, NT + 1, E], 201)
        g_tot = at("g_tot", [P, NT, E], 202)
        g_cmp = at("g_cmp", [P, E, NT], 202.5)
        g_tiles = at("g_tiles", [P, E], 203)
        g_start = at("g_start", [P, E + 1], 203.25)
        g_slot = at("g_slot", [P, NT, E], 203.5)
        g_slotf = at("g_slotf", [P, NT], 204)
        slot = at("slot", [P, NT], 204.25, U32)
        g_cmp2 = at("g_cmp2", [P, MT, E], 204.5)
        g_eid = at("g_eid", [P, MT], 205.5)
        g_base = at("g_base", [P, E], 205.75)
        expert = at("expert", [P, MT], 206, I32)

        ps = top.enter_context(nc.psum_tensor("ps", [P, 8, 512], F32))

        def con(name, n):
            return const[:, CONST_AT[name]:CONST_AT[name] + n]

        def col(name, i=0):
            return cols[:, COLS[name] + i:COLS[name] + i + 1]

        def row(name, n=D):
            return rows[:, ROW_AT[name]:ROW_AT[name] + n]

        ident = con("ident", P)
        x_tiles = x.rearrange("b (j p) d -> p (b j) d", p=P)
        out_rows = out.rearrange("b s d -> (b s) d")

        ld_small, ld_kv, ld_x, ld_attn, ld_ffn, ld_h2 = (sem(n) for n in (
            "ld_small", "ld_kv", "ld_x", "ld_attn", "ld_ffn", "ld_h2"))
        row_filled, places_filled, ffn_copied = sem("row_filled"), sem("places_filled"), sem("ffn_copied")

        loop_sems = []

        def loop_sem(name):
            loop_sems.append(sem(name))
            return loop_sems[-1]

        a_x_full, a_x_out, a_q_full, a_q_taken, a_qT_full, a_qT_even, a_qT_odd, a_s_full, a_s_taken, a_pT_full, \
            a_pT_out, a_pv_full, a_pv_out, a_wo_full, a_wo_taken, a_exp, a_inv, a_prob, a_keys, a_values, a_q_var, \
            a_q_rstd, a_var, a_norm, a_q_dve, a_s_dve, a_r_dve = (loop_sem("a_" + n) for n in (
                "x_full", "x_out", "q_full", "q_taken", "qT_full", "qT_even", "qT_odd", "s_full", "s_taken",
                "pT_full", "pT_out", "pv_full", "pv_out", "wo_full", "wo_taken", "exp", "inv", "prob", "keys", "values",
                "q_var", "q_rstd", "var", "norm", "q_dve", "s_dve", "r_dve"))
        a_in, f_in, c_in, a_kept, f_kept, c_kept = (loop_sem(n + m) for m in ("_in", "_kept") for n in "afc")
        f_tp_full, f_x_hi, f_x_lo, f_mm_full, f_act_out, f_up_taken, f_split, f_y_taken, f_var, f_norm, f_dve = (
            loop_sem("f_" + n) for n in ("tp_full", "x_hi", "x_lo", "mm_full", "act_out", "up_taken", "split",
                                         "y_taken", "var", "norm", "dve"))
        f_bits_sum, f_bits_or, f_checked = (sem("f_" + n) for n in ("bits_sum", "bits_or", "checked"))
        f_check_own = [sem(f"f_check_own{c}") for c in range(2)]
        c_x_full, c_x_out, c_q_full, c_q_out, c_s_full, c_s_taken, c_pT_full, c_pT_out, c_pv_full, c_pv_out, \
            c_wo_full, c_wo_taken, c_sub, c_exp, c_inv, c_prob, c_keys, c_values, c_var, c_norm, c_rows, c_s_dve, \
            c_r_dve = (loop_sem("c_" + n) for n in (
                "x_full", "x_out", "q_full", "q_out", "s_full", "s_taken", "pT_full", "pT_out", "pv_full", "pv_out",
                "wo_full", "wo_taken", "sub", "exp", "inv", "prob", "keys", "values", "var", "norm", "rows",
                "s_dve", "r_dve"))
        e_tp_full, e_xT, e_up_full, e_pre, e_h, e_ht_full, e_hT, e_down_full, e_y_out, e_y_free = (
            loop_sem("e_" + n) for n in ("tp_full", "xT", "up_full", "pre", "h", "ht_full", "hT", "down_full",
                                         "y_out", "y_free"))
        e_ids, e_sum = loop_sem("e_ids"), loop_sem("e_sum")
        e_stored, ld_ew, x_stored = sem("e_stored"), sem("ld_ew"), sem("x_stored")
        e_gathered = [sem(f"e_gathered{u}") for u in range(TURN)]
        e_loaded = [sem(f"e_loaded{u}") for u in range(TURN)]

        def moments(order, i, chunks):
            nc.vector.nop(nofuse=True)
            for c, chunk in enumerate(chunks):
                order.mark(nc.vector.bn_stats(stats[:, i, 6 * c:6 * c + 6], chunk))
            order.join()
            nc.vector.nop(nofuse=True)
            order.step(nc.vector.bn_aggr(mean_var[:, i, :], stats[:, i, 0:6 * len(chunks)]))

        def add_eps(i, n=1):
            return nc.vector.tensor_scalar_add(var_eps[:, i:i + n], mean_var[:, i:i + n, 1], EPS)

        def rstd_pow(i, n=1):
            return nc.gpsimd.tensor_tensor(rstd[:, i:i + n], var_eps[:, i:i + n], con("minus_half", n), ALU.pow)

        def center_scale(dst, src, i):
            return nc.vector.tensor_scalar(dst, src, mean_var[:, i, 0:1], rstd[:, i:i + 1], ALU.subtract, ALU.mult)

        def bit_steps(order, c, weights):
            bits = any_bits[c]
            pieces = []
            for w in weights:
                flat = w[:].bitcast(I32).rearrange("p k n -> p (k n)")
                pieces += [flat[:, n:n + BITS] for n in range(0, flat.shape[1], BITS)]
            so_far = pieces[0]
            for piece in pieces[1:]:
                order.step(nc.vector.tensor_tensor(bits[:], so_far, piece, ALU.bitwise_or))
                so_far = bits[:]
                yield
            n = BITS
            while n > P:
                n //= 2
                order.step(nc.vector.tensor_tensor(bits[:, 0:n], bits[:, 0:n], bits[:, n:2 * n], ALU.bitwise_or))
                yield
            order.step(nc.vector.tensor_scalar(bits[:, 0:n], bits[:, 0:n], 0xFFF, None, ALU.bitwise_and))
            nc.vector.tensor_reduce(weight_bits_f[:, c:c + 1], bits[:, 0:n], AX.X, ALU.max).then_inc(f_bits_or, 1)
            yield

        def all_partitions_bits(pe, c, bank):
            pe.wait_ge(f_bits_or, c + 1)
            nc.tensor.matmul(ps[:, bank, 0:1], con("ones", P), weight_bits_f[:, c:c + 1], start=True, stop=True)\
                .then_inc(f_bits_sum, 1)

        def take_bits(dve, c, bank):
            dve.wait_ge(f_bits_sum, c + 1)
            nc.vector.tensor_copy(inexact[:, c:c + 1], ps[:, bank, 0:1]).then_inc(f_checked, 1)

        def normalise(pool, dst, batch, done, done_turn, per_turn, first, src=x_res):
            def wide(ap):
                return ap.unsqueeze(2).broadcast_to([P, TT, D])

            pool.nop(nofuse=True)
            pool.tensor_tensor(dst, src[:, bass.ts(batch, TT), :], wide(mean_all[:, bass.ts(batch, TT)]),
                               ALU.subtract).then_inc(done, 1)
            after(pool, done, done_turn, per_turn, first + 1)
            pool.nop(nofuse=True)
            pool.tensor_tensor(dst, dst, wide(rstd_all[:, bass.ts(batch, TT)]), ALU.mult).then_inc(done, 1)

        p_var, p_rstd, p_cnorm, p_knorm, p_pe, p_act, p_v1, p_dve = (sem("p_" + n) for n in (
            "var", "rstd", "cnorm", "knorm", "pe", "act", "v1", "dve"))
        with nc.Block() as block:

            @block.sync
            def _(sp):
                sp.dma_start(c_raw[:], ctxt.rearrange("(r b) k d -> (b k) r d", r=2)).then_inc(ld_small, 16)
                sp.dma_start(const[:], const_d).then_inc(ld_small, 16)
                sp.dma_start(cols[:], cols_d).then_inc(ld_small, 16)
                sp.dma_start(rows[:], rows_d.partition_broadcast(P)).then_inc(ld_small, 16)
                for dst, src in ((wv0, wv0_d), (wk0, wk0_d), (wk1, wk1_d), (wv1, wv1_d)):
                    sp.dma_start(dst[:], src).then_inc(ld_kv, 16)
                sp.dma_start(mask_i[:], mask.rearrange("a b (j p) k -> p (a b j) k", p=P)).then_inc(ld_kv, 16)
                sp.dma_start(x_res[:], x_tiles).then_inc(ld_x, 16)
                for dst, src in ((wq0, wq0_d), (wo0, wo0_d), (wq1, wq1_d), (wo1, wo1_d), (gate_w, gate_w_d)):
                    sp.dma_start(dst[:], src).then_inc(ld_attn, 16)
                for dst, src in zip(ffn_copy, (fw1_d, fw2_d, fh1_d, fw3_d, fh2_d)):
                    sp.dma_start(dst, src).then_inc(ffn_copied, 16)

            @block.gpsimd
            def _(pool):
                for s in loop_sems:
                    pool.sem_inc(s, 1)
                for s in (e_y_out, e_y_free):
                    pool.sem_inc(s, TURN - 1)
                pool.sem_inc(f_y_taken, TT - 1)
                pool.memset(k0_blocks[:], 0.0)
                pool.memset(v0_blocks[:], 0.0)
                pool.wait_ge(ld_small, 64)
                for n, (i, m) in enumerate(((NT, 2), (0, NT), (NT + 2, 1), (NT + 3, 1))):
                    pool.wait_ge(p_var, n + 1)
                    rstd_pow(i, m).then_inc(p_rstd, 1)
                for n, (i, m) in enumerate(((0, TT), (TT, NT - TT))):
                    pool.wait_ge(p_var, 5 + n)
                    nc.gpsimd.tensor_tensor(rstd_all[:, i:i + m], var_eps[:, i:i + m], con("minus_half", m), ALU.pow)\
                        .then_inc(p_rstd, 1)
                    pool.tensor_copy(mean_all[:, i:i + m], mean_var[:, i:i + m, 0]).then_inc(p_rstd, 1)
                    if n == 0:
                        pool.wait_ge(p_rstd, 6)
                        normalise(pool, x_in[:], 0, a_in, 0, 2, 0, src=xn)

            @block.vector
            def _(dve):
                order = Order(dve, p_dve)
                dve.wait_ge(ld_small, 64)
                for i in range(2):
                    moments(order, NT + i, [c_raw[:, i, :]])
                add_eps(NT, 2).then_inc(p_var, 1)
                nc.vector.tensor_scalar_mul(scaled[:, 0:2 * PAIRS], cols[:, COLS["q_g"]:COLS["q_g"] + 2 * PAIRS],
                                            DH0 ** -0.5)
                nc.vector.tensor_scalar_mul(scaled[:, 2 * PAIRS:], cols[:, COLS["bq"]:COLS["bq"] + KD], DH1 ** -0.5)
                dve.wait_ge(p_rstd, 1)
                for i in range(2):
                    center_scale(ctx_norm[:, i, :], c_raw[:, i, :], NT + i).then_inc(p_cnorm, 1)
                dve.wait_ge(ld_kv, 80)
                order.step(nc.vector.tensor_copy(keep[:], mask_i[:]))
                order.step(nc.vector.tensor_scalar(keep[:], keep[:], 0.0, None, ALU.not_equal))
                order.step(nc.vector.tensor_scalar(fill[:], keep[:], -1.0, 1e9, ALU.add, ALU.mult))

                def x_moments(src, first, n):
                    for t in range(first, first + n):
                        order.mark(nc.vector.bn_stats(stats[:, t, 0:6], src[:, t, :]))
                    order.join()
                    for t in range(first, first + n):
                        order.mark(nc.vector.bn_aggr(mean_var[:, t, :], stats[:, t, 0:6]))
                    order.join()
                    add_eps(first, n).then_inc(p_var, 1)

                dve.wait_ge(ld_x, 16)
                x_moments(x_res, 0, NT)
                for r in range(2):
                    dve.wait_ge(p_pe, 9 + r)
                    banks = [ps[:, 2 * r + h, 0:HALF] for h in range(2)]
                    moments(order, NT + 2 + r, banks)
                    add_eps(NT + 2 + r).then_inc(p_var, 1)
                    dve.wait_ge(p_rstd, 3 + r)
                    center_scale(k_norm[:, r, :].rearrange("p (h n) -> p h n", h=2),
                                 ps[:, 2 * r:2 * r + 2, 0:HALF], NT + 2 + r).then_inc(p_knorm, 1)
                for t in range(NT):
                    order.mark(center_scale(xn[:, t, :], x_res[:, t, :], t))
                order.join()
                x_moments(xn, 0, TT)
                for b in range(B):
                    dve.wait_ge(p_pe, 13 + b)
                    nc.vector.tensor_tensor(v1[:, b, :], ps[:, 5 + 2 * (b % 2), 0:D], row("bv"), ALU.add)\
                        .then_inc(p_v1, 1)
                x_moments(xn, TT, NT - TT)

            @block.tensor
            def _(pe):
                pe.wait_ge(ld_small, 64)
                pe.wait_ge(p_cnorm, 2)
                for bank, src in ((0, ctx_norm), (2, c_raw)):
                    for k in range(KD):
                        for r in range(2):
                            ins = nc.tensor.transpose(ps[:, bank + k, r * P:(r + 1) * P],
                                                      src[:, r, k * P:(k + 1) * P], ident)
                        ins.then_inc(p_pe, 1)
                pe.wait_ge(ld_kv, 80)
                for b in range(B):
                    pe.wait_ge(p_act, 4 if b < 2 else 7 + b)
                    for h in range(2):
                        for k in range(KD):
                            ins = nc.tensor.matmul(ps[:, 4 + 2 * (b % 2) + h, 0:HALF],
                                                   kvT2[:, k, b].rearrange("p a s -> p (a s)"),
                                                   wv0[:, k, h * HALF:(h + 1) * HALF],
                                                   start=(k == 0), stop=(k == KD - 1))
                    ins.then_inc(p_pe, 1)
                pe.wait_ge(p_act, 8)
                for r in range(2):
                    for h in range(2):
                        for k in range(KD):
                            ins = nc.tensor.matmul(ps[:, 2 * r + h, 0:HALF], kvT[:, k, r * P:(r + 1) * P],
                                                   wk0[:, k, h * HALF:(h + 1) * HALF],
                                                   start=(k == 0), stop=(k == KD - 1))
                    ins.then_inc(p_pe, 1)
                for o in range(NG1):
                    pe.wait_ge(p_act, 11 + o)
                    for k in range(KD):
                        ins = nc.tensor.matmul(ps[:, 4 + 2 * o, 0:ROWS], wk1[:, k, o * P:(o + 1) * P], cT[:, k, :],
                                               start=(k == 0), stop=(k == KD - 1))
                    ins.then_inc(p_pe, 1)
                for b in range(B):
                    if b >= 2:
                        pe.wait_ge(p_v1, b - 1)
                    for k in range(KD):
                        ins = nc.tensor.matmul(ps[:, 5 + 2 * (b % 2), 0:D],
                                               cT2[:, k, b].rearrange("p a s -> p (a s)"), wv1[:, k, :],
                                               start=(k == 0), stop=(k == KD - 1))
                    ins.then_inc(p_pe, 1)
                pe.wait_ge(p_knorm, 2)
                for g in range(PAIRS):
                    pe.wait_ge(p_act, 13 + g)
                    for r in range(2):
                        ins = nc.tensor.transpose(ps[:, 4 + 2 * (g % 2), r * P:(r + 1) * P],
                                                  k_norm[:, r, g * P:(g + 1) * P], ident)
                    ins.then_inc(p_pe, 1)

            @block.scalar
            def _(act):
                for n, (bank, one, two) in enumerate(((0, kvT, kvT2), (2, cT, cT2))):
                    for k in range(KD):
                        act.wait_ge(p_pe, 2 * n + k + 1)
                        src = ps[:, bank + k, 0:ROWS]
                        how = dict(scale=col("tab_g", k), bias=col("tab_b", k)) if n == 0 else {}
                        nc.scalar.activation(one[:, k, :], src, ACT.Identity, **how).then_inc(p_act, 1)
                        twice = src.rearrange("p (b s) -> p b s", b=B)
                        for half in range(2):
                            ins = nc.scalar.activation(two[:, k, :, half, :], twice, ACT.Identity, **how)
                        ins.then_inc(p_act, 1)
                for b in range(B):
                    act.wait_ge(p_pe, 5 + b)
                    nc.scalar.activation(v0[:, b, :].rearrange("p (h n) -> p h n", h=2),
                                         ps[:, 4 + 2 * (b % 2):6 + 2 * (b % 2), 0:HALF], ACT.Identity)\
                        .then_inc(p_act, 1)
                for o in range(NG1):
                    act.wait_ge(p_pe, 11 + o)
                    nc.scalar.activation(k1T[:, o, :], ps[:, 4 + 2 * o, 0:ROWS], ACT.Identity, bias=col("bk", o))\
                        .then_inc(p_act, 1)
                for g in range(PAIRS):
                    act.wait_ge(p_pe, 17 + g)
                    nc.scalar.activation(k0T[:, g, :], ps[:, 4 + 2 * (g % 2), 0:ROWS], ACT.Identity,
                                         scale=col("k_g", g), bias=col("k_b", g)).then_inc(p_act, 1)

        def residual_tile(dve, order, turn, j, full, taken, var, kept, norm, bank, tmp, new, scale=None,
                          bias=None, ahead=0):
            after(dve, full[0], turn, full[1], full[2] + j + 1)
            x_tile = x_res[:, bass.ts(turn * TT + j, 1), :].rearrange("p a d -> p (a d)")
            if scale is None and bias is None:
                after(dve, kept, turn, TT, max(j - 1, 0))
                if j == 0:
                    after(dve, norm, turn, 2, 0)
                nc.vector.nop(nofuse=True)
                nc.vector.tensor_tensor(new[:, j % 2, :], x_tile, ps[:, bank, 0:D], ALU.add).then_inc(taken, 1)
                after(dve, taken, turn, TT, ahead + j + 1)
                moments(order, j, [new[:, j % 2, :]])
                add_eps(j).then_inc(var, 1)
                return
            by, op = (bias, ALU.add) if scale is None else (scale, ALU.mult)
            nc.vector.tensor_tensor(tmp[:, j % 2, :], ps[:, bank, 0:D], by, op).then_inc(taken, 1)
            after(dve, taken, turn, TT, ahead + j + 1)
            after(dve, kept, turn, TT, max(j - 1, 0))
            if j == 0:
                after(dve, norm, turn, 2, 0)
            order.step(nc.vector.tensor_tensor(new[:, j % 2, :], x_tile, tmp[:, j % 2, :], ALU.add))
            moments(order, j, [new[:, j % 2, :]])
            add_eps(j).then_inc(var, 1)

        def keep_tile(pool, turn, j, var, kept, new):
            after(pool, var, turn, TT, j + 1)
            pool.tensor_copy(x_res[:, bass.ts(turn * TT + j, 1), :], new[:, j % 2:j % 2 + 1, :]).then_inc(kept, 1)

        def keep_moments(pool, turn, norm):
            pool.nop(nofuse=True)
            nc.gpsimd.tensor_tensor(rstd_all[:, bass.ts(turn, TT)], var_eps[:, 0:TT], con("minus_half", TT),
                                    ALU.pow).then_inc(norm, 1)
            pool.tensor_copy(mean_all[:, bass.ts(turn, TT)], mean_var[:, 0:TT, 0]).then_inc(norm, 1)

        with nc.Block() as block:

            @block.sync
            def _(sp):
                sp.wait_ge(ffn_copied, 16 * 5)
                for dst, src in zip((fw1, fw2, fh1, fw3), ffn_copy):
                    sp.dma_start(dst[:], src).then_inc(ld_ffn, 16)

            @block.gpsimd
            def _(pool):
                def rows_in(b, n):
                    after(pool, a_x_full, n, KD, 0)
                    after(pool, a_in, n, 2, 0)
                    normalise(pool, x_in[:], b, a_in, n, 2, 0, src=xn)

                def keys(b):
                    after(pool, a_s_full, b, TT, 0)
                    for h in range(2):
                        half = slice(h * DH0, (h + 1) * DH0)
                        after(pool, a_keys, b, 2, h)
                        pool.tensor_copy(k0_blocks[half, :, half], k0T[half, :, bass.ts(b, KEYS)])\
                            .then_inc(a_keys, 1)
                    after(pool, a_keys, b, 2, 2)

                def values(b):
                    after(pool, a_pv_full, b, PAIRS, 0)
                    for h in range(2):
                        half = slice(h * DH0, (h + 1) * DH0)
                        after(pool, a_values, b, 2, h)
                        pool.tensor_copy(v0_blocks[half, :, half],
                                         v0[half, bass.ts(b, 1), :].rearrange("p a (g c) -> p (a g) c", g=PAIRS)[
                                             :, :, half]).then_inc(a_values, 1)
                    after(pool, a_values, b, 2, 2)

                def q_rstd(b):
                    for j in range(TT):
                        after(pool, a_q_var, b, TT, j + 1)
                        rstd_pow(TT + j).then_inc(a_q_rstd, 1)

                def divide(b, j):
                    after(pool, a_inv, b, TT, j + 1)
                    heads = a_tok[:, j, :].rearrange("p (n k) -> p n k", k=KEYS)
                    nc.gpsimd.tensor_tensor(
                        heads, heads, head_sum[:, j, 0:H0].unsqueeze(2).broadcast_to([P, H0, KEYS]), ALU.mult)\
                        .then_inc(a_prob, 1)

                def turn(b, first=False, last=False):
                    values(b)
                    for j in range(TT):
                        divide(b, j)
                        if j and not first:
                            keep_tile(pool, b - 1, j - 1, a_var, a_kept, a_new)
                    if not first:
                        keep_tile(pool, b - 1, TT - 1, a_var, a_kept, a_new)
                        keep_moments(pool, b - 1, a_norm)
                    if not last:
                        q_rstd(b + 1)
                        keys(b + 1)
                        rows_in((b + 2) % B, b + 2)
                    else:
                        pool.wait_ge(a_in, 2 * (B + 1) + 1)
                        normalise(pool, x_in[:], 0, f_in, 0, 2, 0)

                keys(0)
                q_rstd(0)
                rows_in(1, 1)
                turn(0, first=True)
                with pool.Fori(1, B - 1) as i:
                    turn(i)
                turn(B - 1, last=True)
                for j in range(TT):
                    keep_tile(pool, B - 1, j, a_var, a_kept, a_new)
                keep_moments(pool, B - 1, a_norm)
                pool.wait_ge(f_in, 3)

            @block.tensor
            def _(pe):
                def columns(b):
                    after(pe, a_in, b, 2, 2)
                    after(pe, a_qT_even, b, PAIRS // 2, 0)
                    after(pe, a_qT_odd, b, PAIRS // 2, 0)
                    for k in range(KD):
                        for j in range(TT):
                            ins = nc.tensor.transpose(ps[:, k, j * P:(j + 1) * P], x_in[:, j, k * P:(k + 1) * P],
                                                      ident)
                        ins.then_inc(a_x_full, 1)
                    after(pe, a_x_out, b, KD, KD)

                def project(b, j):
                    after(pe, *((a_s_taken, b, TT, j - 1) if j < 2 else (a_q_taken, b, TT, j - 1)))
                    for h in range(2):
                        for k in range(KD):
                            ins = nc.tensor.matmul(ps[:, 2 + 2 * (j % 2) + h, 0:HALF], a_xT[:, k, j * P:(j + 1) * P],
                                                   wq0[:, k, h * HALF:(h + 1) * HALF],
                                                   start=(k == 0), stop=(k == KD - 1))
                    ins.then_inc(a_q_full, 1)

                def pair_columns(src, g, full):
                    for j in range(TT):
                        ins = nc.tensor.transpose(ps[:, g % 2, j * P:(j + 1) * P], src[:, j, g * P:(g + 1) * P],
                                                  ident)
                    ins.then_inc(full, 1)

                def queries(b):
                    after(pe, a_q_taken, b, TT, TT)
                    for g in range(PAIRS):
                        if g >= 2:
                            after(pe, a_qT_odd if g % 2 else a_qT_even, b, PAIRS // 2, g // 2)
                        pair_columns(a_q, g, a_qT_full)

                def probabilities(b):
                    after(pe, a_prob, b, TT, TT)
                    for g in range(PAIRS):
                        if g >= 2:
                            after(pe, a_pT_out, b, PAIRS, g - 1)
                        pair_columns(a_tok, g, a_pT_full)

                def scores(b, j):
                    if j == 0:
                        after(pe, a_qT_even, b, PAIRS // 2, PAIRS // 2)
                        after(pe, a_qT_odd, b, PAIRS // 2, PAIRS // 2)
                        after(pe, a_keys, b, 2, 2)
                    if j >= 2:
                        after(pe, a_s_taken, b, TT, j - 1)
                    for g in range(PAIRS):
                        ins = nc.tensor.matmul(ps[:, 2 + 2 * (j % 2) + g // 3, (g % 3) * P:(g % 3 + 1) * P],
                                               a_feat[:, g, j * P:(j + 1) * P], k0_blocks[:, g, :],
                                               start=True, stop=True)
                    ins.then_inc(a_s_full, 1)

                def heads(b):
                    after(pe, a_wo_taken, b, TT, 0)
                    after(pe, a_values, b, 2, 2)
                    for g in range(PAIRS):
                        after(pe, a_pT_out, b, PAIRS, g + 1)
                        if g >= 2:
                            after(pe, a_pv_out, b, PAIRS, g - 1)
                        nc.tensor.matmul(ps[:, 6 + g % 2, :], v0_blocks[:, g, :], a_pT[:, g, :],
                                         start=True, stop=True).then_inc(a_pv_full, 1)

                def output(b, j):
                    after(pe, a_pv_out, b, PAIRS, PAIRS)
                    if j >= 2:
                        after(pe, a_wo_taken, b, TT, j - 1)
                    for g in range(PAIRS):
                        ins = nc.tensor.matmul(ps[:, 7 - j % 2, 0:D], a_pT[:, g, j * P:(j + 1) * P],
                                               wo0[:, g, :], start=(g == 0), stop=(g == PAIRS - 1))
                    ins.then_inc(a_wo_full, 1)

                def turn(b, first=False, last=False):
                    scores(b, 0)
                    for j in range(TT):
                        if j + 1 < TT:
                            scores(b, j + 1)
                        if not first:
                            output(b - 1, j)
                    if not last:
                        columns(b + 1)
                        project(b + 1, 0)
                        project(b + 1, 1)
                    probabilities(b)
                    if not last:
                        project(b + 1, 2)
                        project(b + 1, 3)
                    heads(b)
                    if not last:
                        queries(b + 1)

                pe.wait_ge(ld_attn, 80)
                columns(0)
                for j in range(TT):
                    project(0, j)
                queries(0)
                turn(0, first=True)
                with pe.Fori(1, B - 1) as i:
                    turn(i)
                turn(B - 1, last=True)
                for j in range(TT):
                    output(B - 1, j)
                all_partitions_bits(pe, 0, 0)

            @block.scalar
            def _(act):
                def project(b):
                    for k in range(KD):
                        after(act, a_x_full, b, KD, k + 1)
                        nc.scalar.activation(a_xT[:, k, :], ps[:, k, :], ACT.Identity, scale=col("vid_g", k),
                                             bias=col("vid_b", k)).then_inc(a_x_out, 1)

                def queries(b):
                    for g in range(0, PAIRS, 2):
                        after(act, a_qT_full, b, PAIRS, g + 1)
                        nc.scalar.activation(a_feat[:, g, :], ps[:, g % 2, :], ACT.Identity,
                                             scale=scaled[:, g:g + 1], bias=scaled[:, PAIRS + g:PAIRS + g + 1])\
                            .then_inc(a_qT_even, 1)

                def turn(b, last=False):
                    for j in range(TT):
                        after(act, a_s_taken, b, TT, j + 1)
                        nc.scalar.activation(a_tok[:, j, :], a_tok[:, j, :], ACT.Exp).then_inc(a_exp, 1)
                    if not last:
                        project(b + 1)
                    for g in range(PAIRS):
                        after(act, a_pT_full, b, PAIRS, g + 1)
                        nc.scalar.activation(a_pT[:, g, :], ps[:, g % 2, :], ACT.Identity).then_inc(a_pT_out, 1)
                    for g in range(PAIRS):
                        after(act, a_pv_full, b, PAIRS, g + 1)
                        nc.scalar.activation(a_pT[:, g, :], ps[:, 6 + g % 2, :], ACT.Identity)\
                            .then_inc(a_pv_out, 1)
                    if not last:
                        queries(b + 1)

                project(0)
                queries(0)
                with act.Fori(0, B - 1) as i:
                    turn(i)
                turn(B - 1, last=True)

            @block.vector
            def _(dve):
                def queries(b):
                    order = Order(dve, a_q_dve, b, 3 * TT)

                    def q_moments(j):
                        after(dve, a_q_full, b, TT, j + 1)
                        moments(order, TT + j, [ps[:, 2 + 2 * (j % 2) + h, 0:HALF] for h in range(2)])
                        add_eps(TT + j).then_inc(a_q_var, 1)

                    for j in range(TT):
                        if j % 2 == 0:
                            q_moments(j)
                            q_moments(j + 1)
                        after(dve, a_q_rstd, b, TT, j + 1)
                        center_scale(a_q[:, j, :].rearrange("p (h n) -> p h n", h=2),
                                     ps[:, 2 + 2 * (j % 2):4 + 2 * (j % 2), 0:HALF], TT + j)\
                            .then_inc(a_q_taken, 1)
                    for g in range(1, PAIRS, 2):
                        after(dve, a_qT_full, b, PAIRS, g + 1)
                        nc.vector.tensor_scalar(a_feat[:, g, :], ps[:, g % 2, :], scaled[:, g:g + 1],
                                                scaled[:, PAIRS + g:PAIRS + g + 1], ALU.mult, ALU.add)\
                            .then_inc(a_qT_odd, 1)
                    order.end()

                def turn(b, first=False, last=False):
                    order = Order(dve, a_s_dve, b, 3 * TT)

                    def subtract_max(j):
                        after(dve, a_s_full, b, TT, j + 1)
                        top_ = head_max[:, j, 0:H0]
                        banks = ps[:, 2 + 2 * (j % 2):4 + 2 * (j % 2), 0:HALF].rearrange(
                            "p h (n k) -> p h n k", k=KEYS)
                        order.step(nc.vector.tensor_reduce(top_.rearrange("p (h n) -> p h n", h=2), banks, AX.X,
                                                           ALU.max))
                        for h in range(2):
                            ins = nc.vector.tensor_tensor(
                                a_tok[:, j, h * HALF:(h + 1) * HALF].rearrange("p (n k) -> p n k", k=KEYS),
                                banks[:, h], top_[:, h * HP:(h + 1) * HP].unsqueeze(2).broadcast_to([P, HP, KEYS]),
                                ALU.subtract)
                            if h == 0:
                                order.mark(ins)
                        ins.then_inc(a_s_taken, 1)

                    def invert_sum(j):
                        after(dve, a_exp, b, TT, j + 1)
                        sums = head_sum[:, j, 0:H0]
                        order.step(nc.vector.tensor_reduce(
                            sums, a_tok[:, j, :].rearrange("p (n k) -> p n k", k=KEYS), AX.X, ALU.add))
                        nc.vector.reciprocal(sums, sums).then_inc(a_inv, 1)

                    rest = None if first else Order(dve, a_r_dve, b - 1, 3 * TT)
                    subtract_max(0)
                    for j in range(TT):
                        if j + 1 < TT:
                            subtract_max(j + 1)
                        invert_sum(j)
                        if j and not first:
                            residual(rest, b - 1, j - 1)
                    if not first:
                        residual(rest, b - 1, TT - 1)
                        rest.end()
                    order.end()
                    if not last:
                        queries(b + 1)

                def residual(order, b, j):
                    residual_tile(dve, order, b, j, (a_wo_full, TT, 0), a_wo_taken, a_var, a_kept, a_norm,
                                  7 - j % 2, a_tmp, a_new, bias=row("bo0"))

                queries(0)
                turn(0, first=True)
                with dve.Fori(1, B - 1) as i:
                    turn(i)
                turn(B - 1, last=True)
                order = Order(dve, a_r_dve, B - 1, 3 * TT)
                dve.wait_ge(ld_ffn, 64)
                steps = bit_steps(Order(dve, f_check_own[0]), 0, (fh1, fw1, fw2, fw3))
                for n in range(5):
                    next(steps)
                for j in range(TT):
                    residual(order, B - 1, j)
                    next(steps, None)
                order.end()
                for _ in steps:
                    pass
                take_bits(dve, 0, 0)

        def ring_bank(n):
            return 2 + n % RING

        def ring_free(pe, turn, n):
            n -= RING
            if n < 0:
                if n >= -TT:
                    after(pe, f_y_taken, turn, TT, n + TT)
            elif n < 2 * KH:
                after(pe, *((f_up_taken, turn, KH) if n % 2 else (f_act_out, turn, F_HID)), n // 2 + 1)
            else:
                after(pe, f_act_out, turn, F_HID, KH + n - 2 * KH + 1)

        F_MM = 4 * KH + TT
        with nc.Block() as block:

            @block.sync
            def _(sp):
                sp.dma_start(fh2[:], ffn_copy[4]).then_inc(ld_h2, 16)
                sp.wait_ge(row_filled, 2)
                sp.dma_start(sorted_x.rearrange("(t p) d -> p t d", p=P),
                             no_row[:].unsqueeze(1).broadcast_to([P, MT, RD])).then_inc(places_filled, 16)
                sp.wait_ge(places_filled, 16)

            @block.gpsimd
            def _(pool):
                pool.memset(no_row[:, 0:D], 0.0).then_inc(row_filled, 1)
                pool.memset(no_row[:, D:RD], NOBODY).then_inc(row_filled, 1)
                with pool.Fori(0, B) as i:
                    after(pool, f_tp_full, i, KD, KD)
                    normalise(pool, x_in[:], (i + 1) % B, f_in, i + 1, 2, 0)
                    for j in range(TT):
                        keep_tile(pool, i, j, f_var, f_kept, f_new)
                    keep_moments(pool, i, f_norm)

            @block.tensor
            def _(pe):
                def product(exact, out, w, x, w_at, x_at, signal, swap=False, ready=None):
                    n = w.shape[1]

                    def passes(one_pass):
                        for k in range(n):
                            if ready is not None:
                                ready(k)
                            for part in range(2):
                                wk = w[:, k, w_at].bitcast(F32R) if one_pass else w[:, k, w_at]
                                xk = x[part][:, k, x_at]
                                xk = xk if one_pass else xk.bitcast(F32)
                                ins = nc.tensor.matmul(out, *((xk, wk) if swap else (wk, xk)),
                                                       start=(k == 0 and part == 0),
                                                       stop=(k == n - 1 and part == 1))
                        ins.then_inc(signal, 1)

                    with pe.If(exact == 0):
                        passes(True)
                    with pe.Else():
                        passes(False)

                def columns(b):
                    after(pe, f_in, b, 2, 2)
                    after(pe, f_x_lo, b, KD, 0)
                    for k in range(KD):
                        for j in range(TT):
                            ins = nc.tensor.transpose(ps[:, k, j * P:(j + 1) * P], x_in[:, j, k * P:(k + 1) * P],
                                                      ident)
                        ins.then_inc(f_tp_full, 1)

                columns(0)
                pe.wait_ge(f_checked, 1)
                with pe.Fori(0, B) as i:
                    first = pe.value_load(inexact[0:1, 0:1])
                    after(pe, f_x_lo, i, KD, KD)
                    for o in range(KH):
                        for n, w in ((2 * o, fw1), (2 * o + 1, fw2)):
                            ring_free(pe, i, n)
                            product(first, ps[:, ring_bank(n), :], w, f_xT, slice(o * P, (o + 1) * P),
                                    slice(0, S), f_mm_full)
                    for at_, w, src in ((2 * KH, fh1, f_ha), (3 * KH, fh2, f_hb)):
                        if w is fh2:
                            with pe.If(i == 0):
                                all_partitions_bits(pe, 1, 0)
                            pe.wait_ge(f_checked, 2)
                            second = pe.value_load(inexact[0:1, 1:2])
                        flag = first if w is fh1 else second
                        for o in range(KH):
                            ring_free(pe, i, at_ + o)
                            ready = (lambda k: after(pe, f_split, i, F_HID, at_ - 2 * KH + k + 1)) if o == 0 else None
                            product(flag, ps[:, ring_bank(at_ + o), :], w, src, slice(o * P, (o + 1) * P),
                                    slice(0, S), f_mm_full, ready=ready)
                    columns(i + 1)
                    for j in range(TT):
                        ring_free(pe, i, 4 * KH + j)
                        ready = (lambda k: after(pe, f_split, i, F_HID, 2 * KH + k + 1)) if j == 0 else None
                        product(first, ps[:, ring_bank(4 * KH + j), 0:D], fw3, f_ha, slice(0, D),
                                slice(j * P, (j + 1) * P), f_mm_full, swap=True, ready=ready)

            @block.scalar
            def _(act):
                with act.Fori(0, B) as i:
                    for m in range(F_HID):
                        o = m % KH
                        n = 2 * o if m < KH else m + KH
                        after(act, f_mm_full, i, F_MM, n + 1)
                        after(act, f_split, i, F_HID, max(m - 2, 0))
                        nc.scalar.activation(f_raw[:, m % 3, :], ps[:, ring_bank(n), :],
                                             ACT.Silu if m < KH else ACT.Gelu,
                                             scale=col(("w1_s", "h1_s", "h2_s")[m // KH], o)).then_inc(f_act_out, 1)

            @block.vector
            def _(dve):
                def columns(b):
                    for k in range(KD):
                        after(dve, f_tp_full, b, KD, k + 1)
                        nc.vector.tensor_copy(f_xT[0][:, k, :], ps[:, k, :]).then_inc(f_x_hi, 1)
                        after(dve, f_x_hi, b, KD, k + 1)
                        nc.vector.tensor_tensor(f_xT[1][:, k, :], ps[:, k, :], f_xT[0][:, k, :].bitcast(F32),
                                                ALU.subtract).then_inc(f_x_lo, 1)

                columns(0)
                with dve.Fori(0, B) as i:
                    order = Order(dve, f_dve, i, F_HID + 3 * TT)
                    for m in range(F_HID):
                        o = m % KH
                        raw = f_raw[:, m % 3, :]
                        if m < KH:
                            after(dve, f_mm_full, i, F_MM, 2 * o + 2)
                            after(dve, f_act_out, i, F_HID, m + 1)
                            nc.vector.scalar_tensor_tensor(raw, ps[:, ring_bank(2 * o + 1), :], col("w2_s", o), raw,
                                                           ALU.mult, ALU.mult).then_inc(f_up_taken, 1)
                            after(dve, f_up_taken, i, KH, o + 1)
                        else:
                            after(dve, f_act_out, i, F_HID, m + 1)
                        hi, lo = (part[:, o, :] for part in (f_hb if m // KH == 1 else f_ha))
                        order.step(nc.vector.tensor_copy(hi, raw))
                        nc.vector.tensor_tensor(lo, raw, hi.bitcast(F32), ALU.subtract).then_inc(f_split, 1)
                        if m == KH - 1:
                            with dve.If(i == 0):
                                dve.wait_ge(ld_h2, 16)
                                for _ in bit_steps(Order(dve, f_check_own[1]), 1, (fh2,)):
                                    pass
                        if m == 2 * KH - 1:
                            with dve.If(i == 0):
                                take_bits(dve, 1, 0)
                    columns(i + 1)
                    for j in range(TT):
                        residual_tile(dve, order, i, j, (f_mm_full, F_MM, 4 * KH), f_y_taken, f_var, f_kept,
                                      f_norm, ring_bank(4 * KH + j), f_tmp, f_new, scale=row("s3"),
                                      ahead=TT - 1)
                    order.end()

        g_tp, g_out, g_mm, g_v, g_act, g_dve, g_dve_own, slots_ready, expert_ready, scattered = (
            sem(n) for n in ("g_tp", "g_out", "g_mm", "g_v", "g_act", "g_dve", "g_dve_own", "slots_ready",
                             "expert_ready", "scattered"))
        EARLY = 1
        with nc.Block() as block:

            @block.sync
            def _(sp):
                sp.dma_start(ew1[:], ew1_d.rearrange("e p k n -> p e k n")).then_inc(ld_ew, 16)
                sp.dma_start(ew2[:, 0:EARLY], ew2_d[0:EARLY].rearrange("e p k n -> p e k n")).then_inc(ld_ew, 16)
                sp.wait_ge(c_pv_full, B * NG1 + 1)
                sp.dma_start(ew2[:, EARLY:E], ew2_d[EARLY:E].rearrange("e p k n -> p e k n")).then_inc(ld_ew, 16)

            @block.gpsimd
            def _(pool):
                pool.sem_inc(c_in, 2)

                def keys(b):
                    after(pool, c_s_full, b, TT, 0)
                    pool.nop(nofuse=True)
                    for o in range(NG1):
                        pool.tensor_tensor(k1_blocks[:, o],
                                           k1T[:, o, bass.ts(b % B, KEYS)].unsqueeze(1).broadcast_to([P, G1, KEYS]),
                                           con("kmask", G1).unsqueeze(2).broadcast_to([P, G1, KEYS]), ALU.mult)\
                            .then_inc(c_keys, 1)

                def values(b):
                    after(pool, c_pv_full, b, NG1, 0)
                    pool.nop(nofuse=True)
                    for o in range(NG1):
                        pool.tensor_tensor(v1_blocks[:, o * TT:(o + 1) * TT, :],
                                           v1[:, bass.ts(b, 1), o * P:(o + 1) * P].broadcast_to([P, TT, P]),
                                           con("vmask", TT * P).rearrange("p (a c) -> p a c", c=P), ALU.mult)\
                            .then_inc(c_values, 1)

                def rows_in(b):
                    after(pool, c_x_full, b, KD, 0)
                    normalise(pool, x_in[:], b % B, c_in, b, 2, 0)

                def divide(b, j):
                    after(pool, c_inv, b, TT, j + 1)
                    after(pool, c_pT_full, b, PAIRS1, 0)
                    nc.gpsimd.tensor_tensor(c_p[:, j], c_tok[:, j],
                                            head_sum[:, j, :].unsqueeze(2).broadcast_to([P, H1, KEYS]), ALU.mult)\
                        .then_inc(c_prob, 1)

                def turn(b, softmax=True, heads=True, output=True, more=True):
                    def keep(j):
                        if output:
                            keep_tile(pool, b - 2, j, c_var, c_kept, c_new)

                    if heads:
                        values(b - 1)
                    if more:
                        rows_in(b + 1)
                    keep(0)
                    keep(1)
                    if softmax:
                        divide(b, 0)
                    if more:
                        keys(b + 1)
                    if softmax:
                        divide(b, 1)
                    keep(2)
                    if softmax:
                        divide(b, 2)
                    keep(3)
                    if output:
                        keep_moments(pool, b - 2, c_norm)
                    if softmax:
                        divide(b, 3)
                    if output:
                        after(pool, c_norm, b - 2, 2, 2)
                        normalise(pool, xn_e[:, bass.ts(b - 2, TT), 0:D], b - 2, c_rows, b - 2, 2, 0)

                keys(0)
                turn(0, heads=False, output=False)
                turn(1, output=False)
                with pool.Fori(2, B) as i:
                    turn(i)
                turn(B, softmax=False, more=False)
                turn(B + 1, softmax=False, heads=False, more=False)
                pool.wait_ge(c_in, 2 * (B + 1) + 1)
                pool.wait_ge(c_rows, 2 * B + 1)

            @block.tensor
            def _(pe):
                def columns(b):
                    after(pe, c_in, b, 2, 2)
                    for k in range(KD):
                        for j in range(TT):
                            ins = nc.tensor.transpose(ps[:, k, j * P:(j + 1) * P], x_in[:, j, k * P:(k + 1) * P],
                                                      ident)
                        ins.then_inc(c_x_full, 1)

                def queries(b):
                    after(pe, c_x_out, b, KD, KD)
                    for o in range(NG1):
                        for k in range(KD):
                            ins = nc.tensor.matmul(ps[:, o, :], wq1[:, k, o * P:(o + 1) * P], c_xT[:, k, :],
                                                   start=(k == 0), stop=(k == KD - 1))
                        ins.then_inc(c_q_full, 1)

                def scores(b, j):
                    if j == 0:
                        after(pe, c_q_out, b, NG1, NG1)
                        after(pe, c_keys, b, NG1, NG1)
                    after(pe, c_s_taken, b, TT, j - 1)
                    for o in range(NG1):
                        ins = nc.tensor.matmul(ps[:, 2 + 2 * (j % 2) + o, :], c_qT[:, o, j * P:(j + 1) * P],
                                               k1_blocks[:, o].rearrange("p g k -> p (g k)"),
                                               start=True, stop=True)
                    ins.then_inc(c_s_full, 1)

                def probabilities(b):
                    after(pe, c_prob, b, TT, TT)
                    after(pe, c_q_out, b + 1, NG1, NG1)
                    for g in range(PAIRS1):
                        if g >= 2:
                            after(pe, c_pT_out, b, PAIRS1, g - 1)
                        for j in range(TT):
                            ins = nc.tensor.transpose(ps[:, g % 2, j * P:(j + 1) * P],
                                                      c_p[:, j, 2 * g:2 * g + 2, :].rearrange("p a k -> p (a k)"),
                                                      ident)
                        ins.then_inc(c_pT_full, 1)

                def heads(b, o):
                    after(pe, c_values, b, NG1, NG1)
                    after(pe, c_pT_out, b, PAIRS1, PAIRS1)
                    for q in range(TT):
                        g = o * TT + q
                        ins = nc.tensor.matmul(ps[:, o, :], v1_blocks[:, g, :], c_pT[:, g, :],
                                               start=(q == 0), stop=(q == TT - 1))
                    ins.then_inc(c_pv_full, 1)

                def project(b, j):
                    after(pe, c_wo_taken, b, TT, j - 1)
                    for o in range(NG1):
                        nc.tensor.matmul(ps[:, 7 - j % 2, 0:D], c_oT[:, o, j * P:(j + 1) * P],
                                         wo1[:, o, :], start=(o == 0), stop=False)
                    ins = nc.tensor.matmul(ps[:, 7 - j % 2, 0:D], con("ones", P)[0:1, :], row("bo1")[0:1, :],
                                           start=False, stop=True)
                    ins.then_inc(c_wo_full, 1)

                def turn(b, softmax=True, with_heads=True, output=True, more=True):
                    if softmax:
                        scores(b, 0)
                        scores(b, 1)
                    if output:
                        project(b - 2, 0)
                        project(b - 2, 1)
                    if with_heads:
                        probabilities(b - 1)
                    if softmax:
                        scores(b, 2)
                    if output:
                        project(b - 2, 2)
                        project(b - 2, 3)
                    if softmax:
                        scores(b, 3)
                    if with_heads:
                        for o in range(NG1):
                            heads(b - 1, o)
                        after(pe, c_pv_out, b - 1, NG1, NG1)
                    if more:
                        columns(b + 1)
                        queries(b + 1)

                def gate_logits(b):
                    pe.wait_ge(c_rows, 2 * (b + 1) + 1)
                    after(pe, c_keys, B, NG1, NG1)
                    for k in range(KD):
                        if b:
                            pe.wait_ge(g_out, KD * (b - 1) + k + 1)
                        for j in range(TT):
                            ins = nc.tensor.transpose(ps[:, k, j * P:(j + 1) * P],
                                                      xn_e[:, b * TT + j, k * P:(k + 1) * P], ident)
                        ins.then_inc(g_tp, 1)
                    pe.wait_ge(g_out, KD * (b + 1))
                    for j in range(TT):
                        for k in range(KD):
                            t = b * TT + j
                            ins = nc.tensor.matmul(ps[:, 2, t * E:(t + 1) * E], g_xT[:, b % 2, k, j * P:(j + 1) * P],
                                                   gate_w[:, k, :], start=(k == 0), stop=(k == KD - 1))
                    ins.then_inc(g_mm, 1)

                columns(0)
                queries(0)
                turn(0, with_heads=False, output=False)
                turn(1, output=False)
                with pe.Fori(2, B) as i:
                    turn(i)
                turn(B, softmax=False, more=False)
                gate_logits(0)
                gate_logits(1)
                turn(B + 1, softmax=False, with_heads=False, more=False)
                for b in range(2, B):
                    gate_logits(b)

            @block.scalar
            def _(act):
                def columns(b):
                    for k in range(KD):
                        after(act, c_x_full, b, KD, k + 1)
                        nc.scalar.activation(c_xT[:, k, :], ps[:, k, :], ACT.Identity).then_inc(c_x_out, 1)

                def queries(b):
                    for o in range(NG1):
                        after(act, c_q_full, b, NG1, o + 1)
                        nc.scalar.activation(c_qT[:, o, :], ps[:, o, :], ACT.Identity, scale=DH1 ** -0.5,
                                             bias=scaled[:, 2 * PAIRS + o:2 * PAIRS + o + 1]).then_inc(c_q_out, 1)

                def turn(b, softmax=True, heads=True, more=True):
                    def exponentials(j):
                        if softmax:
                            after(act, c_sub, b, TT, j + 1)
                            nc.scalar.activation(c_tok[:, j], c_tok[:, j], ACT.Exp).then_inc(c_exp, 1)

                    if heads:
                        for g in range(PAIRS1):
                            after(act, c_pT_full, b - 1, PAIRS1, g + 1)
                            nc.scalar.activation(c_pT[:, g, :], ps[:, g % 2, :], ACT.Identity).then_inc(c_pT_out, 1)
                    for j in range(TT - 1):
                        exponentials(j)
                    if heads:
                        for o in range(NG1):
                            after(act, c_pv_full, b - 1, NG1, o + 1)
                            nc.scalar.activation(c_oT[:, o, :], ps[:, o, :], ACT.Identity).then_inc(c_pv_out, 1)
                    if more:
                        columns(b + 1)
                    exponentials(TT - 1)
                    if more:
                        queries(b + 1)

                columns(0)
                queries(0)
                turn(0, heads=False)
                turn(1)
                with act.Fori(2, B) as i:
                    turn(i)
                turn(B, softmax=False, more=False)
                for b in range(B):
                    for k in range(KD):
                        act.wait_ge(g_tp, KD * b + k + 1)
                        if b >= 2:
                            act.wait_ge(g_mm, b - 1)
                        nc.scalar.activation(g_xT[:, b % 2, k, :], ps[:, k, :], ACT.Identity).then_inc(g_out, 1)

            @block.vector
            def _(dve):
                def turn(b, softmax=True, output=True):
                    order = Order(dve, c_s_dve, b, 4 * TT) if softmax else None
                    rest = Order(dve, c_r_dve, b - 2, 2 * TT) if output else None

                    def subtract_max(j):
                        if not softmax:
                            return
                        after(dve, c_s_full, b, TT, j + 1)
                        after(dve, c_prob, b, TT, 0)
                        mask_row = keep[:, j:j + 1, :].broadcast_to([P, G1, KEYS])
                        for o in range(NG1):
                            ins = nc.vector.tensor_tensor(
                                c_tok[:, j, o * G1:(o + 1) * G1, :],
                                ps[:, 2 + 2 * (j % 2) + o, :].rearrange("p (g k) -> p g k", k=KEYS), mask_row,
                                ALU.mult)
                            if o == 0:
                                order.mark(ins)
                        ins.then_inc(c_s_taken, 1)
                        order.join()
                        after(dve, c_s_taken, b, TT, j + 1)
                        order.step(nc.vector.tensor_tensor(c_tok[:, j], c_tok[:, j],
                                                           fill[:, j:j + 1, :].broadcast_to([P, H1, KEYS]), ALU.add))
                        top_ = head_max[:, j, :]
                        order.step(nc.vector.tensor_reduce(top_, c_tok[:, j], AX.X, ALU.max))
                        nc.vector.tensor_tensor(c_tok[:, j], c_tok[:, j],
                                                top_.unsqueeze(2).broadcast_to([P, H1, KEYS]), ALU.subtract)\
                            .then_inc(c_sub, 1)

                    def invert_sum(j):
                        if not softmax:
                            return
                        after(dve, c_exp, b, TT, j + 1)
                        sums = head_sum[:, j, :]
                        order.step(nc.vector.tensor_reduce(sums, c_tok[:, j], AX.X, ALU.add))
                        nc.vector.reciprocal(sums, sums).then_inc(c_inv, 1)

                    def residual(j):
                        if output:
                            residual_tile(dve, rest, b - 2, j, (c_wo_full, TT, 0), c_wo_taken, c_var, c_kept,
                                          c_norm, 7 - j % 2, None, c_new)

                    subtract_max(0)
                    residual(0)
                    subtract_max(1)
                    residual(1)
                    invert_sum(0)
                    subtract_max(2)
                    invert_sum(1)
                    residual(2)
                    subtract_max(3)
                    invert_sum(2)
                    residual(3)
                    invert_sum(3)
                    for stage in (order, rest):
                        if stage is not None:
                            stage.end()

                turn(0, output=False)
                turn(1, output=False)
                with dve.Fori(2, B) as i:
                    turn(i)
                turn(B, softmax=False)
                turn(B + 1, softmax=False)

        with nc.Block() as block:

            @block.sync
            def _(sp):
                sp.dma_start(x_rows.rearrange("(t p) d -> p t d", p=P), x_res[:]).then_inc(x_stored, 16)
                sp.wait_ge(expert_ready, 1)

                def load_biases(i, u):
                    e = sp.value_load(expert[0:1, bass.ts(i * TURN + u, 1)], min_val=0, max_val=E - 1)
                    after(sp, e_y_out, i, TURN, u)
                    for dst, src in ((eb1[:, u, :], eb1_d[bass.ts(e, 1), :].broadcast_to([P, HID])),
                                     (eb2[:, u, :], eb2_d[bass.ts(e, 1), :].broadcast_to([P, D]))):
                        sp.dma_start(dst, src).then_inc(e_loaded[u], 16)

                def load_rows(i, u):
                    sp.dma_start(xs[:, u, :], sorted_x[bass.ts(i * TURN + u, P), :]).then_inc(e_loaded[u], 16)

                for u in range(TURN):
                    load_biases(0, u)
                sp.wait_ge(scattered, 16 * NT)
                for u in range(TURN):
                    load_rows(0, u)
                with sp.Fori(1, TURNS) as i:
                    for u in range(TURN):
                        load_biases(i, u)
                        load_rows(i, u)
                for u in range(TAIL):
                    load_biases(TURNS, u)
                    load_rows(TURNS, u)
                sp.wait_ge(x_stored, 16)

            @block.gpsimd
            def _(pool):
                pool.wait_ge(slots_ready, 1)
                for t in range(NT):
                    pool.indirect_dma_start(sorted_x, bass.IndirectOffsetOnAxis(ap=slot[:, t:t + 1], axis=0),
                                            xn_e[:, t, :], None).then_inc(scattered, 16)

                def gather(i, v):
                    u = v % TURN
                    after(pool, e_ids, i, 2 * TURN, 2 * v + 2)
                    after(pool, e_y_out, i, TURN, v)
                    pool.nop(nofuse=True)
                    pool.indirect_dma_start(res[:, u, :], None, x_rows,
                                            bass.IndirectOffsetOnAxis(ap=token_in[:, u:u + 1], axis=0))\
                        .then_inc(e_gathered[u], 16)

                def tile(i, u, more=True):
                    if more:
                        gather(i, u + 1)
                    after(pool, e_y_out, i, TURN, TURN + u)
                    pool.nop(nofuse=True)
                    pool.indirect_dma_start(out_rows, bass.IndirectOffsetOnAxis(ap=token[:, u:u + 1], axis=0),
                                            ys[:, u, :], None, bounds_check=NT * P - 1, oob_is_err=False)\
                        .then_inc(e_stored, 16)
                    pool.wait_ge(e_stored, i * (16 * TURN) + (16 * u + 16))
                    pool.sem_inc(e_y_free, 1)

                pool.wait_ge(x_stored, 16)
                gather(0, 0)
                with pool.Fori(0, TURNS) as i:
                    for u in range(TURN):
                        tile(i, u)
                for u in range(TAIL):
                    tile(TURNS, u, more=u + 1 < TAIL)

            @block.tensor
            def _(pe):
                pe.wait_ge(g_v, 2)
                hot = g_hot[:].rearrange("p t e -> p (t e)")
                nc.tensor.matmul(ps[:, 3, 0:P], con("before", P), hot, start=True, stop=True).then_inc(g_mm, 1)
                nc.tensor.matmul(ps[:, 4, 0:P], con("ones", P), hot, start=True, stop=True).then_inc(g_mm, 1)
                pe.wait_ge(expert_ready, 1)
                pe.wait_ge(g_dve, 1)
                pe.wait_ge(ld_ew, 48)

                def columns(i, v):
                    u = v % TURN
                    pe.wait_ge(e_loaded[u], i * 48 + 48 * (v // TURN + 1))
                    after(pe, e_xT, i, TURN, v)
                    for k in range(KD):
                        ins = nc.tensor.transpose(ps[:, 0, k * P:(k + 1) * P], xs[:, u, k * P:(k + 1) * P], ident)
                    ins.then_inc(e_tp_full, 1)

                def up(i, v):
                    e = pe.value_load(expert[0:1, bass.ts(i * TURN + v, 1)], min_val=0, max_val=E - 1)
                    after(pe, e_xT, i, TURN, v + 1)
                    for h in range(2):
                        for k in range(KD):
                            ins = nc.tensor.matmul(
                                ps[:, 2 + 2 * (v % 2) + h, :], xsT[:, v % 2, k, :],
                                ew1[:, bass.ts(e, 1), k, h * S:(h + 1) * S].rearrange("p a n -> p (a n)"),
                                start=(k == 0), stop=(k == KD - 1))
                        ins.then_inc(e_up_full, 1)

                def hidden(i, u):
                    after(pe, e_hT, i, 2 * TURN, 2 * u)
                    for k in range(KH):
                        if k % 4 == 0:
                            after(pe, e_h, i, 2 * TURN, 2 * u + 1 + k // 4)
                        ins = nc.tensor.transpose(ps[:, 6 + k // 4, (k % 4) * P:(k % 4 + 1) * P],
                                                  h_tok[:, u % 2, k * P:(k + 1) * P], ident)
                        if k % 4 == 3:
                            ins.then_inc(e_ht_full, 1)

                def down(i, u):
                    e = pe.value_load(expert[0:1, bass.ts(i * TURN + u, 1)], min_val=0, max_val=E - 1)
                    after(pe, e_y_out, i, TURN, TURN + u - 1)
                    for k in range(KH):
                        if k % 4 == 0:
                            after(pe, e_hT, i, 2 * TURN, 2 * u + 1 + k // 4)
                        ins = nc.tensor.matmul(ps[:, 1, 0:D], hT[:, u % 2, k, :],
                                               ew2[:, bass.ts(e, 1), k, :].rearrange("p a n -> p (a n)"),
                                               start=(k == 0), stop=(k == KH - 1))
                    ins.then_inc(e_down_full, 1)

                def tile(i, u, left=TURN + TAIL):
                    hidden(i, u)
                    if u + 1 < left:
                        up(i, u + 1)
                    if u + 2 < left:
                        columns(i, u + 2)
                    down(i, u)

                columns(0, 0)
                up(0, 0)
                columns(0, 1)
                with pe.Fori(0, TURNS) as i:
                    for u in range(TURN):
                        tile(i, u)
                for u in range(TAIL):
                    tile(TURNS, u, left=TAIL)

            @block.scalar
            def _(act):
                act.wait_ge(g_v, 1)
                nc.scalar.activation(g_e[:], g_e[:], ACT.Exp).then_inc(g_act, 1)

                def tile(i, u):
                    for h in range(2):
                        after(act, e_pre, i, 2 * TURN, 2 * u + h + 1)
                        half = h_tok[:, u % 2, h * S:(h + 1) * S]
                        nc.scalar.activation(half, half, ACT.Gelu).then_inc(e_h, 1)

                with act.Fori(0, TURNS) as i:
                    for u in range(TURN):
                        tile(i, u)
                for u in range(TAIL):
                    tile(TURNS, u)

            @block.vector
            def _(dve):
                order = Order(dve, g_dve_own)

                def spread(ap, n=E):
                    return ap.unsqueeze(2).broadcast_to([P, NT, n])

                dve.wait_ge(g_mm, B)
                order.step(nc.vector.tensor_tensor(
                    g_e[:], ps[:, 2, 0:NT * E].rearrange("p (t e) -> p t e", e=E),
                    row("gate_b", E).unsqueeze(1).broadcast_to([P, NT, E]), ALU.add))
                order.step(nc.vector.tensor_reduce(g_max[:], g_e[:], AX.X, ALU.max))
                nc.vector.tensor_tensor(g_e[:], g_e[:], spread(g_max[:]), ALU.subtract).then_inc(g_v, 1)
                dve.wait_ge(g_act, 1)
                order.step(nc.vector.tensor_reduce(g_sum[:], g_e[:], AX.X, ALU.add))
                order.step(nc.vector.reciprocal(g_inv[:], g_sum[:]))
                order.step(nc.vector.tensor_tensor(g_e[:], g_e[:], spread(g_inv[:]), ALU.mult))
                order.step(nc.vector.tensor_reduce(weight[:], g_e[:], AX.X, ALU.max))
                order.mark(nc.vector.tensor_copy(xn_e[:, :, D], weight[:]))
                order.mark(nc.vector.tensor_copy(xn_e[:, :, D + 1], con("token", NT)))
                order.step(nc.vector.tensor_tensor(g_eq[:], g_e[:], spread(weight[:]), ALU.is_equal))
                order.step(nc.vector.tensor_tensor(
                    g_eq[:], g_eq[:], con("down", E).unsqueeze(1).broadcast_to([P, NT, E]), ALU.mult))
                order.step(nc.vector.tensor_reduce(g_top[:], g_eq[:], AX.X, ALU.max))
                nc.vector.tensor_tensor(g_hot[:], g_eq[:], spread(g_top[:]), ALU.is_equal).then_inc(g_v, 1)
                dve.wait_ge(g_mm, B + 2)
                order.mark(nc.vector.memset(g_pre[:, 0, :], 0.0))
                order.mark(nc.vector.memset(g_start[:, 0:1], 0.0))
                order.step(nc.vector.tensor_copy(g_tot[:].rearrange("p t e -> p (t e)"), ps[:, 4, 0:P]))
                for t in range(NT):
                    order.step(nc.vector.tensor_tensor(g_pre[:, t + 1, :], g_pre[:, t, :], g_tot[:, t, :], ALU.add))
                order.step(nc.vector.tensor_tensor(g_cmp[:], g_pre[:, NT, :].unsqueeze(2).broadcast_to([P, E, NT]),
                                                   con("full", NT).unsqueeze(1).broadcast_to([P, E, NT]),
                                                   ALU.is_gt))
                order.step(nc.vector.tensor_reduce(g_tiles[:], g_cmp[:], AX.X, ALU.add))
                for e in range(E):
                    order.step(nc.vector.tensor_tensor(g_start[:, e + 1:e + 2], g_start[:, e:e + 1],
                                                       g_tiles[:, e:e + 1], ALU.add))
                order.step(nc.vector.tensor_tensor(g_cmp2[:], con("tile_no", MT).unsqueeze(2).broadcast_to([P, MT, E]),
                                                   g_start[:, 1:E + 1].unsqueeze(1).broadcast_to([P, MT, E]),
                                                   ALU.is_ge))
                order.step(nc.vector.tensor_reduce(g_eid[:], g_cmp2[:], AX.X, ALU.add))
                order.step(nc.vector.tensor_scalar(g_eid[:], g_eid[:], float(E - 1), None, ALU.min))
                nc.vector.tensor_copy(expert[:], g_eid[:]).then_inc(expert_ready, 1)
                order.step(nc.vector.tensor_scalar(g_base[:], g_start[:, 0:E], float(P), None, ALU.mult))
                order.step(nc.vector.tensor_tensor(g_slot[:], g_pre[:, 0:NT, :],
                                                   g_base[:].unsqueeze(1).broadcast_to([P, NT, E]), ALU.add))
                ins = nc.vector.tensor_tensor(g_slot[:].rearrange("p t e -> p (t e)"), ps[:, 3, 0:P],
                                              g_slot[:].rearrange("p t e -> p (t e)"), ALU.add)
                ins.then_inc(g_dve, 1)
                dve.wait_ge(g_dve, 1)
                order.step(nc.vector.tensor_tensor(g_slot[:], g_slot[:], g_hot[:], ALU.mult))
                order.step(nc.vector.tensor_reduce(g_slotf[:], g_slot[:], AX.X, ALU.add))
                nc.vector.tensor_copy(slot[:], g_slotf[:]).then_inc(slots_ready, 1)

                def columns(i, v):
                    after(dve, e_tp_full, i, TURN, v + 1)
                    nc.vector.tensor_copy(xsT[:, v % 2].rearrange("p k n -> p (k n)"), ps[:, 0, 0:D])\
                        .then_inc(e_xT, 1)
                    after(dve, e_y_free, i, TURN, v)
                    u = v % TURN
                    nc.vector.tensor_copy(token[:, u:u + 1], xs[:, u, D + 1:RD]).then_inc(e_ids, 1)
                    nc.vector.tensor_scalar(token_in[:, u:u + 1], xs[:, u, D + 1:RD], float(NT * P - 1), None,
                                            ALU.min).then_inc(e_ids, 1)

                def biased(i, v):
                    for h in range(2):
                        after(dve, e_up_full, i, 2 * TURN, 2 * v + h + 1)
                        nc.vector.tensor_tensor(h_tok[:, v % 2, h * S:(h + 1) * S], ps[:, 2 + 2 * (v % 2) + h, :],
                                                eb1[:, v % TURN, h * S:(h + 1) * S], ALU.add).then_inc(e_pre, 1)

                def tile(i, u, left=TURN + TAIL):
                    for h in range(2):
                        after(dve, e_ht_full, i, 2 * TURN, 2 * u + h + 1)
                        nc.vector.tensor_copy(hT[:, u % 2, h * 4:(h + 1) * 4].rearrange("p k n -> p (k n)"),
                                              ps[:, 6 + h, :]).then_inc(e_hT, 1)
                    if u + 1 < left:
                        biased(i, u + 1)
                    if u + 2 < left:
                        columns(i, u + 2)
                    after(dve, e_down_full, i, TURN, u + 1)
                    after(dve, e_y_free, i, TURN, u)
                    nc.vector.tensor_tensor(ys[:, u, :], ps[:, 1, 0:D], eb2[:, u, :], ALU.add).then_inc(e_sum, 1)
                    after(dve, e_sum, i, TURN, u + 1)
                    dve.wait_ge(e_gathered[u], i * 16 + 16)
                    nc.vector.scalar_tensor_tensor(ys[:, u, :], ys[:, u, :], xs[:, u, D:D + 1], res[:, u, :],
                                                   ALU.mult, ALU.add).then_inc(e_y_out, 1)

                columns(0, 0)
                biased(0, 0)
                columns(0, 1)
                with dve.Fori(0, TURNS) as i:
                    for u in range(TURN):
                        tile(i, u)
                for u in range(TAIL):
                    tile(TURNS, u, left=TAIL)


def chunks(w):
    k, n = w.shape
    return np.ascontiguousarray(w.reshape(k // P, P, n).transpose(1, 0, 2))


def shape_constants():
    p = np.arange(P)
    c = np.zeros((P, NCONST), np.float32)

    def put(name, a):
        a = np.asarray(a, np.float32).reshape(a.shape[0], -1)
        c[:, CONST_AT[name]:CONST_AT[name] + a.shape[1]] = a

    put("ident", np.eye(P))
    put("before", p[:, None] < p[None, :])
    put("ones", np.ones((P, P)))
    put("kmask", p[:, None] // DH1 == np.arange(G1)[None, :])
    put("vmask", (p // DH1)[None, None, :] == 2 * np.arange(TT)[None, :, None] + (p // KEYS)[:, None, None])
    put("down", np.broadcast_to(E - np.arange(E), (P, E)))
    put("full", np.broadcast_to(P * np.arange(NT), (P, NT)))
    put("tile_no", np.broadcast_to(np.arange(MT), (P, MT)))
    put("token", p[:, None] + P * np.arange(NT)[None, :])
    put("minus_half", np.full((P, NT), -0.5))
    return c


def kernel(**inputs):
    import concourse.bacc as bacc
    from concourse.bass_utils import run_bass_kernel_spmd

    a = {k: np.asarray(v) for k, v in inputs.items()}
    f0, f1 = "L0_xattn_", "L1_xattn_"
    cols = [a[f0 + n] for n in ("vid_g", "vid_b", "tab_g", "tab_b", "q_g", "q_b", "k_g", "k_b")]
    cols += [a[f1 + n] for n in ("bq", "bk")] + [a["L0_ffn_" + n] for n in ("w1_s", "w2_s", "h1_s", "h2_s")]
    rows = [a[f0 + "bo"], a["L0_ffn_w3_s"], a[f1 + "bv"], a[f1 + "bo"], a["L1_ffn_gate_b"]]
    arrays = {
        "in_x": a["x"], "in_ctx": a["ctx_1024"], "in_mask": a["mask_1x1xSxS2_ik1"],
        "in_cols": np.concatenate([v.reshape(-1, P).T for v in cols], axis=1),
        "in_rows": np.concatenate(rows), "in_const": shape_constants(),
        "in_wk0": chunks(a[f0 + "Wk"]), "in_wv0": chunks(a[f0 + "Wv"]), "in_wq0": chunks(a[f0 + "Wq"]),
        "in_wo0": chunks(a[f0 + "Wo"]),
        "in_wk1": chunks(a[f1 + "Wk"].T), "in_wv1": chunks(a[f1 + "Wv"].T), "in_wq1": chunks(a[f1 + "Wq"].T),
        "in_wo1": chunks(a[f1 + "Wo"].T),
        "in_fw1": chunks(a["L0_ffn_w1_w"].T), "in_fw2": chunks(a["L0_ffn_w2_w"].T),
        "in_fh1": chunks(a["L0_ffn_h1_w"].T), "in_fh2": chunks(a["L0_ffn_h2_w"].T),
        "in_fw3": chunks(a["L0_ffn_w3_w"].T), "in_gate_w": chunks(a["L1_ffn_gate_w"]),
        "in_ew1": a["L1_ffn_w1"].reshape(E, KD, P, HID).transpose(0, 2, 1, 3),
        "in_eb1": a["L1_ffn_b1"],
        "in_ew2": a["L1_ffn_w2"].reshape(E, KH, P, D).transpose(0, 2, 1, 3),
        "in_eb2": a["L1_ffn_b2"],
    }
    arrays = {k: np.ascontiguousarray(v) for k, v in arrays.items()}
    nc = bacc.Bacc("TRN2", target_bir_lowering=False, num_devices=1)
    args = [nc.dram_tensor(k, v.shape, mybir.dt.from_np(v.dtype), kind="ExternalInput").ap()
            for k, v in arrays.items()]
    scratch = [nc.dram_tensor(k, shape, F32, kind="Internal").ap()
               for k, shape in (("sorted_x", (MT * P, RD)), ("x_rows", (NT * P, D)))]
    out = nc.dram_tensor("out_0", (B, S, D), F32, kind="ExternalOutput").ap()
    ffn_copy = [nc.dram_tensor(k + "_copy", arrays["in_" + k].shape, F32, kind="Internal").ap()
                for k in ("fw1", "fw2", "fh1", "fw3", "fh2")]
    build(nc, *args, *scratch, ffn_copy, out)
    return run_bass_kernel_spmd(nc, [arrays], core_ids=[0]).results[0]["out_0"]
```
